# Optimizing a Trainium2 kernel written in Bass

```python
import numpy as np
import jax
import jax.numpy as jnp

def _softmax(x, axis=-1):
    return jax.nn.softmax(x, axis=axis)

def _gelu(x):
    return jax.nn.gelu(x, approximate=True)

def _silu(x):
    return jax.nn.silu(x)

def _sigmoid(x):
    return jax.nn.sigmoid(x)

def _layernorm(x, axis=-1, eps=1e-05):
    m = jnp.mean(x, axis=axis, keepdims=True)
    v = jnp.var(x, axis=axis, keepdims=True)
    return (x - m) / jnp.sqrt(v + eps)

def _scatter_add(tgt, idx, src, axis=0):
    return tgt.at[idx].add(src)

def _segment_sum(src, seg, n):
    return jax.ops.segment_sum(src, seg, n)
kernel_name = 'mk_gps_d1_gnn_r8_e02db2'

def setup_inputs(seed: int=0):
    np.random.seed(seed)
    _w = jnp.asarray

    def _rec_inputs():
        import jax
        import jax.numpy as jnp
        _gk = jax.random.key(seed)
        x = -0.0003713 + 1 * jax.random.normal(jax.random.fold_in(_gk, 1), (6250, 256), jnp.float32)
        src = jax.random.randint(jax.random.fold_in(_gk, 2), (200000,), 0, 6250, jnp.int32)
        dst = jnp.minimum((6250 * jax.random.uniform(jax.random.fold_in(_gk, 3), (200000,)) ** 2.0).astype(jnp.int32), 49999)
        _o = jnp.argsort(dst, stable=True)
        src = src[_o]
        dst = dst[_o]
        edge_weight1 = 0.000937891 + 0.999965 * jax.random.normal(jax.random.fold_in(_gk, 13), (200000, 1), jnp.float32)
        return (x, src, dst, edge_weight1)
    x, src, dst, edge_weight1 = _rec_inputs()

    def _L0_gnn_setup():
        import jax, jax.numpy as jnp
        import numpy as np
        N, E, D = (6250, 100000, 256)
        H, B, A = (8, 4, 3)
        F = D // H
        G = 64
        EPS = 1e-05

        def _forward(node, W_bases, W_comb, b_comb, conv_bias, gn_weight, gn_bias, gn_mean_scale, edge_index, batch):
            n = node.shape[0]
            loops = jnp.arange(n, dtype=edge_index.dtype)
            src = jnp.concatenate([edge_index[0], loops])
            dst = jnp.concatenate([edge_index[1], loops])
            deg = jax.ops.segment_sum(jnp.ones_like(src, dtype=node.dtype), dst, num_segments=n)
            dinv = jnp.where(deg > 0, jax.lax.rsqrt(deg), 0.0)
            sym_w = dinv[src] * dinv[dst]
            bases = node @ W_bases
            comb = node @ W_comb + b_comb
            msg = bases[src]
            agg_sym = jax.ops.segment_sum(msg * sym_w[:, None], dst, num_segments=n)
            agg_sum = jax.ops.segment_sum(msg, dst, num_segments=n)
            agg_max = jax.ops.segment_max(msg, dst, num_segments=n)
            aggregated = jnp.stack([agg_sym, agg_sum, agg_max], axis=1)
            aggregated = aggregated.reshape(n, A * B, F)
            weightings = comb.reshape(n, H, B * A)
            h = jnp.einsum('nhk,nkf->nhf', weightings, aggregated).reshape(n, D) + conv_bias
            counts = jnp.maximum(jax.ops.segment_sum(jnp.ones((n,), node.dtype), batch, num_segments=G), 1.0)
            mean = jax.ops.segment_sum(h, batch, num_segments=G) / counts[:, None]
            hc = h - gn_mean_scale * mean[batch]
            var = jax.ops.segment_sum(hc * hc, batch, num_segments=G) / counts[:, None]
            out = gn_weight * hc * jax.lax.rsqrt(var[batch] + EPS) + gn_bias
            return jax.nn.relu(out)
        key = jax.random.key(seed)
        ks = jax.random.split(key, 8)
        glorot = lambda k, shape: jax.random.normal(k, shape, jnp.float32) * np.sqrt(2.0 / (shape[0] + shape[1])).astype(np.float32)
        return {'node': jax.random.normal(ks[0], (N, D), jnp.float32), 'edge_attr': jax.random.normal(ks[1], (E, 1), jnp.float32), 'W_bases': glorot(ks[2], (D, B * F)), 'W_comb': glorot(ks[3], (D, H * B * A)), 'b_comb': jnp.zeros((H * B * A,), jnp.float32), 'conv_bias': jnp.zeros((D,), jnp.float32), 'gn_weight': jnp.ones((D,), jnp.float32), 'gn_bias': jnp.zeros((D,), jnp.float32), 'gn_mean_scale': jnp.ones((D,), jnp.float32), 'edge_index': jax.random.randint(ks[4], (2, E), 0, N, dtype=jnp.int32), 'batch': jnp.sort(jax.random.randint(ks[5], (N,), 0, G, dtype=jnp.int32))}
    _L0_gnn_all = _L0_gnn_setup()
    _L0_gnn_in = {k: v for k, v in _L0_gnn_all.items() if k in ('W_bases', 'W_comb', 'b_comb', 'conv_bias', 'gn_weight', 'gn_bias', 'gn_mean_scale')}
    del _L0_gnn_all

    def _L0_mix_setup():
        import jax, jax.numpy as jnp
        import numpy as np
        DIM = 256
        HEADS = 4
        DIM_HEAD = 32
        NUM_MEM = 4
        HIDDEN = HEADS * DIM_HEAD
        SCALE = DIM_HEAD ** (-0.5)

        def rmsnorm(x, g):
            n = jnp.linalg.norm(x, axis=-1, keepdims=True)
            return x / jnp.maximum(n, 1e-12) * g * x.shape[-1] ** 0.5
        key = jax.random.key(seed)
        ks = jax.random.split(key, 8)
        B, N = (4, 2048)
        return {'x': jax.random.normal(ks[0], (B, N, DIM), jnp.float32), 't': jax.random.normal(ks[1], (B,), jnp.float32), 'w_qkv': jax.random.normal(ks[2], (DIM, 3 * HIDDEN), jnp.float32) * 0.02, 'mem_kv': jax.random.normal(ks[3], (2, HEADS, DIM_HEAD, NUM_MEM), jnp.float32), 'w_out': jax.random.normal(ks[4], (HIDDEN, DIM), jnp.float32) * 0.02, 'b_out': jnp.zeros((DIM,), jnp.float32), 'g_out': jnp.ones((DIM,), jnp.float32), 'g_pre': jnp.ones((DIM,), jnp.float32)}
    _L0_mix_all = _L0_mix_setup()
    _L0_mix_in = {k: v for k, v in _L0_mix_all.items() if k in ('t', 'w_qkv', 'mem_kv', 'w_out', 'b_out', 'g_out', 'g_pre')}
    del _L0_mix_all

    def _L0_ffn_setup():
        import jax, jax.numpy as jnp
        import numpy as np
        BN_EPS = 0.001

        def _bn(h, g, b, m, v):
            return g * (h - m) * jax.lax.rsqrt(v + BN_EPS) + b
        key = jax.random.key(seed)
        ks = jax.random.split(key, 8)
        B, F, Df = (256, 64, 256)
        E, H, D = (8, 256, 256)
        s1 = 1.0 / np.sqrt(Df)
        s2 = 1.0 / np.sqrt(H)
        return {'x': jax.random.normal(ks[0], (B, F, Df), jnp.float32), 'Wr': jax.random.normal(ks[1], (Df, E), jnp.float32) * s1, 'br': jnp.zeros((E,), jnp.float32), 'W1': jax.random.normal(ks[2], (E, Df, H), jnp.float32) * s1, 'b1': jnp.zeros((E, H), jnp.float32), 'g1': jnp.ones((E, H), jnp.float32), 'be1': jnp.zeros((E, H), jnp.float32), 'm1': jnp.zeros((E, H), jnp.float32), 'v1': jnp.ones((E, H), jnp.float32), 'W2': jax.random.normal(ks[3], (E, H, H), jnp.float32) * s2, 'b2': jnp.zeros((E, H), jnp.float32), 'g2': jnp.ones((E, H), jnp.float32), 'be2': jnp.zeros((E, H), jnp.float32), 'm2': jnp.zeros((E, H), jnp.float32), 'v2': jnp.ones((E, H), jnp.float32), 'Wo': jax.random.normal(ks[4], (E, H, D), jnp.float32) * s2, 'bo': jnp.zeros((E, D), jnp.float32)}
    _L0_ffn_all = _L0_ffn_setup()
    _L0_ffn_in = {k: v for k, v in _L0_ffn_all.items() if k in ('Wr', 'br', 'W1', 'b1', 'g1', 'be1', 'm1', 'v1', 'W2', 'b2', 'g2', 'be2', 'm2', 'v2', 'Wo', 'bo')}
    del _L0_ffn_all
    return {'x': x, 'src': src, 'dst': dst, 'edge_weight1': edge_weight1, 'L0_gnn_W_bases': _L0_gnn_in['W_bases'], 'L0_gnn_W_comb': _L0_gnn_in['W_comb'], 'L0_gnn_b_comb': _L0_gnn_in['b_comb'], 'L0_gnn_conv_bias': _L0_gnn_in['conv_bias'], 'L0_gnn_gn_weight': _L0_gnn_in['gn_weight'], 'L0_gnn_gn_bias': _L0_gnn_in['gn_bias'], 'L0_gnn_gn_mean_scale': _L0_gnn_in['gn_mean_scale'], 'L0_mix_t': _L0_mix_in['t'], 'L0_mix_w_qkv': _L0_mix_in['w_qkv'], 'L0_mix_mem_kv': _L0_mix_in['mem_kv'], 'L0_mix_w_out': _L0_mix_in['w_out'], 'L0_mix_b_out': _L0_mix_in['b_out'], 'L0_mix_g_out': _L0_mix_in['g_out'], 'L0_mix_g_pre': _L0_mix_in['g_pre'], 'L0_ffn_Wr': _L0_ffn_in['Wr'], 'L0_ffn_br': _L0_ffn_in['br'], 'L0_ffn_W1': _L0_ffn_in['W1'], 'L0_ffn_b1': _L0_ffn_in['b1'], 'L0_ffn_g1': _L0_ffn_in['g1'], 'L0_ffn_be1': _L0_ffn_in['be1'], 'L0_ffn_m1': _L0_ffn_in['m1'], 'L0_ffn_v1': _L0_ffn_in['v1'], 'L0_ffn_W2': _L0_ffn_in['W2'], 'L0_ffn_b2': _L0_ffn_in['b2'], 'L0_ffn_g2': _L0_ffn_in['g2'], 'L0_ffn_be2': _L0_ffn_in['be2'], 'L0_ffn_m2': _L0_ffn_in['m2'], 'L0_ffn_v2': _L0_ffn_in['v2'], 'L0_ffn_Wo': _L0_ffn_in['Wo'], 'L0_ffn_bo': _L0_ffn_in['bo']}

def reference(x, src, dst, edge_weight1, L0_gnn_W_bases, L0_gnn_W_comb, L0_gnn_b_comb, L0_gnn_conv_bias, L0_gnn_gn_weight, L0_gnn_gn_bias, L0_gnn_gn_mean_scale, L0_mix_t, L0_mix_w_qkv, L0_mix_mem_kv, L0_mix_w_out, L0_mix_b_out, L0_mix_g_out, L0_mix_g_pre, L0_ffn_Wr, L0_ffn_br, L0_ffn_W1, L0_ffn_b1, L0_ffn_g1, L0_ffn_be1, L0_ffn_m1, L0_ffn_v1, L0_ffn_W2, L0_ffn_b2, L0_ffn_g2, L0_ffn_be2, L0_ffn_m2, L0_ffn_v2, L0_ffn_Wo, L0_ffn_bo):
    import jax
    import jax.numpy as jnp

    def _L0_gnn_ref(node, edge_attr, W_bases, W_comb, b_comb, conv_bias, gn_weight, gn_bias, gn_mean_scale, edge_index, batch):
        import jax, jax.numpy as jnp
        import numpy as np
        N, E, D = (6250, 100000, 256)
        H, B, A = (8, 4, 3)
        F = D // H
        G = 64
        EPS = 1e-05

        def _forward(node, W_bases, W_comb, b_comb, conv_bias, gn_weight, gn_bias, gn_mean_scale, edge_index, batch):
            n = node.shape[0]
            loops = jnp.arange(n, dtype=edge_index.dtype)
            src = jnp.concatenate([edge_index[0], loops])
            dst = jnp.concatenate([edge_index[1], loops])
            deg = jax.ops.segment_sum(jnp.ones_like(src, dtype=node.dtype), dst, num_segments=n)
            dinv = jnp.where(deg > 0, jax.lax.rsqrt(deg), 0.0)
            sym_w = dinv[src] * dinv[dst]
            bases = node @ W_bases
            comb = node @ W_comb + b_comb
            msg = bases[src]
            agg_sym = jax.ops.segment_sum(msg * sym_w[:, None], dst, num_segments=n)
            agg_sum = jax.ops.segment_sum(msg, dst, num_segments=n)
            agg_max = jax.ops.segment_max(msg, dst, num_segments=n)
            aggregated = jnp.stack([agg_sym, agg_sum, agg_max], axis=1)
            aggregated = aggregated.reshape(n, A * B, F)
            weightings = comb.reshape(n, H, B * A)
            h = jnp.einsum('nhk,nkf->nhf', weightings, aggregated).reshape(n, D) + conv_bias
            counts = jnp.maximum(jax.ops.segment_sum(jnp.ones((n,), node.dtype), batch, num_segments=G), 1.0)
            mean = jax.ops.segment_sum(h, batch, num_segments=G) / counts[:, None]
            hc = h - gn_mean_scale * mean[batch]
            var = jax.ops.segment_sum(hc * hc, batch, num_segments=G) / counts[:, None]
            out = gn_weight * hc * jax.lax.rsqrt(var[batch] + EPS) + gn_bias
            return jax.nn.relu(out)
        del edge_attr
        return _forward(node, W_bases, W_comb, b_comb, conv_bias, gn_weight, gn_bias, gn_mean_scale, edge_index, batch)

    def _L0_mix_ref(x, t, w_qkv, mem_kv, w_out, b_out, g_out, g_pre):
        import jax, jax.numpy as jnp
        import numpy as np
        DIM = 256
        HEADS = 4
        DIM_HEAD = 32
        NUM_MEM = 4
        HIDDEN = HEADS * DIM_HEAD
        SCALE = DIM_HEAD ** (-0.5)

        def rmsnorm(x, g):
            n = jnp.linalg.norm(x, axis=-1, keepdims=True)
            return x / jnp.maximum(n, 1e-12) * g * x.shape[-1] ** 0.5
        b, n, c = x.shape
        xn = rmsnorm(x, g_pre)
        qkv = xn @ w_qkv
        q, k, v = jnp.split(qkv, 3, axis=-1)

        def to_heads(z):
            return z.reshape(b, n, HEADS, DIM_HEAD).transpose(0, 2, 3, 1)
        q, k, v = map(to_heads, (q, k, v))
        mk = jnp.broadcast_to(mem_kv[0], (b, HEADS, DIM_HEAD, NUM_MEM))
        mv = jnp.broadcast_to(mem_kv[1], (b, HEADS, DIM_HEAD, NUM_MEM))
        k = jnp.concatenate([mk, k], axis=-1)
        v = jnp.concatenate([mv, v], axis=-1)
        q = jax.nn.softmax(q, axis=-2) * SCALE
        k = jax.nn.softmax(k, axis=-1)
        context = jnp.einsum('bhdn,bhen->bhde', k, v)
        out = jnp.einsum('bhde,bhdn->bhen', context, q)
        out = out.transpose(0, 3, 1, 2).reshape(b, n, HIDDEN)
        out = rmsnorm(out @ w_out + b_out, g_out)
        return out + x

    def _L0_ffn_ref(x, Wr, br, W1, b1, g1, be1, m1, v1, W2, b2, g2, be2, m2, v2, Wo, bo):
        import jax, jax.numpy as jnp
        import numpy as np
        BN_EPS = 0.001

        def _bn(h, g, b, m, v):
            return g * (h - m) * jax.lax.rsqrt(v + BN_EPS) + b
        feat = jnp.mean(x, axis=0)
        w = jax.nn.softmax(feat @ Wr + br, axis=-1)
        h = jnp.einsum('bfd,edh->bfeh', x, W1) + b1
        h = jax.nn.relu(_bn(h, g1, be1, m1, v1))
        h = jnp.einsum('bfeh,ehk->bfek', h, W2) + b2
        h = jax.nn.relu(_bn(h, g2, be2, m2, v2))
        y = jnp.einsum('bfeh,ehd->bfed', h, Wo) + bo
        return jnp.einsum('bfed,fe->bfd', y, w)
    edge_index = jnp.stack([src, dst])
    batch0 = jnp.zeros((6250,), jnp.int32)
    xn = _layernorm(x, axis=-1)
    x = x + _L0_gnn_ref(xn, edge_weight1, L0_gnn_W_bases, L0_gnn_W_comb, L0_gnn_b_comb, L0_gnn_conv_bias, L0_gnn_gn_weight, L0_gnn_gn_bias, L0_gnn_gn_mean_scale, edge_index, batch0) + _L0_mix_ref(xn[None], L0_mix_t, L0_mix_w_qkv, L0_mix_mem_kv, L0_mix_w_out, L0_mix_b_out, L0_mix_g_out, L0_mix_g_pre)[0]
    x = x + _L0_ffn_ref(_layernorm(x, axis=-1)[None], L0_ffn_Wr, L0_ffn_br, L0_ffn_W1, L0_ffn_b1, L0_ffn_g1, L0_ffn_be1, L0_ffn_m1, L0_ffn_v1, L0_ffn_W2, L0_ffn_b2, L0_ffn_g2, L0_ffn_be2, L0_ffn_m2, L0_ffn_v2, L0_ffn_Wo, L0_ffn_bo)[0]
    return x

_drawn_inputs = setup_inputs


def setup_inputs(seed=0):
    import zlib

    import numpy as np

    out = dict(_drawn_inputs(seed))
    spreads = {'L0_gnn_b_comb': (0.0, 0.3),
     'L0_gnn_conv_bias': (0.0, 0.8),
     'L0_gnn_gn_weight': (1.0, 0.2),
     'L0_gnn_gn_bias': (0.0, 0.1),
     'L0_gnn_gn_mean_scale': (1.0, 0.6),
     'L0_mix_b_out': (0.0, 0.1),
     'L0_mix_g_out': (1.0, 0.2),
     'L0_mix_g_pre': (1.0, 0.6),
     'L0_ffn_br': (0.0, 0.505),
     'L0_ffn_b1': (0.0, 0.731),
     'L0_ffn_g1': (1.0, 0.6),
     'L0_ffn_be1': (0.0, 0.722),
     'L0_ffn_m1': (0.0, 0.712),
     'L0_ffn_v1': (1.0, 0.6),
     'L0_ffn_b2': (0.0, 0.523),
     'L0_ffn_g2': (1.0, 0.6),
     'L0_ffn_be2': (0.0, 0.554),
     'L0_ffn_m2': (0.0, 0.541),
     'L0_ffn_v2': (1.0, 0.6),
     'L0_ffn_bo': (0.0, 0.387)}
    factors = {'L0_mix_w_qkv': 8.0, 'L0_mix_mem_kv': 8.0, 'L0_mix_w_out': 8.0}
    for name, (base, spread) in spreads.items():
        noise = np.random.default_rng([zlib.crc32(name.encode()), seed]).standard_normal(out[name].shape)
        drawn = base * np.exp(spread * noise) if base else spread * noise
        out[name] = jnp.asarray(drawn.astype(out[name].dtype))
    for name, factor in factors.items():
        out[name] = (out[name] * factor).astype(out[name].dtype)
    return out
```

```python
from contextlib import ExitStack

import concourse.bass as bass
from concourse import mybir

F32 = mybir.dt.float32
I32 = mybir.dt.int32
ALU = mybir.AluOpType
ACT = mybir.ActivationFunctionType
AX = mybir.AxisListType

N = 6250
E = 200000
D = 256
P = 128
KD = D // P
NT = -(-N // P)
LAST = N - (NT - 1) * P
HEADS, BASES, AGGS = 8, 4, 3
F = D // HEADS
BF = BASES * F
KC = BASES * AGGS
CW = HEADS * KC
AH, AD, MEM = 4, 32, 4
HID = AH * AD
EX = 8
LN_EPS, GN_EPS, BN_EPS = 1e-5, 1e-5, 1e-3
BIG = 3.0e38
FAR = 1.0e9

U = 16
HW = U // 2
WIN = -(-E // (P * U))
T = WIN * U
RW = BF + 4
ST = AGGS * BF
FULL = E // T
REST = E - FULL * T

LB = 125
NB = E // LB
LP = 100
LC = NB // LP

PAIRS = NT // 2
PASS = PAIRS + 1
PLAIN = WIN - 3 * PASS
UNITS = 2 * PASS

GT = 4
GN = GT * P
GROUPS = NT // GT
ROUNDS = EX + 1

L3_START = 3 * GT

RING2 = 2


def done(n):
    return n + 1 + RING2


def free(n):
    return n + 1


class Chain:

    def __init__(self, eng, sem):
        self.eng, self.sem, self.base, self.n = eng, sem, 0, 0

    def __call__(self, ins):
        ins.then_inc(self.sem, 1)
        self.n += 1
        self.eng.wait_ge(self.sem, self.base + self.n)

    def mark(self, ins):
        ins.then_inc(self.sem, 1)
        self.n += 1

    def enter(self, i, per):
        self.start, self.per = self.base + self.n, per
        self.base, self.n = self.start + i * per, 0

    def leave(self, times):
        assert self.n == self.per, (self.n, self.per)
        self.base, self.n = self.start + times * self.per, 0


def bcast(ap, shape):
    return ap.broadcast_to(shape)


def program(nc, a, y, scratch):
    ctx = ExitStack()
    with ctx:
        def sb(name, shape, dt=F32):
            return ctx.enter_context(nc.sbuf_tensor(name, shape, dt))

        def sem(name):
            return ctx.enter_context(nc.semaphore(name))

        X = sb("X", [P, NT * D])
        X3 = X[:, :].rearrange("p (i d) -> p i d", d=D)
        R1 = sb("R1", [P, NT * D])
        H3 = R1[:, :].rearrange("p (i d) -> p i d", d=D)
        blk = R1[:, 0:NT * LB].bitcast(I32).rearrange("p (i j) -> p i j", j=LB)
        OH = -(-NT * LB // 64) * 64
        below = R1[:, OH:OH + NT * LB].rearrange("p (i j) -> p i j", j=LB)
        oh_lo = R1[0:LP, OH:OH + LC * P].rearrange("p (c m) -> p c m", m=P)
        oh_hi = R1[0:LP, OH + LC * P:OH + LC * (P + NT)].rearrange("p (c m) -> p c m", m=NT)
        o = OH + NT * LB
        upto = R1[:, o:o + P]
        iota = R1[:, o + P:o + 2 * P].bitcast(I32)
        assert o + 2 * P <= NT * D
        GS = 2 * RW
        ring = R1[:, 0:U * GS].rearrange("p (u f) -> p u f", f=GS)
        stm = R1[:, U * GS:U * (GS + BF)].rearrange("p (u f) -> p u f", f=BF)
        sts = R1[:, U * (GS + BF):U * (GS + ST)].rearrange("p (u f) -> p u f", f=2 * BF)
        TB = sb("TB", [P, NT * RW])
        TB3 = TB[:, :].rearrange("p (i f) -> p i f", f=RW)
        CB = sb("CB", [P, NT * CW])
        bn_x = CB[:, 0:NT * 6].rearrange("p (i f) -> p i f", f=6)
        CB3 = CB[:, :].rearrange("p (i f) -> p i f", f=CW)
        AUX = sb("AUX", [P, 3 * EX * KD * D])
        idx_all = AUX[:, 0:T + U].bitcast(I32)
        dst_all = AUX[:, T + U:T + U + T + 2].bitcast(I32)
        o = 2 * T + U + 2
        con = AUX[:, o:o + T]
        neg = AUX[:, o + T:o + 2 * T]
        o += 2 * T
        xs = AUX[:, o:o + 2 * D].rearrange("p (b f) -> p b f", b=2)
        xt = AUX[:, o + 512:o + 1024].rearrange("p (b k n) -> p b k n", b=2, k=KD)
        xl = AUX[:, o + 1024:o + 1536].rearrange("p (b k n) -> p b k n", b=2, k=KD)
        kt = AUX[:, o + 1536:o + 1792].rearrange("p (b n) -> p b n", b=2)
        ek = AUX[:, o + 1792:o + 2048].rearrange("p (b n) -> p b n", b=2)
        vs = AUX[:, o + 2048:o + 2048 + 2 * (HID + 1)].rearrange("p (b n) -> p b n", b=2)
        o += 2048 + 2 * (HID + 1) + 2
        qd = AUX[:, o:o + 256].rearrange("p (b n) -> p b n", b=2)
        eq = AUX[:, o + 256:o + 512].rearrange("p (b n) -> p b n", b=2)
        qn = AUX[:, o + 512:o + 768].rearrange("p (b n) -> p b n", b=2)
        qT = AUX[:, o + 768:o + 1024].rearrange("p (b n) -> p b n", b=2)
        mo = AUX[:, o + 1024:o + 1536].rearrange("p (b n) -> p b n", b=2)
        carT = AUX[:, o + 1536:o + 1536 + 3 * (P + 1)].rearrange("p (a n) -> p a n", a=3)
        o += 1536 + 3 * (P + 1) + 1
        wb = AUX[:, o:o + KD * BF].rearrange("p (k n) -> p k n", k=KD)
        o += KD * BF
        wc = AUX[:, o:o + KD * (CW + 3 * HID)].rearrange("p (k n) -> p k n", k=KD)
        o += KD * (CW + 3 * HID)
        wo = AUX[:, o:o + D]
        o += D
        endsT = AUX[0:NT, o:o + P]
        startsT = AUX[0:NT, o + P:o + 2 * P]
        o += 2 * P
        assert o <= 3 * EX * KD * D
        o = U * (GS + ST)
        M, Mb, blockm, runw, runn = [R1[:, o + n * P:o + (n + 1) * P] for n in range(5)]
        m2, b_out, g_out = [R1[:, o + 5 * P + n * D:o + 5 * P + (n + 1) * D] for n in range(3)]
        fix = R1[:, o + 5 * P + 3 * D:o + 5 * P + 3 * D + ST]
        assert o + 5 * P + 3 * D + ST <= NT * D
        GR = 7
        got = AUX[:, 0:GR * ST].rearrange("p (u f) -> p u f", f=ST)
        prod = AUX[:, GR * ST:GR * ST + 2 * KC * D].rearrange("p (b k n) -> p b k n", b=2, k=KC)
        assert GR * ST + 2 * KC * D <= 3 * EX * KD * D
        EW = [AUX[:, n * EX * KD * D:(n + 1) * EX * KD * D].rearrange("p (e k n) -> p e k n", e=EX, k=KD)
              for n in range(3)]
        h1 = TB[:, 0:2 * KD * GN].rearrange("p (b k n) -> p b k n", b=2, k=KD)
        h2 = TB[:, 2 * KD * GN:4 * KD * GN].rearrange("p (b k n) -> p b k n", b=2, k=KD)
        acc = TB[:, 4 * KD * GN:4 * KD * GN + 2 * GT * D].rearrange("p (b s n) -> p b s n", b=2, s=GT)
        xg = CB[:, 0:2 * KD * GN].rearrange("p (b k n) -> p b k n", b=2, k=KD)
        sq = CB[:, 2 * KD * GN:2 * KD * GN + 2 * D].rearrange("p (b n) -> p b n", b=2)
        xf = CB[:, 2 * KD * GN + 2 * D:2 * KD * GN + 4 * D].rearrange("p (b n) -> p b n", b=2)
        o = 2 * KD * GN + 4 * D
        gnA, gnc, gnt = [CB[:, o + n * D:o + (n + 1) * D] for n in range(3)]
        wT = CB[0:EX, o + 3 * D:o + 3 * D + GN]
        assert o + 3 * D + GN <= NT * CW

        ident = sb("ident", [P, P])
        ones = sb("ones", [P, P])
        ones_last = sb("ones_last", [P, P])
        node = sb("node", [P, NT], I32)
        lk = sb("lk", [LP, LC], I32)
        lo = sb("lo", [LP, LC], I32)
        hi = sb("hi", [LP, LC], I32)
        tabs = sb("tabs", [P, 24, NT])
        (hist, tot, incl, bf, cnt, ends, starts, edges, deg, dinv, has, nohas, mean, var, rstd,
         nmr, rn, opr, ta, tb_, tc, posf, one_nt, spare) = [tabs[:, n, :] for n in range(24)]
        bidx = sb("bidx", [P, NT], I32)
        pos = sb("pos", [P, NT], I32)
        bn6 = sb("bn6", [P, 2, 6])
        mv = sb("mv", [P, 2, 2])
        nrm = sb("nrm", [P, 8])
        esum = sb("esum", [P, 4 * AH])
        iw = sb("iw", [P, U], I32)
        wr = sb("wr", [P, KD, EX])
        bo = sb("bo", [EX, D])
        gpre = sb("gpre", [P, KD])
        rows = sb("rows", [P, 4, D])
        conv_b, gn_w, gn_b, gn_s = [rows[:, n, :] for n in range(4)]
        b_comb = sb("b_comb", [P, CW])
        b_r = sb("b_r", [P, EX])
        bnp = sb("bnp", [5 * EX * KD, 2, P])
        bnT = sb("bnT", [P, 2, 5 * EX * KD])
        bns = sb("bns", [P, 2, EX * KD])
        bnb = sb("bnb", [P, 2, EX * KD])
        bnt = sb("bnt", [P, 2, EX * KD])
        diag = sb("diag", [P, P])
        mk = sb("mk", [P, 2, MEM])
        mkm = sb("mkm", [P, 8])
        mT = sb("mT", [MEM, 2 * P + 1])
        col = sb("col", [P, 24])
        nidx = sb("nidx", [P, 1], I32)
        fidx = sb("fidx", [P, 1], I32)
        small = sb("small", [P, 2, 32])
        lg = sb("lg", [P, GT, EX])
        wsm = sb("wsm", [P, 2, GT, EX])
        rsm = sb("rsm", [P, 2, GT])
        cf = sb("cf", [P, 2, 8])

        bank = [ctx.enter_context(nc.psum_tensor(f"bank{n}", [P, 512], F32)) for n in range(8)]

        tbl, xtd, Wd, e_d = scratch["tbl"], scratch["xtd"], (scratch["maxes"], scratch["sums"]), scratch["ends"]
        tbl_p = tbl.rearrange("(i p) f -> p i f", p=P)
        x_in = a["x"]
        W_run = [w.rearrange("(p t) f -> p (t f)", p=P) for w in Wd]
        src1, dst1 = a["src"], a["dst"]
        dst_blocks = dst1.rearrange("(k j) -> k j", j=LB)

        def row_of(v):
            return v.partition_broadcast(P)

        s_pad = sem("s_pad"); s_lk = sem("s_lk")
        XCH = 4
        s_x = [sem(f"s_x{n}") for n in range(XCH + 1)]
        s_runs = sem("s_runs"); s_w = sem("s_w"); s_wide = sem("s_wide")
        s_mask = sem("s_mask"); s_con = sem("s_con"); s_blk = sem("s_blk")
        s_oh = sem("s_oh"); s_hist = sem("s_hist"); s_hists = sem("s_hists"); s_pref = sem("s_pref"); s_bidx = sem("s_bidx")
        s_dve = sem("s_dve"); s_act = sem("s_act")
        s_step = sem("s_step"); s_q1 = sem("s_q1"); s_q2 = sem("s_q2")
        s_xs = sem("s_xs"); s_tr = sem("s_tr"); s_xt = sem("s_xt"); s_bs = sem("s_bs"); s_tb = sem("s_tb")
        s_xst = [sem("s_xst0"), sem("s_xst1")]
        s_e = sem("s_e"); s_eT = sem("s_eT"); s_eTs = sem("s_eTs"); s_ed = sem("s_ed"); s_sld = sem("s_sld")
        s_sT = sem("s_sT"); s_dv = sem("s_dv"); s_tbl = sem("s_tbl")
        s_bnT = sem("s_bnT"); s_bnv = sem("s_bnv"); s_bnq = sem("s_bnq")
        s_g = [sem(f"s_g{u}") for u in range(U)]
        s_iw = sem("s_iw"); s_prod = sem("s_prod"); s_max = sem("s_max"); s_sum = sem("s_sum"); s_seen = sem("s_seen")
        s_out = [sem("s_out0"), sem("s_out1")]
        s_xl = [sem("s_xl0"), sem("s_xl1")]
        s_pu = sem("s_pu"); s_kb = sem("s_kb"); s_kt = sem("s_kt"); s_ek = sem("s_ek"); s_cx = sem("s_cx")
        s_Mw = sem("s_Mw"); s_MT = sem("s_MT"); s_dg = sem("s_dg"); s_Mb = sem("s_Mb"); s_mk = sem("s_mk")
        s_em = sem("s_em"); s_emT = sem("s_emT"); s_emc = sem("s_emc"); s_mem = sem("s_mem")
        s_cbd = sem("s_cbd"); s_cT = sem("s_cT"); s_cTc = sem("s_cTc"); s_m2 = sem("s_m2"); s_m2c = sem("s_m2c")
        s_qd = sem("s_qd"); s_eq = sem("s_eq"); s_qn = sem("s_qn"); s_qT = sem("s_qT"); s_qTc = sem("s_qTc")
        s_mx = sem("s_mx"); s_mo = sem("s_mo"); s_nr = sem("s_nr"); s_xb = sem("s_xb")
        s_nix = sem("s_nix"); s_en = sem("s_en"); s_dgw = sem("s_dgw"); s_Bw = sem("s_Bw")
        s_tl = sem("s_tl"); s_car = sem("s_car"); s_carT = sem("s_carT"); s_fixg = sem("s_fixg"); s_fix = sem("s_fix"); s_fixs = sem("s_fixs"); s_fz = sem("s_fz")
        s_gf = [sem(f"s_gf{j}") for j in range(GR)]
        s_ag = sem("s_ag"); s_pr = sem("s_pr"); s_ph = sem("s_ph"); s_h = sem("s_h"); s_sm = sem("s_sm")
        s_sq = sem("s_sq"); s_hc = sem("s_hc"); s_vr = sem("s_vr"); s_gq = sem("s_gq"); s_gr = sem("s_gr")
        s_ew = sem("s_ew"); s_f1 = sem("s_f1"); s_f2 = sem("s_f2"); s_f3 = sem("s_f3"); s_f4 = sem("s_f4"); s_f5 = sem("s_f5")
        s_L1 = sem("s_L1"); s_h1 = sem("s_h1"); s_L2 = sem("s_L2"); s_h2 = sem("s_h2"); s_L3 = sem("s_L3"); s_acc = sem("s_acc")
        s_lg = sem("s_lg"); s_lm = sem("s_lm"); s_le = sem("s_le"); s_ws = sem("s_ws"); s_wT = sem("s_wT"); s_wTc = sem("s_wTc")
        s_y = [sem("s_y0"), sem("s_y1")]

        CONST = 7
        block = ctx.enter_context(nc.Block())

        @block.sync
        def _(sp):
            with nc.allow_non_contiguous_dma(reason="one edge of each block"):
                sp.dma_start(lk[:, :], dst1.rearrange("(p c j) -> p c j", c=LC, j=LB)[:, :, LB - 1]).then_inc(s_lk, 16)
            tiles = (NT - 1) // XCH
            for n in range(XCH):
                sp.dma_start(X3[:, n * tiles:(n + 1) * tiles, :],
                             x_in[n * tiles * P:(n + 1) * tiles * P, :].rearrange("(i p) d -> p i d", p=P)).then_inc(s_x[n], 16)
            sp.wait_ge(s_pad, 5)
            sp.dma_start(X3[0:LAST, NT - 1, :], x_in[(NT - 1) * P:N, :]).then_inc(s_x[XCH], 16)
            even = FULL // 16 * 16
            for n, (v, at) in enumerate(((dst1, dst_all[:, 1:T + 1]), (src1, idx_all[:, 0:T]))):
                sp.dma_start(at[0:even, :], v[0:even * T].rearrange("(p t) -> p t", t=T)).then_inc(s_runs, 16)
                sp.dma_start(at[even:FULL, :], v[even * T:FULL * T].rearrange("(p t) -> p t", t=T)).then_inc(s_runs, 16)
                sp.dma_start(at[FULL:FULL + 1, 0:REST], v[FULL * T:E].rearrange("(p t) -> p t", p=1)).then_inc(s_runs, 16)
            with nc.allow_non_contiguous_dma(reason="the edge before each run"):
                sp.dma_start(dst_all[1:P, 0:1], 
                             dst1[0:(P - 1) * T].rearrange("(p t) -> p t", t=T)[:, T - 1:T]).then_inc(s_runs, 16)
            with sp.Fori(0, PAIRS) as i:
                for h in range(2):
                    sp.wait_ge(s_xt, done(i * 2 + h))
                    sp.dma_start(xtd[bass.ds((i * 2 + h) * P, P), :], xt[:, h, :, :].rearrange("p k n -> p (k n)")).then_inc(s_xst[h], 16)
            sp.wait_ge(s_xt, done(NT - 1))
            sp.dma_start(xtd[(NT - 1) * P:NT * P, :], xt[:, 0, :, :].rearrange("p k n -> p (k n)")).then_inc(s_xst[0], 16)
            sp.wait_ge(s_eTs, 1)
            sp.dma_start(e_d[1:NT * P + 1, :].rearrange("(i p) a -> i (p a)", p=P), endsT[:, :]).then_inc(s_ed, 16)
            sp.wait_ge(s_con, CONST)
            sp.dma_start(e_d[0:1, :], upto[1:2, 0:1]).then_inc(s_ed, 16)
            sp.wait_ge(s_ed, 32)
            sp.dma_start(startsT[:, :], e_d[0:NT * P, :].rearrange("(i p) a -> i (p a)", p=P)).then_inc(s_sld, 16)
            sp.wait_ge(s_dv, 1)
            sp.dma_start(tbl_p, TB3).then_inc(s_tbl, 16)

            def window(w, loads=(None, None)):
                for h in range(2):
                    if loads[h]:
                        load_tile(*loads[h])
                    sp.wait_ge(s_max, w * U + (h + 1) * HW + U)
                    sp.wait_ge(s_sum, w * U + (h + 1) * HW + U)
                    for to, ring_, c in ((W_run[0], stm, BF), (W_run[1], sts, 2 * BF)):
                        sp.dma_start(to[:, bass.ds(w * (U * c) + h * HW * c, HW * c)],
                                     ring_[:, h * HW:(h + 1) * HW, :].rearrange("p a b -> p (a b)")).then_inc(s_out[h], 16)

            def load_tile(n, ti, h):
                sp.wait_ge(s_pu, free(n))
                sp.dma_start(xl[:, h, :, :].rearrange("p k n -> p (k n)"), xtd[bass.ds(ti * P, P), :]).then_inc(s_xl[h], 16)

            sp.wait_ge(s_xst[0], 16 * PASS + 16)
            sp.wait_ge(s_xst[1], 16 * PAIRS + 16)
            load_tile(0, 0, 0)
            load_tile(1, 1, 1)
            for ps in range(3):
                n0 = ps * UNITS
                for h in range(2):
                    load_tile(n0 + 2 + h, 2 + h, h)
                with sp.Fori(0, PAIRS - 2) as i:
                    window(i + ps * PASS, [(i * 2 + (n0 + 4 + h), i * 2 + (4 + h), h) for h in range(2)])
                window(ps * PASS + PAIRS - 2, ((n0 + NT - 1, NT - 1, 0), None))
                window(ps * PASS + PAIRS - 1, [(n0 + UNITS + h, h, h) if ps < 2 else None for h in range(2)])
                window(ps * PASS + PAIRS)
            with sp.Fori(3 * PASS, WIN) as w:
                window(w)
            sp.wait_ge(s_ph, done(NT - 1))
            for n, name in enumerate(("L0_ffn_W1", "L0_ffn_W2", "L0_ffn_Wo")):
                for k in range(KD):
                    sp.dma_start(EW[n][:, :, k, :], a[name][:, k * P:(k + 1) * P, :].rearrange("e p n -> p e n")).then_inc(s_ew, 16)

            def store(g, b, first, n=GT):
                sp.wait_ge(s_acc, (g + 1) * (ROUNDS * GT) + GT)
                if n == GT:
                    sp.dma_start(y[bass.ds(g * GN, GN), :].rearrange("(s p) d -> p s d", p=P), acc[:, b, :, :]).then_inc(s_y[b], 16)
                else:
                    sp.dma_start(y[(NT - 1) * P:N, :], acc[0:LAST, b, 0, :]).then_inc(s_y[b], 16)

            with sp.Fori(0, GROUPS // 2 - 1) as i:
                store(i * 2, 0, None)
                store(i * 2 + 1, 1, None)
            store(GROUPS - 2, 0, None)
            store(GROUPS - 1, 1, None)
            store(GROUPS, 0, None, 1)
            sp.wait_ge(s_y[0], 16 * (GROUPS // 2 + 1) + 16)
            sp.wait_ge(s_y[1], 16 * (GROUPS // 2) + 16)

        @block.gpsimd
        def _(pool):
            pool.iota(iota[:, :], pattern=[[1, P]], base=0, channel_multiplier=0).then_inc(s_con, 1)
            pool.iota(node[:, :], pattern=[[P, NT]], base=0, channel_multiplier=1).then_inc(s_con, 1)
            pool.memset(ident[:, :], 0.0).then_inc(s_mask, 1)
            pool.memset(ones[:, :], 1.0).then_inc(s_con, 1)
            pool.wait_ge(s_con, 3)
            pool.wait_ge(s_mask, 1)
            pool.affine_select(out=upto[:, :], in_=ones[:, :], compare_op=ALU.is_ge, fill=0.0, base=0,
                               pattern=[[1, P]], channel_multiplier=-1).then_inc(s_con, 1)
            pool.affine_select(out=ident[:, :], in_=ident[:, :], compare_op=ALU.not_equal, fill=1.0, base=0,
                               pattern=[[-1, P]], channel_multiplier=1).then_inc(s_con, 1)
            pool.affine_select(out=ones_last[:, :], in_=ones[:, :], compare_op=ALU.is_ge, fill=0.0, base=LAST - 1,
                               pattern=[[0, P]], channel_multiplier=-1).then_inc(s_con, 1)
            pool.memset(TB3[:, :, BF + 1:RW], 0.0).then_inc(s_con, 1)
            for n, name in enumerate(("L0_gnn_conv_bias", "L0_gnn_gn_weight", "L0_gnn_gn_bias", "L0_gnn_gn_mean_scale")):
                pool.dma_start(rows[:, n, :], row_of(a[name])).then_inc(s_wide, 16)
            pool.dma_start(b_comb[:, :], row_of(a["L0_gnn_b_comb"])).then_inc(s_wide, 16)
            pool.dma_start(b_r[:, :], row_of(a["L0_ffn_br"])).then_inc(s_wide, 16)
            pool.wait_ge(s_bidx, 1)
            for i in range(NT):
                pool.indirect_dma_start(out=blk[:, i, :], out_offset=None, in_=dst_blocks,
                                        in_offset=bass.IndirectOffsetOnAxis(ap=bidx[:, i:i + 1], axis=0)).then_inc(s_blk, 16)
            pool.wait_ge(s_ed, 32)
            pool.wait_ge(s_nix, 1)
            pool.indirect_dma_start(out=col[:, 3:4], out_offset=None, in_=e_d[:, :],
                                    in_offset=bass.IndirectOffsetOnAxis(ap=nidx[:, 0:1], axis=0)).then_inc(s_en, 16)
            pool.wait_ge(s_tbl, 16)
            pool.dma_start(b_out, row_of(a["L0_mix_b_out"])).then_inc(s_wide, 16)
            pool.dma_start(g_out, row_of(a["L0_mix_g_out"])).then_inc(s_wide, 16)
            with pool.Fori(0, WIN) as w:
                for u in range(U):
                    if u % HW == 0:
                        pool.wait_ge(s_iw, w * 2 + u // HW + 1)
                    if u % 4 == 0:
                        pool.wait_ge(s_max, w * U + u + 4)
                        pool.wait_ge(s_sum, w * U + u + 4)
                        pool.sem_inc(s_seen, 1)
                    pool.indirect_dma_start(out=ring[:, u, 0:RW], out_offset=None, in_=tbl[:, :],
                                            in_offset=bass.IndirectOffsetOnAxis(ap=iw[:, u:u + 1], axis=0)).then_inc(s_g[u], 16)
            pool.wait_ge(s_iw, 2 * WIN + 2)
            pool.wait_ge(s_out[0], 32 * WIN + 32)
            pool.wait_ge(s_out[1], 32 * WIN + 32)
            pool.wait_ge(s_fz, 1)
            at = bass.IndirectOffsetOnAxis(ap=fidx[:, 0:1], axis=0)
            parts = ((Wd[0], 0, BF), (Wd[1], BF, ST))
            for wd, c0, c1 in parts:
                pool.indirect_dma_start(out=fix[:, c0:c1], out_offset=None, in_=wd[:, :], in_offset=at,
                                        bounds_check=E - 1, oob_is_err=False).then_inc(s_fixg, 16)
            pool.wait_ge(s_fix, 3)
            for wd, c0, c1 in parts:
                pool.indirect_dma_start(out=wd[:, :], out_offset=at, in_=fix[:, c0:c1], in_offset=None,
                                        bounds_check=E - 1, oob_is_err=False).then_inc(s_fixs, 16)
            pool.wait_ge(s_fixs, 32)
            for i in range(NT):
                if i >= GR:
                    pool.wait_ge(s_pr, done(i - GR))
                for wd, c0, c1 in parts:
                    pool.indirect_dma_start(out=got[:, i % GR, c0:c1], out_offset=None, in_=wd[:, :],
                                            in_offset=bass.IndirectOffsetOnAxis(ap=pos[:, i:i + 1], axis=0)).then_inc(s_gf[i % GR], 16)

        @block.scalar
        def _(act):
            act.dma_start(wb[:, :, :], a["L0_gnn_W_bases"].rearrange("(k p) n -> p k n", p=P)).then_inc(s_w, 16)
            act.dma_start(wc[:, :, 0:CW], a["L0_gnn_W_comb"].rearrange("(k p) n -> p k n", p=P)).then_inc(s_w, 16)
            wq = a["L0_mix_w_qkv"].rearrange("(k p) n -> p k n", p=P)
            act.dma_start(wc[:, :, CW:CW + 2 * HID], wq[:, :, HID:3 * HID]).then_inc(s_w, 16)
            act.dma_start(wc[:, :, CW + 2 * HID:CW + 3 * HID], wq[:, :, 0:HID]).then_inc(s_w, 16)
            act.dma_start(wo[:, :], a["L0_mix_w_out"]).then_inc(s_w, 16)
            act.dma_start(wr[:, :, :], a["L0_ffn_Wr"].rearrange("(k p) n -> p k n", p=P)).then_inc(s_w, 16)
            act.dma_start(bo[:, :], a["L0_ffn_bo"]).then_inc(s_w, 16)
            for l in range(2):
                for n, name in enumerate(("b", "g", "be", "m", "v")):
                    act.dma_start(bnp[n * EX * KD:(n + 1) * EX * KD, l, :],
                                  a[f"L0_ffn_{name}{l + 1}"].rearrange("e (k p) -> (e k) p", p=P)).then_inc(s_w, 16)
            for n in range(2):
                act.dma_start(mk[:, n, :], a["L0_mix_mem_kv"][n].rearrange("h d m -> (h d) m")).then_inc(s_w, 16)
            with nc.allow_non_contiguous_dma(reason="a vector as columns"):
                act.dma_start(gpre[:, :], a["L0_mix_g_pre"].rearrange("(k p) -> p k", p=P)).then_inc(s_w, 16)
            for s in (s_xt, s_tb, s_ek, s_h, s_sq, s_f2, s_f5):
                act.sem_inc(s, RING2)
            act.sem_inc(s_h1, 2 * KD)
            act.sem_inc(s_h2, 2 * KD)
            act.wait_ge(s_q1, 1)
            act.activation(tb_, ta, ACT.Sqrt).then_inc(s_q2, 1)
            act.wait_ge(s_q1, 2)
            act.activation(tb_, ta, ACT.Sqrt).then_inc(s_q2, 1)

            def tile_a(n, i, h):
                act.wait_ge(s_tr, done(n))
                act.wait_ge(s_bs, free(n))
                act.wait_ge(s_xst[h], i * 16 + 16)
                act.activation(xt[:, h, :, :].rearrange("p k n -> p (k n)"), bank[5 * h][:, 0:D], ACT.Copy).then_inc(s_xt, 1)

            def tile_b(n, h):
                act.wait_ge(s_bs, done(n))
                act.activation(TB3[:, bass.ds(n, 1), 0:BF].rearrange("p a f -> p (a f)"), bank[1 + h][:, 0:BF], ACT.Copy).then_inc(s_tb, 1)

            with act.Fori(0, PAIRS) as i:
                for h in range(2):
                    tile_a(i * 2 + h, i, h)
                for h in range(2):
                    tile_b(i * 2 + h, h)
            tile_a(NT - 1, PAIRS, 0)
            tile_b(NT - 1, 0)
            act.wait_ge(s_q1, 3)
            act.activation(tb_, ta, ACT.Sqrt).then_inc(s_q2, 1)
            act.wait_ge(s_runs, 16 * 7)
            act.wait_ge(s_pad, 5)
            for h in range(2):
                act.copy(iw[:, h * HW:(h + 1) * HW], idx_all[:, h * HW:(h + 1) * HW]).then_inc(s_iw, 1)
            act.wait_ge(s_bnv, 1)
            act.activation(bnt[:, :, :].rearrange("p a b -> p (a b)"), bns[:, :, :].rearrange("p a b -> p (a b)"), ACT.Sqrt).then_inc(s_bnq, 1)

            def window(w, hook):
                for u in range(U):
                    act.wait_ge(s_g[u], w * 16 + 16)
                    act.activation(ring[:, u, RW:RW + BF], ring[:, u, 0:BF], ACT.Copy, scale=ring[:, u, BF:BF + 1]).then_inc(s_prod, 1)
                    if u % HW == HW - 1:
                        h = u // HW
                        act.copy(iw[:, h * HW:(h + 1) * HW], idx_all[:, bass.ds(w * U + U + h * HW, HW)]).then_inc(s_iw, 1)
                    if hook:
                        hook(u)

            def pass_c(n, h, s, last=False):
                R = LAST if last else P
                if s == 2:
                    act.wait_ge(s_pu, done(n + UNITS))
                    act.wait_ge(s_cx, free(n))
                    act.activation(vs[0:R, h, 0:HID], bank[5 + h][0:R, 0:HID], ACT.Copy, scale=rn[0:R, bass.ds(n, 1)])
                    act.wait_ge(s_kt, done(n))
                    act.activation(ek[0:R, h, :], kt[0:R, h, :], ACT.Exp).then_inc(s_ek, 2 if last else 1)

            def pass_d(i, u, m=2):
                if u == 2:
                    act.wait_ge(s_qd, i + 1)
                    for h in range(m):
                        e = act.activation(eq[:, h, :], qd[:, h, :], ACT.Exp, scale=rn[:, bass.ds(i * 2 + h, 1)])
                    e.then_inc(s_eq, 1)
                if u == 4:
                    for h in range(m):
                        x1 = X3[:, bass.ds(i * 2 + h, 1), :].rearrange("p a f -> p (a f)")
                        act.activation(x1, x1, ACT.Identity, scale=opr[:, bass.ds(i * 2 + h, 1)], bias=nmr[:, bass.ds(i * 2 + h, 1)])
                if u == 7:
                    act.wait_ge(s_qT, i + 1)
                    act.activation(qT[:, 0:m, :], bank[4][:, 0:m * P].rearrange("p (b n) -> p b n", b=m), ACT.Copy).then_inc(s_qTc, 1)
                if u == 9:
                    act.wait_ge(s_mx, i + 1)
                    for h in range(m):
                        q = act.activation(xs[:, h, :], bank[5 + h][:, 0:D], ACT.Square, accum_out=nrm[:, h:h + 1])
                    q.then_inc(s_act, 1)
                    act.wait_ge(s_act, i + 1)
                    act.activation(nrm[:, 2:2 + m], nrm[:, 0:m], ACT.Sqrt).then_inc(s_nr, 1)

            with act.Fori(0, PASS) as w:
                window(w, None)
            act.wait_ge(s_em, 1)
            act.activation(mkm[:, 0:MEM], mk[:, 0, :], ACT.Exp, bias=col[:, 8:9]).then_inc(s_em, 1)
            act.wait_ge(s_emT, 1)
            act.activation(mT[:, 0:2 * P], bank[6][0:MEM, 0:2 * P], ACT.Copy).then_inc(s_emc, 1)
            with act.Fori(0, PAIRS) as i:
                window(i + PASS, lambda u: pass_c(i * 2 + u // HW, u // HW, u % HW))
            window(PASS + PAIRS, lambda u: pass_c(NT - 1, 0, u, True) if u < HW else None)
            act.wait_ge(s_cT, 1)
            act.activation(diag[:, :], bank[7][:, 256:384], ACT.Copy).then_inc(s_cTc, 1)
            act.wait_ge(s_m2, 1)
            act.activation(m2[:, :], bank[7][:, 0:D], ACT.Copy).then_inc(s_m2c, 1)
            with act.Fori(0, PAIRS) as i:
                window(i + 2 * PASS, lambda u: pass_d(i, u))
            window(2 * PASS + PAIRS, lambda u: pass_d(PAIRS, u, 1))
            with act.Fori(3 * PASS, WIN) as w:
                window(w, None)

            def h_out(n, b):
                act.wait_ge(s_ph, done(n))
                act.activation(H3[:, bass.ds(n, 1), :].rearrange("p a f -> p (a f)"), bank[1 + b][:, 0:D], ACT.Copy).then_inc(s_h, 1)

            with act.Fori(0, PAIRS) as i:
                for b in range(2):
                    h_out(i * 2 + b, b)
            h_out(NT - 1, 0)

            def square(n, b):
                act.wait_ge(s_hc, n + 1)
                act.wait_ge(s_vr, free(n))
                act.activation(sq[:, b, :], H3[:, bass.ds(n, 1), :].rearrange("p a f -> p (a f)"), ACT.Square).then_inc(s_sq, 1)

            with act.Fori(0, PAIRS) as i:
                for b in range(2):
                    square(i * 2 + b, b)
            square(NT - 1, 0)
            act.wait_ge(s_gq, 1)
            act.activation(gnt[:, :], gnc[:, :], ACT.Sqrt).then_inc(s_gr, 1)

            def front_sqrt(n, b):
                act.wait_ge(s_f1, done(n))
                act.activation(cf[:, b, 2:3], cf[:, b, 1:2], ACT.Sqrt).then_inc(s_f2, 1)

            def front_out(n, b, gb, s):
                act.wait_ge(s_f4, done(n))
                act.activation(xg[:, gb, :, s * P:(s + 1) * P], bank[6][:, 0:D].rearrange("p (k n) -> p k n", k=KD),
                               ACT.Copy).then_inc(s_f5, 1)

            def evac(l, g, e, gb, w):
                src, sL, hb, sh, sN = ((0, s_L1, h1, s_h1, s_L2), (2, s_L2, h2, s_h2, s_L3))[l]
                q2 = g * (2 * EX) + 2 * e
                for m in range(KD):
                    act.wait_ge(sL, q2 + m + 5)
                    if m == 0 and l == 0:
                        act.wait_ge(s_L2, q2 + 2)
                    if m == 0 and l == 1:
                        act.wait_ge(s_L3, g * (ROUNDS * GT) + e * GT + (GT if e >= 2 else 0) + L3_START - 2 * GT)
                    act.activation(hb[:, e % 2, m, 0:w], bank[src + m][:, 0:w], ACT.Relu,
                                   bias=bnb[:, l, e * KD + m:e * KD + m + 1], scale=bns[:, l, e * KD + m:e * KD + m + 1]).then_inc(sh, 1)

            def group(g, gb, w, nxt, n_next):
                ng = w // P
                evac(0, g, 0, gb, w)
                for e in range(EX):
                    if e == 0:
                        act.wait_ge(s_lm, g + 1)
                        act.activation(lg[:, 0:ng, :], lg[:, 0:ng, :], ACT.Exp).then_inc(s_le, 1)
                    if e == 1:
                        act.wait_ge(s_wT, g + 1)
                        act.activation(wT[:, 0:w], bank[7][0:EX, 0:w], ACT.Copy).then_inc(s_wTc, 1)
                    if e + 1 < EX:
                        evac(0, g, e + 1, gb, w)
                    evac(1, g, e, gb, w)
                    if 3 <= e < 3 + n_next:
                        front_out(nxt * GT + e - 3, (e - 3) % 2, 1 - gb, e - 3)
                    if e < n_next:
                        front_sqrt(nxt * GT + e, e % 2)

            for s in range(GT):
                front_sqrt(s, s % 2)
                front_out(s, s % 2, 0, s)
            with act.Fori(0, GROUPS // 2 - 1) as i:
                group(i * 2, 0, GN, i * 2 + 1, GT)
                group(i * 2 + 1, 1, GN, i * 2 + 2, GT)
            group(GROUPS - 2, 0, GN, GROUPS - 1, GT)
            group(GROUPS - 1, 1, GN, GROUPS, 1)
            group(GROUPS, 0, P, None, 0)

        @block.tensor
        def _(pe):
            for s in (s_tr, s_bs, s_pu, s_cx, s_ph, s_vr, s_f4):
                pe.sem_inc(s, RING2)
            pe.sem_inc(s_L1, 4)
            pe.sem_inc(s_wTc, 1)
            pe.sem_inc(s_L2, 4)
            pe.sem_inc(s_L3, L3_START)
            pe.wait_ge(s_con, CONST)
            pe.wait_ge(s_oh, 2)
            for c in range(LC):
                mm = pe.matmul(bank[3][:, 0:NT], oh_lo[:, c, :], oh_hi[:, c, :], start=(c == 0), stop=(c == LC - 1))
            mm.then_inc(s_hist, 1)
            pe.wait_ge(s_hists, 1)
            pe.matmul(bank[3][:, 64:64 + NT], upto[:, :], hist, start=True, stop=True)
            pe.matmul(bank[3][:, 128:128 + NT], ones[:, :], hist, start=True, stop=True).then_inc(s_pref, 1)
            pe.wait_ge(s_w, 16 * 20)

            def turn(n, h):
                pe.wait_ge(s_xs, done(n))
                pe.wait_ge(s_xt, free(n))
                for k in range(KD):
                    mm = pe.transpose(bank[5 * h][:, k * P:(k + 1) * P], xs[:, h, k * P:(k + 1) * P], ident[:, :])
                mm.then_inc(s_tr, 1)

            def base(n, h):
                pe.wait_ge(s_xt, done(n))
                pe.wait_ge(s_tb, free(n))
                for k in range(KD):
                    mm = pe.matmul(bank[1 + h][:, 0:BF], xt[:, h, k, :], wb[:, k, :], start=(k == 0), stop=(k == KD - 1))
                mm.then_inc(s_bs, 1)

            with pe.Fori(0, PAIRS) as i:
                for h in range(2):
                    turn(i * 2 + h, h)
                for h in range(2):
                    base(i * 2 + h, h)
            turn(NT - 1, 0)
            base(NT - 1, 0)
            pe.wait_ge(s_e, 1)
            pe.transpose(bank[3][0:NT, 0:P], ends, ident[:, :]).then_inc(s_eT, 1)
            pe.wait_ge(s_sld, 16)
            pe.transpose(bank[3][:, 128:128 + NT], startsT[:, :], ident[0:NT, 0:NT]).then_inc(s_sT, 1)
            for l in range(2):
                mm = pe.transpose(bank[4][:, l * P:l * P + 5 * EX * KD], bnp[:, l, :], ident[0:5 * EX * KD, 0:5 * EX * KD])
            mm.then_inc(s_bnT, 1)
            pe.wait_ge(s_dgw, 1)
            pe.matmul(bank[0][:, 0:P], ones[:, :], diag[:, :], start=True, stop=True).then_inc(s_Bw, 1)

            def unit(ps, i, h, parts, inc=1):
                pe.wait_ge(s_xl[h], i * 16 + 16 * (ps * (PAIRS if h else PASS) + 1))
                for to, c0, c1 in parts:
                    for k in range(KD):
                        mm = pe.matmul(bank[to + h][:, 0:c1 - c0], xl[:, h, k, :], wc[:, k, c0:c1], start=(k == 0), stop=(k == KD - 1))
                mm.then_inc(s_pu, inc)

            pe.wait_ge(s_tb, done(NT - 1))
            pe.wait_ge(s_mask, 3)
            with pe.Fori(0, PAIRS) as i:
                for h in range(2):
                    pe.wait_ge(s_kb, free(i * 2 + h))
                    unit(0, i, h, ((1, 0, CW + HID),))
            pe.wait_ge(s_kb, free(NT - 1))
            unit(0, PAIRS, 0, ((1, 0, CW + HID),), 2)
            pe.wait_ge(s_Mw, 1)
            pe.transpose(bank[7][:, 384:512], M[:, :], ident[:, :]).then_inc(s_MT, 1)
            pe.wait_ge(s_dg, 1)
            pe.matmul(bank[7][:, 256:384], ones[:, :], diag[:, :], start=True, stop=True).then_inc(s_Mb, 1)
            pe.wait_ge(s_em, 2)
            pe.transpose(bank[6][0:MEM, 0:P], mkm[:, 0:MEM], ident[:, :])
            pe.transpose(bank[6][0:MEM, P:2 * P], mk[:, 1, :], ident[:, :]).then_inc(s_emT, 1)
            pe.wait_ge(s_emc, 1)
            pe.wait_ge(s_mem, 1)
            pe.matmul(bank[3][:, 0:HID + 1], mT[:, 0:P], mT[:, P:2 * P + 1], start=True, stop=False)

            def ctx_mm(n, h, last=False):
                R = LAST if last else P
                pe.wait_ge(s_ek, done(n))
                pe.matmul(bank[3][:, 0:HID + 1], ek[0:R, h, :], vs[0:R, h, :], start=False, stop=last).then_inc(s_cx, 2 if last else 1)

            def kv(n, i, h, inc=1):
                pe.wait_ge(s_kt, free(n))
                pe.wait_ge(s_ek, free(n))
                unit(1, i, h, ((1, CW, CW + HID), (5, CW + HID, CW + 2 * HID)), inc)

            pe.wait_ge(s_kb, done(NT))
            for h in range(2):
                kv(h, 0, h)
            with pe.Fori(0, PAIRS - 1) as i:
                for h in range(2):
                    ctx_mm(i * 2 + h, h)
                    kv(i * 2 + (2 + h), i + 1, h)
            ctx_mm(NT - 3, 0)
            kv(NT - 1, PAIRS, 0, 2)
            ctx_mm(NT - 2, 1)
            ctx_mm(NT - 1, 0, True)
            pe.wait_ge(s_cbd, 1)
            pe.transpose(bank[7][:, 256:384], diag[:, :], ident[:, :]).then_inc(s_cT, 1)
            pe.wait_ge(s_cTc, 1)
            pe.matmul(bank[7][:, 0:D], diag[:, :], wo[:, :], start=True, stop=True).then_inc(s_m2, 1)
            pe.wait_ge(s_m2c, 1)

            def q_mm(i, m=2):
                for h in range(m):
                    unit(2, i, h, ((1, CW + 2 * HID, CW + 3 * HID),), 3 - m)

            def mix(i, m=2):
                pe.wait_ge(s_qn, i + 1)
                for h in range(m):
                    mm = pe.transpose(bank[4][:, h * P:(h + 1) * P], qn[:, h, :], ident[:, :])
                mm.then_inc(s_qT, 1)
                pe.wait_ge(s_qTc, i + 1)
                pe.wait_ge(s_mo, i + 1)
                for h in range(m):
                    pe.matmul(bank[5 + h][:, 0:D], ones[0:1, 0:P], b_out[0:1, :], start=True, stop=False)
                    mm = pe.matmul(bank[5 + h][:, 0:D], qT[:, h, :], m2[:, :], start=False, stop=True)
                mm.then_inc(s_mx, 1)

            pe.wait_ge(s_kt, done(NT))
            pe.wait_ge(s_ek, done(NT))
            q_mm(0)
            with pe.Fori(0, PAIRS - 1) as i:
                pe.wait_ge(s_qd, i + 1)
                q_mm(i + 1)
                mix(i)
            pe.wait_ge(s_qd, PAIRS)
            q_mm(PAIRS, 1)
            mix(PAIRS - 1)
            mix(PAIRS, 1)

            pe.wait_ge(s_max, WIN * U + U)
            pe.wait_ge(s_sum, WIN * U + U)
            for n in range(AGGS):
                mm = pe.transpose(bank[4][:, n * P:(n + 1) * P], stm[:, U - 1, :] if n == 0 else sts[:, U - 1, (n - 1) * BF:n * BF], ident[:, :])
            mm.then_inc(s_tl, 1)
            pe.wait_ge(s_car, AGGS)
            pe.wait_ge(s_mo, PASS + 1)
            for n in range(AGGS):
                mm = pe.transpose(bank[5][:, n * P:(n + 1) * P], carT[:, n, 0:P], ident[:, :])
            mm.then_inc(s_carT, 1)

            def add_up(n, b):
                pe.wait_ge(s_pr, done(n))
                pe.wait_ge(s_h, free(n))
                for k in range(KC):
                    mm = pe.matmul(bank[1 + b][:, 0:D], ident[:, :], prod[:, b, k, :], start=(k == 0), stop=(k == KC - 1))
                mm.then_inc(s_ph, 1)

            def sum_nodes(n, start=False, stop=False):
                pe.wait_ge(s_h, done(n))
                return pe.matmul(bank[3][:, 0:D], ones[:, :], H3[:, bass.ds(n, 1), :].rearrange("p a f -> p (a f)"), start=start, stop=stop)

            add_up(0, 0)
            sum_nodes(0, start=True)
            with pe.Fori(0, PAIRS - 1) as i:
                add_up(i * 2 + 1, 1)
                add_up(i * 2 + 2, 0)
                sum_nodes(i * 2 + 1)
                sum_nodes(i * 2 + 2)
            add_up(NT - 2, 1)
            add_up(NT - 1, 0)
            sum_nodes(NT - 2)
            sum_nodes(NT - 1, stop=True).then_inc(s_sm, 1)

            def sum_squares(n, b, w, start=False, stop=False):
                pe.wait_ge(s_sq, done(n))
                pe.matmul(bank[4][:, 0:D], w, sq[:, b, :], start=start, stop=stop).then_inc(s_vr, 1)

            sum_squares(0, 0, ones[:, :], start=True)
            sum_squares(1, 1, ones[:, :])
            with pe.Fori(1, PAIRS) as i:
                for b in range(2):
                    sum_squares(i * 2 + b, b, ones[:, :])
            sum_squares(NT - 1, 0, ones_last[:, :], stop=True)

            def front_turn(n, b):
                pe.wait_ge(s_f3, done(n))
                pe.wait_ge(s_f5, done(n - 1))
                for k in range(KD):
                    mm = pe.transpose(bank[6][:, k * P:(k + 1) * P], xf[:, b, k * P:(k + 1) * P], ident[:, :])
                mm.then_inc(s_f4, 1)

            def layer(l, g, e, gb, w):
                q2 = g * (2 * EX) + 2 * e
                sL, sE = ((s_L1, s_h1), (s_L2, s_h2))[l]
                for m in range(KD):
                    pe.wait_ge(sE, q2 + m + 3)
                    if l == 1 and m == 0:
                        pe.wait_ge(s_h1, q2 + 2 + 4)
                    for k in range(KD):
                        rhs = xg[:, gb, k, 0:w] if l == 0 else h1[:, e % 2, k, 0:w]
                        mm = pe.matmul(bank[2 * l + m][:, 0:w], EW[l][:, e, k, m * P:(m + 1) * P], rhs, start=(k == 0), stop=(k == KD - 1))
                    mm.then_inc(sL, 1)

            def layer3(g, e, w):
                pe.wait_ge(s_h2, g * (2 * EX) + 2 * e + 2 + 4)
                ng = w // P
                for s in range(ng):
                    r = g * (ROUNDS * GT) + e * GT + s
                    if s % 2 == 0:
                        pe.wait_ge(s_acc, r + 2)
                    for k in range(KD):
                        mm = pe.matmul(bank[4 + s // 2][:, s % 2 * D:(s % 2 + 1) * D], h2[:, e % 2, k, s * P:(s + 1) * P],
                                       EW[2][:, e, k, :], start=(k == 0), stop=(k == KD - 1))
                    mm.then_inc(s_L3, 1 if ng == GT else GT)

            def router(g, gb, w):
                pe.wait_ge(s_wTc, g + 1)
                for s in range(w // P):
                    for k in range(KD):
                        mm = pe.matmul(bank[7][:, s * EX:(s + 1) * EX], xg[:, gb, k, s * P:(s + 1) * P], wr[:, k, :],
                                       start=(k == 0), stop=(k == KD - 1))
                mm.then_inc(s_lg, 1)

            def weights_out(g, gb, w):
                pe.wait_ge(s_ws, g + 1)
                for s in range(w // P):
                    mm = pe.transpose(bank[7][0:EX, s * P:(s + 1) * P], wsm[:, gb, s, :], ident[:, :])
                mm.then_inc(s_wT, 1)

            def bias_round(g, w):
                pe.wait_ge(s_wTc, g + 2)
                ng = w // P
                for s in range(ng):
                    r = g * (ROUNDS * GT) + EX * GT + s
                    if s % 2 == 0:
                        pe.wait_ge(s_acc, r + 2)
                    pe.matmul(bank[4 + s // 2][:, s % 2 * D:(s % 2 + 1) * D], wT[:, s * P:(s + 1) * P], bo[:, :],
                              start=True, stop=True).then_inc(s_L3, 1 if ng == GT else GT)

            def group(g, gb, w, nxt, n_next):
                pe.wait_ge(s_f5, g * GT + w // P + RING2)
                layer(0, g, 0, gb, w)
                router(g, gb, w)
                for e in range(EX):
                    if e + 1 < EX:
                        layer(0, g, e + 1, gb, w)
                    if e == 0:
                        weights_out(g, gb, w)
                    layer(1, g, e, gb, w)
                    if 2 <= e < 2 + n_next:
                        front_turn(nxt * GT + e - 2, (e - 2) % 2)
                    if e > 0:
                        layer3(g, e - 1, w)
                layer3(g, EX - 1, w)
                bias_round(g, w)

            for s in range(GT):
                front_turn(s, s % 2)
            pe.wait_ge(s_ew, 16 * 6)
            with pe.Fori(0, GROUPS // 2 - 1) as i:
                group(i * 2, 0, GN, i * 2 + 1, GT)
                group(i * 2 + 1, 1, GN, i * 2 + 2, GT)
            group(GROUPS - 2, 0, GN, GROUPS - 1, GT)
            group(GROUPS - 1, 1, GN, GROUPS, 1)
            group(GROUPS, 0, P, None, 0)

        @block.vector
        def _(v):
            ch = Chain(v, s_dve)
            for s in (s_xs, s_kb, s_kt, s_pr, s_f1, s_f3):
                v.sem_inc(s, RING2)
            v.sem_inc(s_acc, GT)
            for h in range(2):
                v.sem_inc(s_out[h], 32)
                v.sem_inc(s_y[h], 16)
                v.sem_inc(s_xst[h], 16)
            v.memset(idx_all[96:P, REST:T + U], 0).then_inc(s_pad, 1)
            v.memset(idx_all[0:96, T:T + U], 0).then_inc(s_pad, 1)
            v.memset(dst_all[96:P, REST + 1:T + 1], -1).then_inc(s_pad, 1)
            v.memset(dst_all[0:1, 0:1], -1).then_inc(s_pad, 1)
            v.memset(X3[96:P, NT - 1, :], 0.0).then_inc(s_pad, 1)

            def inv_root(y, val, t):
                ch(v.tensor_tensor(t, y, y, ALU.mult))
                ch(v.tensor_tensor(t, t, val, ALU.mult))
                ch(v.tensor_scalar(t, t, -0.5, 1.5, ALU.mult, ALU.add))
                ch(v.tensor_tensor(y, y, t, ALU.mult))

            v.wait_ge(s_lk, 16)
            ch.mark(v.tensor_scalar(lo[:, :], lk[:, :], P - 1, None, ALU.bitwise_and))
            ch(v.tensor_scalar(hi[:, :], lk[:, :], 7, None, ALU.arith_shift_right))
            v.wait_ge(s_con, CONST)
            v.tensor_tensor(oh_lo, bcast(iota[0:LP, :].unsqueeze(1), [LP, LC, P]), bcast(lo[:, :].unsqueeze(2), [LP, LC, P]),
                            ALU.is_equal).then_inc(s_oh, 1)
            v.tensor_tensor(oh_hi, bcast(iota[0:LP, 0:NT].unsqueeze(1), [LP, LC, NT]), bcast(hi[:, :].unsqueeze(2), [LP, LC, NT]),
                            ALU.is_equal).then_inc(s_oh, 1)
            ch(v.memset(one_nt, 1.0))
            v.wait_ge(s_hist, 1)
            v.tensor_copy(hist, bank[3][:, 0:NT]).then_inc(s_hists, 1)
            v.wait_ge(s_pref, 1)
            ch(v.tensor_copy(tot, bank[3][:, 128:128 + NT]))
            ch(v.tensor_tensor_scan(incl, one_nt, tot, 0.0, ALU.mult, ALU.add))
            ch(v.tensor_tensor(incl, incl, tot, ALU.subtract))
            ch(v.tensor_tensor(bf, incl, bank[3][:, 64:64 + NT], ALU.add))
            ch(v.tensor_scalar(bf, bf, float(NB - 1), None, ALU.min))
            v.tensor_copy(bidx[:, :], bf).then_inc(s_bidx, 1)

            def stats(n):
                ch.mark(v.bn_stats(bn_x[:, bass.ds(n, 1), :].rearrange("p a f -> p (a f)"), X3[:, bass.ds(n, 1), :].rearrange("p a f -> p (a f)")))

            tiles = (NT - 1) // XCH
            for c in range(XCH):
                v.wait_ge(s_x[c], 16)
                for n in range(c * tiles, (c + 1) * tiles):
                    stats(n)
            v.wait_ge(s_x[XCH], 16)
            stats(NT - 1)
            v.wait_ge(s_dve, ch.n)
            half = [bn_x[:, :, n:n + 1].rearrange("p i a -> p (i a)") for n in range(6)]
            ch.mark(v.tensor_tensor(mean, half[1], half[4], ALU.add))
            ch.mark(v.tensor_tensor(tc, half[1], half[4], ALU.subtract))
            ch(v.tensor_tensor(var, half[2], half[5], ALU.add))
            ch.mark(v.tensor_scalar(mean, mean, 0.5, None, ALU.mult))
            ch.mark(v.tensor_scalar(var, var, 1.0 / D, None, ALU.mult))
            ch(v.tensor_tensor(tc, tc, tc, ALU.mult))
            ch(v.scalar_tensor_tensor(out=var, in0=tc, scalar=0.25, in1=var, op0=ALU.mult, op1=ALU.add))
            v.tensor_scalar(ta, var, LN_EPS, None, ALU.add).then_inc(s_q1, 1)
            v.wait_ge(s_q2, 1)
            ch(v.reciprocal(rstd, tb_))
            inv_root(rstd, ta, tc)
            ch(v.scalar_tensor_tensor(out=nmr, in0=mean, scalar=-1.0, in1=rstd, op0=ALU.mult, op1=ALU.mult))
            ch(v.tensor_tensor(tc, rstd, rstd, ALU.mult))
            ch(v.tensor_scalar(opr, rstd, 1.0, None, ALU.add))
            v.scalar_tensor_tensor(out=ta, in0=var, scalar=float(D), in1=tc, op0=ALU.mult, op1=ALU.mult).then_inc(s_q1, 1)

            def norm(n, h):
                v.wait_ge(s_tr, free(n))
                v.tensor_scalar(xs[:, h, :], X3[:, bass.ds(n, 1), :].rearrange("p a f -> p (a f)"), rstd[:, bass.ds(n, 1)], nmr[:, bass.ds(n, 1)],
                                ALU.mult, ALU.add).then_inc(s_xs, 1)

            with v.Fori(0, PAIRS) as i:
                for h in range(2):
                    norm(i * 2 + h, h)
            norm(NT - 1, 0)
            v.wait_ge(s_q2, 2)
            ch(v.tensor_scalar(tb_, tb_, 1e-12, None, ALU.max))
            ch(v.reciprocal(rn, tb_))
            ch(v.tensor_scalar(rn, rn, float(D) ** 0.5, None, ALU.mult))

            v.wait_ge(s_runs, 16 * 7)
            ch(v.tensor_tensor(con, dst_all[:, 1:T + 1], dst_all[:, 0:T], ALU.is_equal))
            ch(v.tensor_copy(col[:, 0:1], con[:, 0:1]))
            ch(v.memset(con[:, 0:1], 0.0))
            ch(v.tensor_scalar(neg, con, 1.0, BIG, ALU.subtract, ALU.mult))
            ch(v.tensor_tensor(col[:, 1:2], dst_all[:, 1:2], dst_all[:, T:T + 1], ALU.is_equal))
            ch(v.tensor_tensor(col[:, 1:2], col[:, 1:2], col[:, 0:1], ALU.mult))
            v.tensor_scalar(diag[:, :], ident[:, :], col[:, 1:2], None, ALU.mult).then_inc(s_dgw, 1)
            v.tensor_scalar(nidx[:, :], dst_all[:, 1:2], 1.0, None, ALU.add).then_inc(s_nix, 1)

            v.wait_ge(s_blk, 16 * NT)
            ch(v.tensor_tensor(below, blk, bcast(node[:, :].unsqueeze(2), [P, NT, LB]), ALU.is_le))
            ch(v.tensor_reduce(cnt, below, AX.X, ALU.add))
            v.scalar_tensor_tensor(out=ends, in0=bf, scalar=float(LB), in1=cnt, op0=ALU.mult, op1=ALU.add).then_inc(s_e, 1)
            v.wait_ge(s_eT, 1)
            v.tensor_copy(endsT[:, :], bank[3][0:NT, 0:P]).then_inc(s_eTs, 1)
            v.wait_ge(s_sT, 1)
            ch(v.tensor_copy(starts, bank[3][:, 128:128 + NT]))
            ch(v.tensor_tensor(edges, ends, starts, ALU.subtract))
            ch(v.tensor_scalar(deg, edges, 1.0, None, ALU.add))
            v.tensor_copy(ta, deg).then_inc(s_q1, 1)
            v.wait_ge(s_q2, 3)
            ch(v.reciprocal(dinv, tb_))
            inv_root(dinv, deg, tc)
            v.wait_ge(s_tb, done(NT - 1))
            ch(v.tensor_copy(TB3[:, :, BF:BF + 1].rearrange("p i a -> p (i a)"), dinv))
            v.sem_inc(s_dv, 1)
            ch(v.tensor_scalar(has, edges, 1.0, None, ALU.min))
            ch(v.tensor_scalar(nohas, has, 1.0, BIG, ALU.subtract, ALU.mult))
            ch(v.tensor_scalar(posf, ends, 1.0, 0.0, ALU.subtract, ALU.max))
            ch(v.tensor_copy(pos[:, :], posf))
            v.wait_ge(s_w, 16 * 20)
            for k in range(KD):
                v.tensor_scalar(wc[:, k, CW:CW + 3 * HID], wc[:, k, CW:CW + 3 * HID], gpre[:, k:k + 1], None, ALU.mult).then_inc(s_mask, 1)
            v.wait_ge(s_bnT, 1)
            for l in range(2):
                ch(v.tensor_copy(bnT[:, l, :], bank[4][:, l * P:l * P + 5 * EX * KD]))
            bp = [bnT[:, :, n * EX * KD:(n + 1) * EX * KD] for n in range(5)]
            ch(v.tensor_scalar(bp[4], bp[4], BN_EPS, None, ALU.add))
            v.tensor_copy(bns[:, :, :], bp[4]).then_inc(s_bnv, 1)
            v.wait_ge(s_bnq, 1)
            ch(v.reciprocal(bns[:, :, :], bnt[:, :, :]))
            inv_root(bns[:, :, :], bp[4], bnt[:, :, :])
            ch(v.tensor_tensor(bns[:, :, :], bns[:, :, :], bp[1], ALU.mult))
            ch(v.tensor_tensor(bnb[:, :, :], bp[0], bp[3], ALU.subtract))
            ch(v.tensor_tensor(bnb[:, :, :], bnb[:, :, :], bns[:, :, :], ALU.mult))
            ch(v.tensor_tensor(bnb[:, :, :], bnb[:, :, :], bp[2], ALU.add))
            v.wait_ge(s_Bw, 1)
            ch(v.tensor_copy(runw[:, :], bank[0][:, 0:P]))
            ch(v.tensor_scalar(runn[:, :], runw[:, :], 1.0, BIG, ALU.subtract, ALU.mult))
            ch(v.memset(carT[:, :, 0:1], 0.0))
            ch(v.memset(fix[:, :], 0.0))
            v.wait_ge(s_en, 16)
            ch(v.tensor_scalar(col[:, 4:5], node[:, 0:1], float(T), float(T), ALU.mult, ALU.add))
            ch(v.tensor_tensor(col[:, 4:5], col[:, 3:4], col[:, 4:5], ALU.is_le))
            ch(v.tensor_tensor(col[:, 4:5], col[:, 4:5], col[:, 0:1], ALU.mult))
            ch(v.scalar_tensor_tensor(out=col[:, 5:6], in0=col[:, 3:4], scalar=-1.0, in1=col[:, 4:5], op0=ALU.add, op1=ALU.mult))
            ch(v.tensor_scalar(col[:, 6:7], col[:, 4:5], -FAR, FAR, ALU.mult, ALU.add))
            ch(v.tensor_tensor(col[:, 5:6], col[:, 5:6], col[:, 6:7], ALU.add))
            v.tensor_copy(fidx[:, :], col[:, 5:6]).then_inc(s_fz, 1)
            ch(v.memset(M[:, :], -BIG))
            ch(v.memset(blockm[:, :], 0.0))
            for h in range(AH):
                ch(v.memset(blockm[h * AD:(h + 1) * AD, h * AD:(h + 1) * AD], float(AD) ** -0.5))
            ch(v.memset(vs[:, :, HID:HID + 1], 1.0))
            ch(v.memset(mT[:, 2 * P:2 * P + 1], 1.0))

            v.memset(stm[:, U - 1, :], 0.0).then_inc(s_max, U)
            v.memset(sts[:, U - 1, :], 0.0).then_inc(s_sum, U)

            def window(w, hook):
                for u in range(U):
                    pv = (u - 1) % U
                    if u % HW == 0:
                        v.wait_ge(s_out[u // HW], w * 32 + 32)
                    v.wait_ge(s_prod, w * U + u + 1)
                    v.wait_ge(s_max, w * U + U + u)
                    v.scalar_tensor_tensor(out=stm[:, u, :], in0=stm[:, pv, :], scalar=neg[:, bass.ds(w * U + u, 1)],
                                           in1=ring[:, u, 0:BF], op0=ALU.add, op1=ALU.max).then_inc(s_max, 1)
                    v.wait_ge(s_sum, w * U + U + u)
                    v.scalar_tensor_tensor(out=sts[:, u, :].rearrange("p (a b) -> p a b", a=2),
                                           in0=sts[:, pv, :].rearrange("p (a b) -> p a b", a=2),
                                           scalar=con[:, bass.ds(w * U + u, 1)],
                                           in1=ring[:, u, :].rearrange("p (a b) -> p a b", a=2)[:, :, 0:BF],
                                           op0=ALU.mult, op1=ALU.add).then_inc(s_sum, 1)
                    if hook:
                        hook(u)

            def pass_b(n, h, s, last=False):
                R = LAST if last else P
                if s == 2:
                    v.wait_ge(s_pu, done(n))
                    ch(v.scalar_tensor_tensor(out=M[0:R, :], in0=bank[1 + h][0:R, CW:CW + HID], scalar=rn[0:R, bass.ds(n, 1)],
                                              in1=M[0:R, :], op0=ALU.mult, op1=ALU.max))
                if s == 4:
                    v.tensor_tensor(CB3[:, bass.ds(n, 1), :].rearrange("p a f -> p (a f)"), bank[1 + h][:, 0:CW], b_comb[:, :],
                                    ALU.add).then_inc(s_kb, 2 if last else 1)

            v.wait_ge(s_wide, 16 * 8)
            with v.Fori(0, PAIRS) as i:
                ch.enter(i, 2)
                window(i, lambda u: pass_b(i * 2 + u // HW, u // HW, u % HW))
                ch.leave(PAIRS)
            window(PAIRS, lambda u: pass_b(NT - 1, 0, u, True) if u < HW else None)
            v.sem_inc(s_Mw, 1)
            v.wait_ge(s_MT, 1)
            ch(v.tensor_reduce(col[:, 9:10], bank[7][:, 384:512], AX.X, ALU.max))
            ch(v.tensor_reduce(col[:, 10:11], mk[:, 0, :], AX.X, ALU.max))
            ch(v.tensor_tensor(col[:, 9:10], col[:, 9:10], col[:, 10:11], ALU.max))
            v.tensor_scalar(col[:, 8:9], col[:, 9:10], -1.0, None, ALU.mult).then_inc(s_em, 1)
            v.tensor_scalar(diag[:, :], ident[:, :], col[:, 9:10], None, ALU.mult).then_inc(s_dg, 1)
            v.wait_ge(s_Mb, 1)
            ch(v.tensor_copy(Mb[:, :], bank[7][:, 256:384]))
            v.sem_inc(s_mem, 1)
            v.wait_ge(s_kb, done(NT))
            sym = CB3.rearrange("p i (h k) -> p i h k", h=HEADS)
            for h in range(HEADS):
                ch(v.tensor_tensor(sym[:, :, h, 0:BASES], sym[:, :, h, 0:BASES], bcast(dinv.unsqueeze(2), [P, NT, BASES]), ALU.mult))

            def pass_c(n, h, s, last=False):
                R = LAST if last else P
                if s == 0:
                    v.wait_ge(s_pu, done(n + UNITS))
                    v.wait_ge(s_ek, free(n))
                    v.scalar_tensor_tensor(out=kt[0:R, h, :], in0=bank[1 + h][0:R, 0:HID], scalar=rn[0:R, bass.ds(n, 1)], in1=Mb[0:R, :],
                                           op0=ALU.mult, op1=ALU.subtract).then_inc(s_kt, 2 if last else 1)

            with v.Fori(0, PAIRS) as i:
                window(i + PASS, lambda u: pass_c(i * 2 + u // HW, u // HW, u % HW))
            window(PASS + PAIRS, lambda u: pass_c(NT - 1, 0, u, True) if u < HW else None)
            v.wait_ge(s_cx, done(NT))
            ch(v.reciprocal(col[:, 11:12], bank[3][:, HID:HID + 1]))
            v.scalar_tensor_tensor(out=diag[:, :], in0=bank[3][:, 0:HID], scalar=col[:, 11:12], in1=blockm[:, :],
                                   op0=ALU.mult, op1=ALU.mult).then_inc(s_cbd, 1)

            v.sem_inc(s_mo, 1)
            ch(v.tensor_scalar(g_out, g_out, float(D) ** 0.5, None, ALU.mult))

            def pass_d(i, u, m=2):
                b3 = [P, AH, AD]
                if u < m:
                    q3 = bank[1 + u][:, 0:HID].rearrange("p (h d) -> p h d", h=AH)
                    if u == 0:
                        v.wait_ge(s_pu, i * 2 + (2 * UNITS + 2 + RING2))
                    ch(v.tensor_reduce(small[:, u, 0:AH], q3, AX.X, ALU.max))
                    t = v.tensor_tensor(qd[:, u, :].rearrange("p (h d) -> p h d", h=AH), q3, bcast(small[:, u, 0:AH].unsqueeze(2), b3),
                                        ALU.subtract)
                    if u == m - 1:
                        t.then_inc(s_qd, 1)
                if u == 4:
                    e3 = eq[:, 0:m, :].rearrange("p b (h d) -> p (b h) d", h=AH)
                    v.wait_ge(s_eq, i + 1)
                    ch(v.tensor_reduce(esum[:, 0:m * AH], e3, AX.X, ALU.add))
                    ch(v.reciprocal(esum[:, 2 * AH:(2 + m) * AH], esum[:, 0:m * AH]))
                    v.tensor_tensor(qn[:, 0:m, :].rearrange("p b (h d) -> p (b h) d", h=AH), e3,
                                    bcast(esum[:, 2 * AH:(2 + m) * AH].unsqueeze(2), [P, m * AH, AD]), ALU.mult).then_inc(s_qn, 1)
                if u == 12:
                    v.wait_ge(s_nr, i + 1)
                    ch(v.tensor_scalar(nrm[:, 4:4 + m], nrm[:, 2:2 + m], 1e-12, None, ALU.max))
                    ch(v.reciprocal(nrm[:, 6:6 + m], nrm[:, 4:4 + m]))
                if 13 <= u < 13 + m:
                    h = u - 13
                    x1 = X3[:, bass.ds(i * 2 + h, 1), :].rearrange("p a f -> p (a f)")
                    ch(v.scalar_tensor_tensor(out=mo[:, h, :], in0=bank[5 + h][:, 0:D], scalar=nrm[:, 6 + h:7 + h], in1=g_out,
                                              op0=ALU.mult, op1=ALU.mult))
                    t = v.tensor_tensor(x1, x1, mo[:, h, :], ALU.add)
                    if h == m - 1:
                        t.then_inc(s_mo, 1)

            with v.Fori(0, PAIRS) as i:
                ch.enter(i, 8)
                window(i + 2 * PASS, lambda u: pass_d(i, u))
                ch.leave(PAIRS)
            window(2 * PASS + PAIRS, lambda u: pass_d(PAIRS, u, 1))
            with v.Fori(3 * PASS, WIN) as w:
                window(w, None)

            v.wait_ge(s_tl, 1)
            for n in range(AGGS):
                v.tensor_tensor_scan(carT[:, n, 1:P + 1], (runn if n == 0 else runw)[:, :], bank[4][:, n * P:(n + 1) * P], 0.0,
                                     ALU.add if n == 0 else ALU.mult, ALU.max if n == 0 else ALU.add).then_inc(s_car, 1)
            v.wait_ge(s_carT, 1)
            v.wait_ge(s_fixg, 32)
            for n in range(AGGS):
                v.tensor_tensor(fix[:, n * BF:(n + 1) * BF], fix[:, n * BF:(n + 1) * BF], bank[5][:, n * P:(n + 1) * P],
                                ALU.max if n == 0 else ALU.add).then_inc(s_fix, 1)

            def combine(n, j, b, i7):
                g = got[:, j, :]
                own = TB3[:, bass.ds(n, 1), 0:BF].rearrange("p a f -> p (a f)")
                v.wait_ge(s_gf[j], i7 * 32 + 32)
                v.scalar_tensor_tensor(out=g[:, 0:BF], in0=g[:, 0:BF], scalar=nohas[:, bass.ds(n, 1)], in1=own,
                                       op0=ALU.add, op1=ALU.max).then_inc(s_dve, 1)
                v.scalar_tensor_tensor(out=g[:, BF:2 * BF], in0=g[:, BF:2 * BF], scalar=has[:, bass.ds(n, 1)], in1=own,
                                       op0=ALU.mult, op1=ALU.add).then_inc(s_dve, 1)
                v.tensor_scalar(g[:, 2 * BF:3 * BF], g[:, 2 * BF:3 * BF], has[:, bass.ds(n, 1)], None, ALU.mult).then_inc(s_dve, 1)
                ch.n += 3
                v.wait_ge(s_dve, ch.base + ch.n)
                ch(v.scalar_tensor_tensor(out=g[:, 2 * BF:3 * BF], in0=own, scalar=dinv[:, bass.ds(n, 1)], in1=g[:, 2 * BF:3 * BF],
                                          op0=ALU.mult, op1=ALU.add))
                v.wait_ge(s_ph, free(n))
                c = CB3[:, bass.ds(n, 1), :].rearrange("p a (h k) -> p k (a h)", h=HEADS)
                for k0, at in ((0, 2), (BASES, 1), (2 * BASES, 0)):
                    m = v.tensor_tensor(prod[:, b, k0:k0 + BASES, :].rearrange("p k (h f) -> p k h f", h=HEADS),
                                        bcast(c[:, k0:k0 + BASES, :].unsqueeze(3), [P, BASES, HEADS, F]),
                                        bcast(g[:, at * BF:(at + 1) * BF].rearrange("p (k f) -> p k f", k=BASES).unsqueeze(2), [P, BASES, HEADS, F]),
                                        ALU.mult)
                m.then_inc(s_pr, 1)

            full = NT // (2 * GR)
            with v.Fori(0, full) as i:
                ch.enter(i, 4 * 2 * GR)
                for j in range(2 * GR):
                    combine(i * (2 * GR) + j, j % GR, j % 2, i * 2 + j // GR)
                ch.leave(full)
            for n in range(full * 2 * GR, NT):
                combine(n, n % GR, n % 2, n // GR)

            v.wait_ge(s_sm, 1)
            ch(v.scalar_tensor_tensor(out=gnc[:, :], in0=bank[3][:, 0:D], scalar=1.0 / N, in1=conv_b, op0=ALU.mult, op1=ALU.add))
            ch(v.tensor_tensor(gnc[:, :], gnc[:, :], gn_s, ALU.mult))
            ch(v.tensor_tensor(gnc[:, :], conv_b, gnc[:, :], ALU.subtract))

            def center(n):
                h = H3[:, bass.ds(n, 1), :].rearrange("p a f -> p (a f)")
                v.tensor_tensor(h, h, gnc[:, :], ALU.add).then_inc(s_hc, 1)

            with v.Fori(0, PAIRS) as i:
                for b in range(2):
                    center(i * 2 + b)
            center(NT - 1)
            v.wait_ge(s_vr, done(NT - 1))
            v.wait_ge(s_hc, NT)
            v.tensor_scalar(gnc[:, :], bank[4][:, 0:D], 1.0 / N, GN_EPS, ALU.mult, ALU.add).then_inc(s_gq, 1)
            v.wait_ge(s_gr, 1)
            ch(v.reciprocal(gnA[:, :], gnt[:, :]))
            inv_root(gnA[:, :], gnc[:, :], gnt[:, :])
            ch(v.tensor_tensor(gnA[:, :], gnA[:, :], gn_w, ALU.mult))

            FRONT1, FRONT2 = 5, 6

            def front1(n, b):
                h = H3[:, bass.ds(n, 1), :].rearrange("p a f -> p (a f)")
                x1 = X3[:, bass.ds(n, 1), :].rearrange("p a f -> p (a f)")
                ch(v.tensor_tensor(h, h, gnA[:, :], ALU.mult))
                ch(v.tensor_tensor(h, h, gn_b, ALU.add))
                ch(v.scalar_tensor_tensor(out=x1, in0=h, scalar=0.0, in1=x1, op0=ALU.max, op1=ALU.add))
                v.sem_inc(s_step, 1)
                ch(v.bn_stats(bn6[:, b, :], x1))
                v.sem_inc(s_step, 1)
                ch(v.bn_aggr(mv[:, b, :], bn6[:, b, :]))
                v.tensor_scalar(cf[:, b, 1:2], mv[:, b, 1:2], LN_EPS, None, ALU.add).then_inc(s_f1, 1)

            def front2(n, b):
                v.wait_ge(s_f2, done(n))
                ch(v.reciprocal(cf[:, b, 3:4], cf[:, b, 2:3]))
                inv_root(cf[:, b, 3:4], cf[:, b, 1:2], cf[:, b, 4:5])
                ch(v.scalar_tensor_tensor(out=cf[:, b, 5:6], in0=mv[:, b, 0:1], scalar=-1.0, in1=cf[:, b, 3:4], op0=ALU.mult, op1=ALU.mult))
                v.wait_ge(s_f4, free(n))
                v.tensor_scalar(xf[:, b, :], X3[:, bass.ds(n, 1), :].rearrange("p a f -> p (a f)"), cf[:, b, 3:4], cf[:, b, 5:6],
                                ALU.mult, ALU.add).then_inc(s_f3, 1)

            def softmax(g, gb, ng):
                b3 = [P, ng, EX]
                v.wait_ge(s_lg, g + 1)
                ch(v.tensor_tensor(lg[:, 0:ng, :], bank[7][:, 0:ng * EX].rearrange("p (s e) -> p s e", s=ng),
                                   bcast(b_r[:, :].unsqueeze(1), b3), ALU.add))
                ch(v.tensor_reduce(rsm[:, 0, 0:ng], lg[:, 0:ng, :], AX.X, ALU.max))
                v.tensor_tensor(lg[:, 0:ng, :], lg[:, 0:ng, :], bcast(rsm[:, 0, 0:ng].unsqueeze(2), b3), ALU.subtract).then_inc(s_lm, 1)
                v.wait_ge(s_le, g + 1)
                ch(v.tensor_reduce(rsm[:, 1, 0:ng], lg[:, 0:ng, :], AX.X, ALU.add))
                ch(v.reciprocal(rsm[:, 0, 0:ng], rsm[:, 1, 0:ng]))
                v.tensor_tensor(wsm[:, gb, 0:ng, :], lg[:, 0:ng, :], bcast(rsm[:, 0, 0:ng].unsqueeze(2), b3), ALU.mult).then_inc(s_ws, 1)

            def add_round(g, gb, e, ng):
                for s in range(ng):
                    r = g * (ROUNDS * GT) + e * GT + s
                    inc = 1 if ng == GT else GT
                    ps = bank[4 + s // 2][:, s % 2 * D:(s % 2 + 1) * D]
                    v.wait_ge(s_L3, r + inc + L3_START + (1 if ng == GT and s % 2 == 0 else 0))
                    out = acc[:, gb, s, :]
                    v.wait_ge(s_acc, r + 1)
                    if e == 0:
                        x1 = X3[:, bass.ds(g * GT + s, 1), :].rearrange("p a f -> p (a f)")
                        v.scalar_tensor_tensor(out=out, in0=ps, scalar=wsm[:, gb, s, 0:1], in1=x1, op0=ALU.mult, op1=ALU.add).then_inc(s_acc, inc)
                    elif e < EX:
                        v.scalar_tensor_tensor(out=out, in0=ps, scalar=wsm[:, gb, s, e:e + 1], in1=out, op0=ALU.mult, op1=ALU.add).then_inc(s_acc, inc)
                    else:
                        v.tensor_tensor(out, out, ps, ALU.add).then_inc(s_acc, inc)

            def group(g, gb, w, nxt, n_next, prev_stores):
                ng = w // P
                softmax(g, gb, ng)
                for e in range(ROUNDS):
                    if e < n_next:
                        front1(nxt * GT + e, e % 2)
                    if e == 0:
                        v.wait_ge(s_ws, g + 1)
                        v.wait_ge(s_y[gb], prev_stores + 16)
                    if 1 <= e < 1 + n_next:
                        front2(nxt * GT + e - 1, (e - 1) % 2)
                    add_round(g, gb, e, ng)

            for s in range(GT):
                front1(s, s % 2)
                front2(s, s % 2)
            with v.Fori(0, GROUPS // 2 - 1) as i:
                ch.enter(i, 2 * (4 + GT * (FRONT1 + FRONT2)))
                group(i * 2, 0, GN, i * 2 + 1, GT, i * 16)
                group(i * 2 + 1, 1, GN, i * 2 + 2, GT, i * 16)
                ch.leave(GROUPS // 2 - 1)
            group(GROUPS - 2, 0, GN, GROUPS - 1, GT, 16 * (GROUPS // 2 - 1))
            group(GROUPS - 1, 1, GN, GROUPS, 1, 16 * (GROUPS // 2 - 1))
            group(GROUPS, 0, P, None, 0, 16 * (GROUPS // 2))


_INS = ["x", "src", "dst", "L0_gnn_W_bases", "L0_gnn_W_comb", "L0_gnn_b_comb", "L0_gnn_conv_bias", "L0_gnn_gn_weight",
        "L0_gnn_gn_bias", "L0_gnn_gn_mean_scale", "L0_mix_w_qkv", "L0_mix_mem_kv", "L0_mix_w_out", "L0_mix_b_out",
        "L0_mix_g_out", "L0_mix_g_pre", "L0_ffn_Wr", "L0_ffn_br"] + [
        f"L0_ffn_{n}{l}" for l in (1, 2) for n in ("W", "b", "g", "be", "m", "v")] + ["L0_ffn_Wo", "L0_ffn_bo"]


def kernel(**inputs):
    import numpy as _np
    import concourse.bacc as _bacc
    from concourse import mybir as _mybir
    from concourse.bass_utils import run_bass_kernel_spmd as _run

    nc = _bacc.Bacc("TRN2", target_bir_lowering=False, num_devices=1)
    arrays, aps = {}, {}
    for name in _INS:
        arr = _np.ascontiguousarray(inputs[name])
        arrays[f"in_{name}"] = arr
        aps[name] = nc.dram_tensor(f"in_{name}", arr.shape, _mybir.dt.from_np(arr.dtype), kind="ExternalInput").ap()
    out = nc.dram_tensor("out_y", (N, D), F32, kind="ExternalOutput").ap()
    scratch = {
        "tbl": nc.dram_tensor("scratch_table", (NT * P, RW), F32, kind="Internal").ap(),
        "xtd": nc.dram_tensor("scratch_xt", (NT * P, D), F32, kind="Internal").ap(),
        "maxes": nc.dram_tensor("scratch_maxes", (P * T, BF), F32, kind="Internal").ap(),
        "sums": nc.dram_tensor("scratch_sums", (P * T, 2 * BF), F32, kind="Internal").ap(),
        "ends": nc.dram_tensor("scratch_ends", (NT * P + 1, 1), F32, kind="Internal").ap(),
    }
    program(nc, aps, out, scratch)
    r = _run(nc, [arrays], core_ids=[0])
    return r.results[0]["out_y"]
```

```python
from contextlib import ExitStack

import concourse.bass as bass
from concourse import mybir

F32 = mybir.dt.float32
I32 = mybir.dt.int32
F32R = mybir.dt.float32r
ALU = mybir.AluOpType
ACT = mybir.ActivationFunctionType
AX = mybir.AxisListType

N = 6250
E = 200000
D = 256
P = 128
KD = D // P
NT = -(-N // P)
LAST = N - (NT - 1) * P
HEADS, BASES, AGGS = 8, 4, 3
F = D // HEADS
BF = BASES * F
KC = BASES * AGGS
CW = HEADS * KC
AH, AD, MEM = 4, 32, 4
HID = AH * AD
EX = 8
LN_EPS, GN_EPS, BN_EPS = 1e-5, 1e-5, 1e-3
BIG = 3.0e38
FAR = 1.0e9

U = 16
HW = U // 2
WIN = -(-E // (P * U))
T = WIN * U
RW = BF + 4
ST = AGGS * BF
FULL = E // T
REST = E - FULL * T

LB = 125
NB = E // LB
LP = 100
LC = NB // LP

PAIRS = NT // 2
PASS = PAIRS + 1
PLAIN = WIN - 3 * PASS
UNITS = 2 * PASS

SQ = 4

GT = 2
GN = GT * P
GROUPS = NT // GT
ROUNDS = EX + 1

L_START = 4
L3_START = 3 * GT

RING2 = 2


def done(n):
    return n + 1 + RING2


def free(n):
    return n + 1


class Chain:

    def __init__(self, eng, sem):
        self.eng, self.sem, self.base, self.n = eng, sem, 0, 0

    def __call__(self, ins):
        ins.then_inc(self.sem, 1)
        self.n += 1
        self.eng.wait_ge(self.sem, self.base + self.n)

    def mark(self, ins):
        ins.then_inc(self.sem, 1)
        self.n += 1

    def enter(self, i, per):
        self.start, self.per = self.base + self.n, per
        self.base, self.n = self.start + i * per, 0

    def leave(self, times):
        assert self.n == self.per, (self.n, self.per)
        self.base, self.n = self.start + times * self.per, 0


def as_f32(ap):
    return ap.bitcast(F32)


def bcast(ap, shape):
    return ap.broadcast_to(shape)


def program(nc, a, y, scratch):
    ctx = ExitStack()
    with ctx:
        def sb(name, shape, dt=F32):
            return ctx.enter_context(nc.sbuf_tensor(name, shape, dt))

        def sem(name):
            return ctx.enter_context(nc.semaphore(name))

        X = sb("X", [P, NT * D])
        X3 = X[:, :].rearrange("p (i d) -> p i d", d=D)
        sizes = {"R1": NT * D, "TB": NT * RW, "CB": NT * CW, "AUX": 3 * EX * KD * D}
        with ExitStack() as first_use:
            R1, TB, CB, AUX = [first_use.enter_context(nc.sbuf_tensor(n, [P, w], F32)) for n, w in sizes.items()]
        R1H, TBH, CBH, AUXH = [ctx.enter_context(nc.sbuf_tensor(n + "_rounded", [P, w], F32R)) for n, w in sizes.items()]
        H3 = R1[:, :].rearrange("p (i d) -> p i d", d=D)
        blk = R1[:, 0:NT * LB].bitcast(I32).rearrange("p (i j) -> p i j", j=LB)
        OH = -(-NT * LB // 64) * 64
        below = R1[:, OH:OH + NT * LB].rearrange("p (i j) -> p i j", j=LB)
        oh_lo = R1[0:LP, OH:OH + LC * P].rearrange("p (c m) -> p c m", m=P)
        oh_hi = R1[0:LP, OH + LC * P:OH + LC * (P + NT)].rearrange("p (c m) -> p c m", m=NT)
        o = OH + NT * LB
        upto = R1[:, o:o + P]
        iota = R1[:, o + P:o + 2 * P].bitcast(I32)
        assert o + 2 * P <= NT * D
        GS = 2 * RW
        ring = R1[:, 0:U * GS].rearrange("p (u f) -> p u f", f=GS)
        stm = R1[:, U * GS:U * (GS + BF)].rearrange("p (u f) -> p u f", f=BF)
        sts = R1[:, U * (GS + BF):U * (GS + ST)].rearrange("p (u f) -> p u f", f=2 * BF)
        TB3 = TB[:, :].rearrange("p (i f) -> p i f", f=RW)
        bn_x = CB[:, 0:NT * 6].rearrange("p (i f) -> p i f", f=6)
        CB3 = CB[:, :].rearrange("p (i f) -> p i f", f=CW)
        idx_all = AUX[:, 0:T + U].bitcast(I32)
        dst_all = AUX[:, T + U:T + U + T + 2].bitcast(I32)
        o = 2 * T + U + 2
        con = AUX[:, o:o + T]
        neg = AUX[:, o + T:o + 2 * T]
        o += 2 * T
        xs = AUX[:, o:o + 2 * D].rearrange("p (b f) -> p b f", b=2)
        xt = AUX[:, o + 512:o + 1024].rearrange("p (b k n) -> p b k n", b=2, k=KD)
        xl = AUX[:, o + 1024:o + 1536].rearrange("p (b k n) -> p b k n", b=2, k=KD)
        kt = AUX[:, o + 1536:o + 1792].rearrange("p (b n) -> p b n", b=2)
        ek = AUX[:, o + 1792:o + 2048].rearrange("p (b n) -> p b n", b=2)
        vs = AUX[:, o + 2048:o + 2048 + 2 * (HID + 1)].rearrange("p (b n) -> p b n", b=2)
        o += 2048 + 2 * (HID + 1) + 2
        qd = AUX[:, o:o + 256].rearrange("p (b n) -> p b n", b=2)
        eq = AUX[:, o + 256:o + 512].rearrange("p (b n) -> p b n", b=2)
        qn = AUX[:, o + 512:o + 768].rearrange("p (b n) -> p b n", b=2)
        qT = AUX[:, o + 768:o + 1024].rearrange("p (b n) -> p b n", b=2)
        mo = AUX[:, o + 1024:o + 1536].rearrange("p (b n) -> p b n", b=2)
        carT = AUX[:, o + 1536:o + 1536 + 3 * (P + 1)].rearrange("p (a n) -> p a n", a=3)
        o += 1536 + 3 * (P + 1) + 1
        wb = AUX[:, o:o + KD * BF].rearrange("p (k n) -> p k n", k=KD)
        o += KD * BF
        wc = AUX[:, o:o + KD * (CW + 3 * HID)].rearrange("p (k n) -> p k n", k=KD)
        o += KD * (CW + 3 * HID)
        wo = AUX[:, o:o + D]
        o += D
        endsT = AUX[0:NT, o:o + P]
        startsT = AUX[0:NT, o + P:o + 2 * P]
        o += 2 * P
        assert o <= 3 * EX * KD * D
        o = U * (GS + ST)
        M, Mb, blockm, runw, runn = [R1[:, o + n * P:o + (n + 1) * P] for n in range(5)]
        m2, b_out, g_out = [R1[:, o + 5 * P + n * D:o + 5 * P + (n + 1) * D] for n in range(3)]
        fix = R1[:, o + 5 * P + 3 * D:o + 5 * P + 3 * D + ST]
        assert o + 5 * P + 3 * D + ST <= NT * D
        PRE = 2
        GR = 7
        got = AUX[:, 0:GR * ST].rearrange("p (u f) -> p u f", f=ST)
        prod = AUX[:, GR * ST:GR * ST + 2 * KC * D].rearrange("p (b k n) -> p b k n", b=2, k=KC)
        assert GR * ST + 2 * KC * D <= 3 * EX * KD * D
        EWN = EX * KD * D
        EW = [AUX[:, n * EWN:(n + 1) * EWN] for n in range(3)]
        EWH, EWL = [[t[:, n * EWN:(n + 1) * EWN] for n in range(3)] for t in (R1H, AUXH)]
        EWP = [[t.rearrange("p (e k n) -> p e k n", e=EX, k=KD) for t in (EWH[n], EWL[n])] for n in range(3)]
        HB = 2 * 2 * KD * GN
        hid = [TBH[:, l * HB:(l + 1) * HB].rearrange("p (b q f) -> p b q f", b=2, q=2) for l in range(2)]
        hf = TB[:, 2 * HB:2 * HB + 2 * KD * GN].rearrange("p (l f) -> p l f", l=2)
        o = 2 * HB + 2 * KD * GN
        acc = TB[:, o:o + 2 * GT * D].rearrange("p (b s n) -> p b s n", b=2, s=GT)
        assert o + 2 * GT * D <= NT * RW
        xg = CBH[:, 0:HB].rearrange("p (b q f) -> p b q f", b=2, q=2)
        sq = CB[:, HB:HB + SQ * D].rearrange("p (b n) -> p b n", b=SQ)
        xf = CB[:, HB + 2 * D:HB + 4 * D].rearrange("p (b n) -> p b n", b=2)
        o = HB + 4 * D
        gnA, gnc, gnt = [CB[:, o + n * D:o + (n + 1) * D] for n in range(3)]
        wT = CB[0:EX, o + 3 * D:o + 3 * D + GN]
        assert o + 3 * D + GN <= NT * CW

        ident = sb("ident", [P, P])
        ones = sb("ones", [P, P])
        ones_last = sb("ones_last", [P, P])
        node = sb("node", [P, NT], I32)
        lk = sb("lk", [LP, LC], I32)
        lo = sb("lo", [LP, LC], I32)
        hi = sb("hi", [LP, LC], I32)
        tabs = sb("tabs", [P, 24, NT])
        (hist, tot, incl, bf, cnt, ends, starts, edges, deg, dinv, has, nohas, mean, var, rstd,
         nmr, rn, opr, ta, tb_, tc, posf, one_nt, spare) = [tabs[:, n, :] for n in range(24)]
        bidx = sb("bidx", [P, NT], I32)
        pos = sb("pos", [P, NT], I32)
        bn6 = sb("bn6", [P, 2, 6])
        mv = sb("mv", [P, 2, 2])
        nrm = sb("nrm", [P, 8])
        esum = sb("esum", [P, 4 * AH])
        iw = sb("iw", [P, U], I32)
        wr = sb("wr", [P, KD, EX])
        bo = sb("bo", [EX, D])
        gpre = sb("gpre", [P, KD])
        rows = sb("rows", [P, 4, D])
        conv_b, gn_w, gn_b, gn_s = [rows[:, n, :] for n in range(4)]
        b_comb = sb("b_comb", [P, CW])
        b_r = sb("b_r", [P, EX])
        bnp = sb("bnp", [5 * EX * KD, 2, P])
        bnT = sb("bnT", [P, 2, 5 * EX * KD])
        bns = sb("bns", [P, 2, EX * KD])
        bnb = sb("bnb", [P, 2, EX * KD])
        bnt = sb("bnt", [P, 2, EX * KD])
        diag = sb("diag", [P, P])
        mk = sb("mk", [P, 2, MEM])
        mkm = sb("mkm", [P, 8])
        mT = sb("mT", [MEM, 2 * P + 1])
        col = sb("col", [P, 24])
        nidx = sb("nidx", [P, 1], I32)
        fidx = sb("fidx", [P, 1], I32)
        small = sb("small", [P, 2, 32])
        lg = sb("lg", [P, GT, EX])
        wsm = sb("wsm", [P, 2, GT, EX])
        rsm = sb("rsm", [P, 2, GT])
        ln = sb("ln", [P, 6, GT])
        cf = sb("cf", [P, 2, 8])

        bank = [ctx.enter_context(nc.psum_tensor(f"bank{n}", [P, 512], F32)) for n in range(8)]

        tbl, xtd, Wd, e_d = scratch["tbl"], scratch["xtd"], (scratch["maxes"], scratch["sums"]), scratch["ends"]
        tbl_p = tbl.rearrange("(i p) f -> p i f", p=P)
        x_in = a["x"]
        W_run = [w.rearrange("(p t) f -> p (t f)", p=P) for w in Wd]
        src1, dst1 = a["src"], a["dst"]
        dst_blocks = dst1.rearrange("(k j) -> k j", j=LB)

        def row_of(v):
            return v.partition_broadcast(P)

        s_pad = sem("s_pad"); s_lk = sem("s_lk")
        XCH = 4
        s_x = [sem(f"s_x{n}") for n in range(XCH + 1)]
        s_runs = sem("s_runs"); s_w = sem("s_w"); s_wide = sem("s_wide")
        s_mask = sem("s_mask"); s_con = sem("s_con"); s_blk = sem("s_blk")
        s_oh = sem("s_oh"); s_hist = sem("s_hist"); s_hists = sem("s_hists"); s_pref = sem("s_pref"); s_bidx = sem("s_bidx")
        s_dve = sem("s_dve"); s_act = sem("s_act")
        s_step = sem("s_step"); s_q1 = sem("s_q1"); s_q2 = sem("s_q2")
        s_xs = sem("s_xs"); s_tr = sem("s_tr"); s_xt = sem("s_xt"); s_bs = sem("s_bs"); s_tb = sem("s_tb")
        s_xst = [sem("s_xst0"), sem("s_xst1")]
        s_e = sem("s_e"); s_eT = sem("s_eT"); s_eTs = sem("s_eTs"); s_ed = sem("s_ed"); s_sld = sem("s_sld")
        s_sT = sem("s_sT"); s_dv = sem("s_dv"); s_tbl = sem("s_tbl")
        s_bnT = sem("s_bnT"); s_bnv = sem("s_bnv"); s_bnq = sem("s_bnq")
        s_g = [sem(f"s_g{u}") for u in range(U)]
        s_iw = sem("s_iw"); s_prod = sem("s_prod"); s_max = sem("s_max"); s_sum = sem("s_sum"); s_seen = sem("s_seen")
        s_out = [sem("s_out0"), sem("s_out1")]
        s_xl = [sem("s_xl0"), sem("s_xl1")]
        s_pu = sem("s_pu"); s_kb = sem("s_kb"); s_kt = sem("s_kt"); s_ek = sem("s_ek"); s_cx = sem("s_cx")
        s_Mw = sem("s_Mw"); s_MT = sem("s_MT"); s_dg = sem("s_dg"); s_Mb = sem("s_Mb"); s_mk = sem("s_mk")
        s_em = sem("s_em"); s_emT = sem("s_emT"); s_emc = sem("s_emc"); s_mem = sem("s_mem")
        s_cbd = sem("s_cbd"); s_cT = sem("s_cT"); s_cTc = sem("s_cTc"); s_m2 = sem("s_m2"); s_m2c = sem("s_m2c")
        s_qd = sem("s_qd"); s_eq = sem("s_eq"); s_qn = sem("s_qn"); s_qT = sem("s_qT"); s_qTc = sem("s_qTc")
        s_mx = sem("s_mx"); s_mo = sem("s_mo"); s_nr = sem("s_nr"); s_xb = sem("s_xb")
        s_nix = sem("s_nix"); s_en = sem("s_en"); s_dgw = sem("s_dgw"); s_Bw = sem("s_Bw")
        s_tl = sem("s_tl"); s_car = sem("s_car"); s_carT = sem("s_carT"); s_fixg = sem("s_fixg"); s_fix = sem("s_fix"); s_fixs = sem("s_fixs"); s_fz = sem("s_fz")
        s_gf = [sem(f"s_gf{j}") for j in range(GR)]
        s_ag = sem("s_ag"); s_pr = sem("s_pr"); s_ph = sem("s_ph"); s_h = sem("s_h"); s_sm = sem("s_sm")
        s_sq = sem("s_sq"); s_hc = sem("s_hc"); s_vr = sem("s_vr"); s_gq = sem("s_gq"); s_gr = sem("s_gr")
        s_ew = [sem(f"s_ew{n}") for n in range(3)]; s_bo = sem("s_bo"); s_wh = sem("s_wh"); s_wl = sem("s_wl"); s_f6 = sem("s_f6"); s_ln = sem("s_ln")
        s_lo = [sem("s_lo1"), sem("s_lo2")]; s_up = [sem("s_up1"), sem("s_up2")]; s_f1 = sem("s_f1"); s_f2 = sem("s_f2"); s_f3 = sem("s_f3"); s_f4 = sem("s_f4"); s_f5 = sem("s_f5")
        s_L1 = sem("s_L1"); s_h1 = sem("s_h1"); s_L2 = sem("s_L2"); s_h2 = sem("s_h2"); s_L3 = sem("s_L3"); s_acc = sem("s_acc")
        s_lg = sem("s_lg"); s_lm = sem("s_lm"); s_le = sem("s_le"); s_ws = sem("s_ws"); s_wT = sem("s_wT"); s_wTc = sem("s_wTc")
        s_y = [sem("s_y0"), sem("s_y1")]

        CONST = 7
        block = ctx.enter_context(nc.Block())

        @block.sync
        def _(sp):
            with nc.allow_non_contiguous_dma(reason="one edge of each block"):
                sp.dma_start(lk[:, :], dst1.rearrange("(p c j) -> p c j", c=LC, j=LB)[:, :, LB - 1]).then_inc(s_lk, 16)
            tiles = (NT - 1) // XCH
            for n in range(XCH):
                sp.dma_start(X3[:, n * tiles:(n + 1) * tiles, :],
                             x_in[n * tiles * P:(n + 1) * tiles * P, :].rearrange("(i p) d -> p i d", p=P)).then_inc(s_x[n], 16)
            sp.wait_ge(s_pad, 5)
            sp.dma_start(X3[0:LAST, NT - 1, :], x_in[(NT - 1) * P:N, :]).then_inc(s_x[XCH], 16)
            even = FULL // 16 * 16
            for n, (v, at) in enumerate(((dst1, dst_all[:, 1:T + 1]), (src1, idx_all[:, 0:T]))):
                sp.dma_start(at[0:even, :], v[0:even * T].rearrange("(p t) -> p t", t=T)).then_inc(s_runs, 16)
                sp.dma_start(at[even:FULL, :], v[even * T:FULL * T].rearrange("(p t) -> p t", t=T)).then_inc(s_runs, 16)
                sp.dma_start(at[FULL:FULL + 1, 0:REST], v[FULL * T:E].rearrange("(p t) -> p t", p=1)).then_inc(s_runs, 16)
            with nc.allow_non_contiguous_dma(reason="the edge before each run"):
                sp.dma_start(dst_all[1:P, 0:1], 
                             dst1[0:(P - 1) * T].rearrange("(p t) -> p t", t=T)[:, T - 1:T]).then_inc(s_runs, 16)
            with sp.Fori(0, PAIRS) as i:
                for h in range(2):
                    sp.wait_ge(s_xt, done(i * 2 + h))
                    sp.dma_start(xtd[bass.ds((i * 2 + h) * P, P), :], xt[:, h, :, :].rearrange("p k n -> p (k n)")).then_inc(s_xst[h], 16)
            sp.wait_ge(s_xt, done(NT - 1))
            sp.dma_start(xtd[(NT - 1) * P:NT * P, :], xt[:, 0, :, :].rearrange("p k n -> p (k n)")).then_inc(s_xst[0], 16)
            sp.wait_ge(s_eTs, 1)
            sp.dma_start(e_d[1:NT * P + 1, :].rearrange("(i p) a -> i (p a)", p=P), endsT[:, :]).then_inc(s_ed, 16)
            sp.wait_ge(s_con, CONST)
            sp.dma_start(e_d[0:1, :], upto[1:2, 0:1]).then_inc(s_ed, 16)
            sp.wait_ge(s_ed, 32)
            sp.dma_start(startsT[:, :], e_d[0:NT * P, :].rearrange("(i p) a -> i (p a)", p=P)).then_inc(s_sld, 16)
            sp.wait_ge(s_dv, 1)
            sp.dma_start(tbl_p, TB3).then_inc(s_tbl, 16)

            def window(w, loads=(None, None)):
                for h in range(2):
                    if loads[h]:
                        load_tile(*loads[h])
                    sp.wait_ge(s_max, w * U + (h + 1) * HW + U)
                    sp.wait_ge(s_sum, w * U + (h + 1) * HW + U)
                    for to, ring_, c in ((W_run[0], stm, BF), (W_run[1], sts, 2 * BF)):
                        sp.dma_start(to[:, bass.ds(w * (U * c) + h * HW * c, HW * c)],
                                     ring_[:, h * HW:(h + 1) * HW, :].rearrange("p a b -> p (a b)")).then_inc(s_out[h], 16)

            def load_tile(n, ti, h):
                sp.wait_ge(s_pu, free(n))
                sp.dma_start(xl[:, h, :, :].rearrange("p k n -> p (k n)"), xtd[bass.ds(ti * P, P), :]).then_inc(s_xl[h], 16)

            sp.wait_ge(s_xst[0], 16 * PASS + 16)
            sp.wait_ge(s_xst[1], 16 * PAIRS + 16)
            load_tile(0, 0, 0)
            load_tile(1, 1, 1)
            for ps in range(3):
                n0 = ps * UNITS
                for h in range(2):
                    load_tile(n0 + 2 + h, 2 + h, h)
                with sp.Fori(0, PAIRS - 2) as i:
                    window(i + ps * PASS, [(i * 2 + (n0 + 4 + h), i * 2 + (4 + h), h) for h in range(2)])
                window(ps * PASS + PAIRS - 2, ((n0 + NT - 1, NT - 1, 0), None))
                window(ps * PASS + PAIRS - 1, [(n0 + UNITS + h, h, h) if ps < 2 else None for h in range(2)])
                window(ps * PASS + PAIRS)
            with sp.Fori(3 * PASS, WIN) as w:
                window(w)
            sp.wait_ge(s_ph, done(NT - 1))
            for n, name in enumerate(("L0_ffn_W1", "L0_ffn_W2", "L0_ffn_Wo")):
                for k in range(KD):
                    sp.dma_start(EW[n].rearrange("p (e k n) -> p e k n", e=EX, k=KD)[:, :, k, :], a[name][:, k * P:(k + 1) * P, :].rearrange("e p n -> p e n")).then_inc(s_ew[n], 16)

            def store(g, b, n=GT):
                sp.wait_ge(s_acc, (g + 1) * (ROUNDS * GT) + GT)
                if n == GT:
                    sp.dma_start(y[bass.ds(g * GN, GN), :].rearrange("(s p) d -> p s d", p=P), acc[:, b, :, :]).then_inc(s_y[b], 16)
                else:
                    sp.dma_start(y[(NT - 1) * P:N, :], acc[0:LAST, b, 0, :]).then_inc(s_y[b], 16)

            store(0, 0)
            with sp.Fori(0, GROUPS // 2 - 1) as i:
                store(i * 2 + 1, 1)
                store(i * 2 + 2, 0)
            store(GROUPS - 1, 1)
            store(GROUPS, 0, 1)
            sp.wait_ge(s_y[0], 16 * (GROUPS // 2 + 1) + 16)
            sp.wait_ge(s_y[1], 16 * (GROUPS // 2) + 16)

        @block.gpsimd
        def _(pool):
            pool.iota(iota[:, :], pattern=[[1, P]], base=0, channel_multiplier=0).then_inc(s_con, 1)
            pool.iota(node[:, :], pattern=[[P, NT]], base=0, channel_multiplier=1).then_inc(s_con, 1)
            pool.memset(ident[:, :], 0.0).then_inc(s_mask, 1)
            pool.memset(ones[:, :], 1.0).then_inc(s_con, 1)
            pool.wait_ge(s_con, 3)
            pool.wait_ge(s_mask, 1)
            pool.affine_select(out=upto[:, :], in_=ones[:, :], compare_op=ALU.is_ge, fill=0.0, base=0,
                               pattern=[[1, P]], channel_multiplier=-1).then_inc(s_con, 1)
            pool.affine_select(out=ident[:, :], in_=ident[:, :], compare_op=ALU.not_equal, fill=1.0, base=0,
                               pattern=[[-1, P]], channel_multiplier=1).then_inc(s_con, 1)
            pool.affine_select(out=ones_last[:, :], in_=ones[:, :], compare_op=ALU.is_ge, fill=0.0, base=LAST - 1,
                               pattern=[[0, P]], channel_multiplier=-1).then_inc(s_con, 1)
            pool.memset(TB3[:, :, BF + 1:RW], 0.0).then_inc(s_con, 1)
            for n, name in enumerate(("L0_gnn_conv_bias", "L0_gnn_gn_weight", "L0_gnn_gn_bias", "L0_gnn_gn_mean_scale")):
                pool.dma_start(rows[:, n, :], row_of(a[name])).then_inc(s_wide, 16)
            pool.dma_start(b_comb[:, :], row_of(a["L0_gnn_b_comb"])).then_inc(s_wide, 16)
            pool.dma_start(b_r[:, :], row_of(a["L0_ffn_br"])).then_inc(s_wide, 16)
            pool.wait_ge(s_bidx, 1)
            for i in range(NT):
                pool.indirect_dma_start(out=blk[:, i, :], out_offset=None, in_=dst_blocks,
                                        in_offset=bass.IndirectOffsetOnAxis(ap=bidx[:, i:i + 1], axis=0)).then_inc(s_blk, 16)
            pool.wait_ge(s_ed, 32)
            pool.wait_ge(s_nix, 1)
            pool.indirect_dma_start(out=col[:, 3:4], out_offset=None, in_=e_d[:, :],
                                    in_offset=bass.IndirectOffsetOnAxis(ap=nidx[:, 0:1], axis=0)).then_inc(s_en, 16)
            pool.wait_ge(s_tbl, 16)
            pool.dma_start(b_out, row_of(a["L0_mix_b_out"])).then_inc(s_wide, 16)
            pool.dma_start(g_out, row_of(a["L0_mix_g_out"])).then_inc(s_wide, 16)
            with pool.Fori(0, WIN) as w:
                for u in range(U):
                    if u % HW == 0:
                        pool.wait_ge(s_iw, w * 2 + u // HW + 1)
                    if u % 4 == 0:
                        pool.wait_ge(s_max, w * U + u + 4)
                        pool.wait_ge(s_sum, w * U + u + 4)
                        pool.sem_inc(s_seen, 1)
                    pool.indirect_dma_start(out=ring[:, u, 0:RW], out_offset=None, in_=tbl[:, :],
                                            in_offset=bass.IndirectOffsetOnAxis(ap=iw[:, u:u + 1], axis=0)).then_inc(s_g[u], 16)
            pool.wait_ge(s_iw, 2 * WIN + 2)
            pool.wait_ge(s_out[0], 32 * WIN + 32)
            pool.wait_ge(s_out[1], 32 * WIN + 32)
            pool.wait_ge(s_fz, 1)
            at = bass.IndirectOffsetOnAxis(ap=fidx[:, 0:1], axis=0)
            parts = ((Wd[0], 0, BF), (Wd[1], BF, ST))
            for wd, c0, c1 in parts:
                pool.indirect_dma_start(out=fix[:, c0:c1], out_offset=None, in_=wd[:, :], in_offset=at,
                                        bounds_check=E - 1, oob_is_err=False).then_inc(s_fixg, 16)
            pool.wait_ge(s_fix, 3)
            for wd, c0, c1 in parts:
                pool.indirect_dma_start(out=wd[:, :], out_offset=at, in_=fix[:, c0:c1], in_offset=None,
                                        bounds_check=E - 1, oob_is_err=False).then_inc(s_fixs, 16)
            pool.wait_ge(s_fixs, 32)
            for i in range(NT):
                if i >= GR:
                    pool.wait_ge(s_pr, done(i - GR))
                for wd, c0, c1 in parts:
                    pool.indirect_dma_start(out=got[:, i % GR, c0:c1], out_offset=None, in_=wd[:, :],
                                            in_offset=bass.IndirectOffsetOnAxis(ap=pos[:, i:i + 1], axis=0)).then_inc(s_gf[i % GR], 16)

            for n in range(3):
                pool.wait_ge(s_wh, n + 1)
                pool.tensor_tensor(EWL[n], EW[n], as_f32(EWH[n]), ALU.subtract).then_inc(s_wl, 1)

        @block.scalar
        def _(act):
            act.dma_start(wb[:, :, :], a["L0_gnn_W_bases"].rearrange("(k p) n -> p k n", p=P)).then_inc(s_w, 16)
            act.dma_start(wc[:, :, 0:CW], a["L0_gnn_W_comb"].rearrange("(k p) n -> p k n", p=P)).then_inc(s_w, 16)
            wq = a["L0_mix_w_qkv"].rearrange("(k p) n -> p k n", p=P)
            act.dma_start(wc[:, :, CW:CW + 2 * HID], wq[:, :, HID:3 * HID]).then_inc(s_w, 16)
            act.dma_start(wc[:, :, CW + 2 * HID:CW + 3 * HID], wq[:, :, 0:HID]).then_inc(s_w, 16)
            act.dma_start(wo[:, :], a["L0_mix_w_out"]).then_inc(s_w, 16)
            act.dma_start(wr[:, :, :], a["L0_ffn_Wr"].rearrange("(k p) n -> p k n", p=P)).then_inc(s_w, 16)
            act.dma_start(bo[:, :], a["L0_ffn_bo"]).then_inc(s_w, 16)
            for l in range(2):
                for n, name in enumerate(("b", "g", "be", "m", "v")):
                    act.dma_start(bnp[n * EX * KD:(n + 1) * EX * KD, l, :],
                                  a[f"L0_ffn_{name}{l + 1}"].rearrange("e (k p) -> (e k) p", p=P)).then_inc(s_w, 16)
            for n in range(2):
                act.dma_start(mk[:, n, :], a["L0_mix_mem_kv"][n].rearrange("h d m -> (h d) m")).then_inc(s_w, 16)
            with nc.allow_non_contiguous_dma(reason="a vector as columns"):
                act.dma_start(gpre[:, :], a["L0_mix_g_pre"].rearrange("(k p) -> p k", p=P)).then_inc(s_w, 16)
            for s in (s_xt, s_tb, s_ek, s_h, s_sq):
                act.sem_inc(s, RING2)
            act.sem_inc(s_h1, KD)
            act.sem_inc(s_h2, KD)
            act.wait_ge(s_q1, 1)
            act.activation(tb_, ta, ACT.Sqrt).then_inc(s_q2, 1)
            act.wait_ge(s_q1, 2)
            act.activation(tb_, ta, ACT.Sqrt).then_inc(s_q2, 1)

            def tile_a(n, i, h):
                act.wait_ge(s_tr, done(n))
                act.wait_ge(s_bs, free(n))
                act.wait_ge(s_xst[h], i * 16 + 16)
                act.activation(xt[:, h, :, :].rearrange("p k n -> p (k n)"), bank[5 * h][:, 0:D], ACT.Copy).then_inc(s_xt, 1)

            def tile_b(n, h):
                act.wait_ge(s_bs, done(n))
                act.activation(TB3[:, bass.ds(n, 1), 0:BF].rearrange("p a f -> p (a f)"), bank[1 + h][:, 0:BF], ACT.Copy).then_inc(s_tb, 1)

            with act.Fori(0, PAIRS) as i:
                for h in range(2):
                    tile_a(i * 2 + h, i, h)
                for h in range(2):
                    tile_b(i * 2 + h, h)
            tile_a(NT - 1, PAIRS, 0)
            tile_b(NT - 1, 0)
            act.wait_ge(s_q1, 3)
            act.activation(tb_, ta, ACT.Sqrt).then_inc(s_q2, 1)
            act.wait_ge(s_runs, 16 * 7)
            act.wait_ge(s_pad, 5)
            for h in range(2):
                act.copy(iw[:, h * HW:(h + 1) * HW], idx_all[:, h * HW:(h + 1) * HW]).then_inc(s_iw, 1)
            act.wait_ge(s_bnv, 1)
            act.activation(bnt[:, :, :].rearrange("p a b -> p (a b)"), bns[:, :, :].rearrange("p a b -> p (a b)"), ACT.Sqrt).then_inc(s_bnq, 1)

            def window(w, hook):
                for u in range(U):
                    act.wait_ge(s_g[u], w * 16 + 16)
                    act.activation(ring[:, u, RW:RW + BF], ring[:, u, 0:BF], ACT.Copy, scale=ring[:, u, BF:BF + 1]).then_inc(s_prod, 1)
                    if u % HW == HW - 1:
                        h = u // HW
                        act.copy(iw[:, h * HW:(h + 1) * HW], idx_all[:, bass.ds(w * U + U + h * HW, HW)]).then_inc(s_iw, 1)
                    if hook:
                        hook(u)

            def pass_c(n, h, s, last=False):
                R = LAST if last else P
                if s == 2:
                    act.wait_ge(s_pu, done(n + UNITS))
                    act.wait_ge(s_cx, free(n))
                    act.activation(vs[0:R, h, 0:HID], bank[5 + h][0:R, 0:HID], ACT.Copy, scale=rn[0:R, bass.ds(n, 1)])
                    act.wait_ge(s_kt, done(n))
                    act.activation(ek[0:R, h, :], kt[0:R, h, :], ACT.Exp).then_inc(s_ek, 2 if last else 1)

            def pass_d(i, u, m=2):
                if u == 4:
                    act.wait_ge(s_qd, i + 1)
                    for h in range(m):
                        e = act.activation(eq[:, h, :], qd[:, h, :], ACT.Exp, scale=rn[:, bass.ds(i * 2 + h, 1)])
                    e.then_inc(s_eq, 1)
                if u == 1:
                    for h in range(m):
                        x1 = X3[:, bass.ds(i * 2 + h, 1), :].rearrange("p a f -> p (a f)")
                        act.activation(x1, x1, ACT.Identity, scale=opr[:, bass.ds(i * 2 + h, 1)], bias=nmr[:, bass.ds(i * 2 + h, 1)])
                if u == 10:
                    act.wait_ge(s_qT, i + 1)
                    act.activation(qT[:, 0:m, :], bank[4][:, 0:m * P].rearrange("p (b n) -> p b n", b=m), ACT.Copy).then_inc(s_qTc, 1)
                if u == 13:
                    act.wait_ge(s_mx, i + 1)
                    for h in range(m):
                        q = act.activation(xs[:, h, :], bank[5 + h][:, 0:D], ACT.Square, accum_out=nrm[:, h:h + 1])
                    q.then_inc(s_act, 1)
                    act.wait_ge(s_act, i + 1)
                    act.activation(nrm[:, 2:2 + m], nrm[:, 0:m], ACT.Sqrt).then_inc(s_nr, 1)

            with act.Fori(0, PASS) as w:
                window(w, None)
            act.wait_ge(s_em, 1)
            act.activation(mkm[:, 0:MEM], mk[:, 0, :], ACT.Exp, bias=col[:, 8:9]).then_inc(s_em, 1)
            act.wait_ge(s_emT, 1)
            act.activation(mT[:, 0:2 * P], bank[6][0:MEM, 0:2 * P], ACT.Copy).then_inc(s_emc, 1)
            with act.Fori(0, PAIRS) as i:
                window(i + PASS, lambda u: pass_c(i * 2 + u // HW, u // HW, u % HW))
            window(PASS + PAIRS, lambda u: pass_c(NT - 1, 0, u, True) if u < HW else None)
            act.wait_ge(s_cT, 1)
            act.activation(diag[:, :], bank[7][:, 256:384], ACT.Copy).then_inc(s_cTc, 1)
            with act.Fori(0, PAIRS) as i:
                window(i + 2 * PASS, lambda u: pass_d(i, u))
            window(2 * PASS + PAIRS, lambda u: pass_d(PAIRS, u, 1))
            with act.Fori(3 * PASS, WIN) as w:
                window(w, None)

            def h_out(n, b):
                act.wait_ge(s_ph, done(n))
                act.activation(H3[:, bass.ds(n, 1), :].rearrange("p a f -> p (a f)"), bank[1 + b][:, 0:D], ACT.Copy).then_inc(s_h, 1)

            with act.Fori(0, PAIRS) as i:
                for b in range(2):
                    h_out(i * 2 + b, b)
            h_out(NT - 1, 0)

            def square(n, b):
                act.wait_ge(s_hc, n + 1)
                act.wait_ge(s_vr, n + 1)
                act.activation(sq[:, b, :], H3[:, bass.ds(n, 1), :].rearrange("p a f -> p (a f)"), ACT.Square).then_inc(s_sq, 1)

            with act.Fori(0, NT // SQ) as i:
                for b in range(SQ):
                    square(i * SQ + b, b)
            square(NT - 1, 0)
            act.wait_ge(s_gq, 1)
            act.activation(gnt[:, :], gnc[:, :], ACT.Sqrt).then_inc(s_gr, 1)


            def evac(l, g, e, w, m_bias):
                sL, sh = ((s_L1, s_h1), (s_L2, s_h2))[l]
                q = g * EX + e
                act.wait_ge(s_lo[l], q + 1)
                if l == 0:
                    act.wait_ge(s_L2, q * 2 + (L_START - 2))
                else:
                    act.wait_ge(s_L3, g * (ROUNDS * GT) + e * GT + (GT if e >= 2 else 0) + L3_START - 2 * GT)
                for m in range(KD):
                    act.wait_ge(sL, q * 2 + (m + 1 + L_START))
                    bias, scale = bnb[:, l, m_bias + m:m_bias + m + 1], bns[:, l, m_bias + m:m_bias + m + 1]
                    act.activation(hf[:, l, m * w:(m + 1) * w], bank[2 * l + m][:, 0:w], ACT.Relu, bias=bias, scale=scale).then_inc(sh, 1)

            def front_root(G, ng=GT):
                act.wait_ge(s_f1, G + 1)
                act.activation(ln[:, 1, 0:ng], ln[:, 0, 0:ng], ACT.Ln).then_inc(s_ln, 1)
                act.wait_ge(s_ln, G + 1)
                act.activation(ln[:, 2, 0:ng], ln[:, 1, 0:ng], ACT.Exp, scale=-0.5).then_inc(s_f2, 1)

            def front_out(G, gb, w=GN):
                act.wait_ge(s_f4, G + 1)
                act.activation(xg[:, gb, 0, 0:KD * w], bank[6][:, 0:KD * w], ACT.Copy).then_inc(s_f5, 1)

            def group(g, gb, w, w_next):
                ng = w // P
                for e in range(EX):
                    if e + 1 < EX:
                        evac(0, g, e + 1, w, (e + 1) * KD)
                    elif w_next:
                        evac(0, g + 1, 0, w_next, 0)
                    evac(1, g, e, w, e * KD)
                    if e == 0:
                        act.wait_ge(s_lm, g + 1)
                        act.activation(lg[:, 0:ng, :], lg[:, 0:ng, :], ACT.Exp).then_inc(s_le, 1)
                    if e == 2:
                        act.wait_ge(s_wT, g + 1)
                        act.activation(wT[:, 0:w], bank[7][0:EX, 0:w], ACT.Copy).then_inc(s_wTc, 1)
                    if e == 2 and w_next:
                        front_root(g + 1, w_next // P)
                    if e == 5 and w_next:
                        front_out(g + 1, 1 - gb, w_next)

            front_root(0)
            front_out(0, 0)
            for n in range(3):
                act.wait_ge(s_ew[n], 16 * KD)
                act.wait_ge(s_bo, min(-(-(n + 1) * EWN // D), NT))
                act.activation(EWH[n], EW[n], ACT.Copy).then_inc(s_wh, 1)
            evac(0, 0, 0, GN, 0)
            group(0, 0, GN, GN)
            with act.Fori(0, GROUPS // 2 - 1) as i:
                group(i * 2 + 1, 1, GN, GN)
                group(i * 2 + 2, 0, GN, GN)
            group(GROUPS - 1, 1, GN, P)
            group(GROUPS, 0, P, 0)

        @block.tensor
        def _(pe):
            for s in (s_tr, s_bs, s_pu, s_cx, s_ph):
                pe.sem_inc(s, RING2)
            pe.sem_inc(s_vr, SQ)
            pe.sem_inc(s_L1, L_START)
            pe.sem_inc(s_wTc, 1)
            pe.sem_inc(s_L2, L_START)
            pe.sem_inc(s_L3, L3_START)
            pe.wait_ge(s_con, CONST)
            pe.wait_ge(s_oh, 2)
            for c in range(LC):
                mm = pe.matmul(bank[3][:, 0:NT], oh_lo[:, c, :], oh_hi[:, c, :], start=(c == 0), stop=(c == LC - 1))
            mm.then_inc(s_hist, 1)
            pe.wait_ge(s_hists, 1)
            pe.matmul(bank[3][:, 64:64 + NT], upto[:, :], hist, start=True, stop=True)
            pe.matmul(bank[3][:, 128:128 + NT], ones[:, :], hist, start=True, stop=True).then_inc(s_pref, 1)
            pe.wait_ge(s_w, 16 * 20)

            def turn(n, h):
                pe.wait_ge(s_xs, done(n))
                pe.wait_ge(s_xt, free(n))
                for k in range(KD):
                    mm = pe.transpose(bank[5 * h][:, k * P:(k + 1) * P], xs[:, h, k * P:(k + 1) * P], ident[:, :])
                mm.then_inc(s_tr, 1)

            def base(n, h):
                pe.wait_ge(s_xt, done(n))
                pe.wait_ge(s_tb, free(n))
                for k in range(KD):
                    mm = pe.matmul(bank[1 + h][:, 0:BF], xt[:, h, k, :], wb[:, k, :], start=(k == 0), stop=(k == KD - 1))
                mm.then_inc(s_bs, 1)

            with pe.Fori(0, PAIRS) as i:
                for h in range(2):
                    turn(i * 2 + h, h)
                for h in range(2):
                    base(i * 2 + h, h)
            turn(NT - 1, 0)
            base(NT - 1, 0)
            pe.wait_ge(s_e, 1)
            pe.transpose(bank[3][0:NT, 0:P], ends, ident[:, :]).then_inc(s_eT, 1)
            pe.wait_ge(s_sld, 16)
            pe.transpose(bank[3][:, 128:128 + NT], startsT[:, :], ident[0:NT, 0:NT]).then_inc(s_sT, 1)
            for l in range(2):
                mm = pe.transpose(bank[4][:, l * P:l * P + 5 * EX * KD], bnp[:, l, :], ident[0:5 * EX * KD, 0:5 * EX * KD])
            mm.then_inc(s_bnT, 1)
            pe.wait_ge(s_dgw, 1)
            pe.matmul(bank[0][:, 0:P], ones[:, :], diag[:, :], start=True, stop=True).then_inc(s_Bw, 1)

            def unit(ps, i, h, parts, inc=1):
                pe.wait_ge(s_xl[h], i * 16 + 16 * (ps * (PAIRS if h else PASS) + 1))
                for to, c0, c1 in parts:
                    for k in range(KD):
                        mm = pe.matmul(bank[to + h][:, 0:c1 - c0], xl[:, h, k, :], wc[:, k, c0:c1], start=(k == 0), stop=(k == KD - 1))
                mm.then_inc(s_pu, inc)

            pe.wait_ge(s_tb, done(NT - 1))
            pe.wait_ge(s_mask, 3)
            with pe.Fori(0, PAIRS) as i:
                for h in range(2):
                    pe.wait_ge(s_kb, free(i * 2 + h))
                    unit(0, i, h, ((1, 0, CW + HID),))
            pe.wait_ge(s_kb, free(NT - 1))
            unit(0, PAIRS, 0, ((1, 0, CW + HID),), 2)
            pe.wait_ge(s_Mw, 1)
            pe.transpose(bank[7][:, 384:512], M[:, :], ident[:, :]).then_inc(s_MT, 1)
            pe.wait_ge(s_dg, 1)
            pe.matmul(bank[7][:, 256:384], ones[:, :], diag[:, :], start=True, stop=True).then_inc(s_Mb, 1)
            pe.wait_ge(s_em, 2)
            pe.transpose(bank[6][0:MEM, 0:P], mkm[:, 0:MEM], ident[:, :])
            pe.transpose(bank[6][0:MEM, P:2 * P], mk[:, 1, :], ident[:, :]).then_inc(s_emT, 1)
            pe.wait_ge(s_emc, 1)
            pe.wait_ge(s_mem, 1)
            pe.matmul(bank[3][:, 0:HID + 1], mT[:, 0:P], mT[:, P:2 * P + 1], start=True, stop=False)

            def ctx_mm(n, h, last=False):
                R = LAST if last else P
                pe.wait_ge(s_ek, done(n))
                pe.matmul(bank[3][:, 0:HID + 1], ek[0:R, h, :], vs[0:R, h, :], start=False, stop=last).then_inc(s_cx, 2 if last else 1)

            def kv(n, i, h, inc=1):
                pe.wait_ge(s_kt, free(n))
                pe.wait_ge(s_ek, free(n))
                unit(1, i, h, ((1, CW, CW + HID), (5, CW + HID, CW + 2 * HID)), inc)

            pe.wait_ge(s_kb, done(NT))
            for h in range(2):
                kv(h, 0, h)
            with pe.Fori(0, PAIRS - 1) as i:
                for h in range(2):
                    ctx_mm(i * 2 + h, h)
                    kv(i * 2 + (2 + h), i + 1, h)
            ctx_mm(NT - 3, 0)
            kv(NT - 1, PAIRS, 0, 2)
            ctx_mm(NT - 2, 1)
            ctx_mm(NT - 1, 0, True)
            pe.wait_ge(s_cbd, 1)
            pe.transpose(bank[7][:, 256:384], diag[:, :], ident[:, :]).then_inc(s_cT, 1)
            pe.wait_ge(s_cTc, 1)
            pe.matmul(bank[7][:, 0:D], diag[:, :], wo[:, :], start=True, stop=True).then_inc(s_m2, 1)
            pe.wait_ge(s_m2c, 1)

            def q_mm(i, m=2):
                for h in range(m):
                    unit(2, i, h, ((1, CW + 2 * HID, CW + 3 * HID),), 3 - m)

            def mix(i, m=2):
                pe.wait_ge(s_qn, i + 1)
                for h in range(m):
                    mm = pe.transpose(bank[4][:, h * P:(h + 1) * P], qn[:, h, :], ident[:, :])
                mm.then_inc(s_qT, 1)
                pe.wait_ge(s_qTc, i + 1)
                pe.wait_ge(s_mo, i + 1)
                for h in range(m):
                    mm = pe.matmul(bank[5 + h][:, 0:D], qT[:, h, :], m2[:, :], start=True, stop=True)
                mm.then_inc(s_mx, 1)

            pe.wait_ge(s_kt, done(NT))
            pe.wait_ge(s_ek, done(NT))
            q_mm(0)
            with pe.Fori(0, PAIRS - 1) as i:
                pe.wait_ge(s_qd, i + 1)
                q_mm(i + 1)
                mix(i)
            pe.wait_ge(s_qd, PAIRS)
            q_mm(PAIRS, 1)
            mix(PAIRS - 1)
            mix(PAIRS, 1)

            pe.wait_ge(s_max, WIN * U + U)
            pe.wait_ge(s_sum, WIN * U + U)
            for n in range(AGGS):
                mm = pe.transpose(bank[4][:, n * P:(n + 1) * P], stm[:, U - 1, :] if n == 0 else sts[:, U - 1, (n - 1) * BF:n * BF], ident[:, :])
            mm.then_inc(s_tl, 1)
            pe.wait_ge(s_car, AGGS)
            pe.wait_ge(s_mo, PASS + 1)
            for n in range(AGGS):
                mm = pe.transpose(bank[5][:, n * P:(n + 1) * P], carT[:, n, 0:P], ident[:, :])
            mm.then_inc(s_carT, 1)

            def add_up(n, b):
                pe.wait_ge(s_pr, done(n))
                pe.wait_ge(s_h, free(n))
                for k in (*range(2 * BASES), *range(2 * BASES + PRE, KC)):
                    mm = pe.matmul(bank[1 + b][:, 0:D], ident[:, :], prod[:, b, k, :], start=(k == 0), stop=(k == KC - 1))
                mm.then_inc(s_ph, 1)

            def sum_nodes(n, start=False, stop=False):
                pe.wait_ge(s_h, done(n))
                return pe.matmul(bank[3][:, 0:D], ones[:, :], H3[:, bass.ds(n, 1), :].rearrange("p a f -> p (a f)"), start=start, stop=stop)

            add_up(0, 0)
            sum_nodes(0, start=True)
            with pe.Fori(0, PAIRS - 1) as i:
                add_up(i * 2 + 1, 1)
                add_up(i * 2 + 2, 0)
                sum_nodes(i * 2 + 1)
                sum_nodes(i * 2 + 2)
            add_up(NT - 2, 1)
            add_up(NT - 1, 0)
            sum_nodes(NT - 2)
            sum_nodes(NT - 1, stop=True).then_inc(s_sm, 1)

            def sum_squares(n, b, w, start=False, stop=False):
                pe.wait_ge(s_sq, done(n))
                pe.matmul(bank[4][:, 0:D], w, sq[:, b, :], start=start, stop=stop).then_inc(s_vr, 1)

            sum_squares(0, 0, ones[:, :], start=True)
            sum_squares(1, 1, ones[:, :])
            sum_squares(2, 2, ones[:, :])
            sum_squares(3, 3, ones[:, :])
            with pe.Fori(1, NT // SQ) as i:
                for b in range(SQ):
                    sum_squares(i * SQ + b, b, ones[:, :])
            sum_squares(NT - 1, 0, ones_last[:, :], stop=True)

            PARTS = ((0, 0), (1, 0), (0, 1))

            def front_turn(G, w=GN):
                pe.wait_ge(s_f3, G + 1)
                for k in range(KD):
                    for s in range(w // P):
                        mm = pe.transpose(bank[6][:, k * w + s * P:k * w + (s + 1) * P], xf[:, s, k * P:(k + 1) * P], ident[:, :])
                mm.then_inc(s_f4, 1)

            def layer(l, g, e, gb, w):
                q = g * EX + e
                sL, sE = ((s_L1, s_h1), (s_L2, s_h2))[l]
                rhs = xg[:, gb, :, :] if l == 0 else hid[0][:, e % 2, :, :]
                if isinstance(g, int) and g == 0:
                    pe.wait_ge(s_wl, l + 1)
                if l == 1:
                    pe.wait_ge(s_up[0], q + 1)
                for parts in (PARTS[:2], PARTS[2:]):
                    if l == 1 and parts == PARTS[2:]:
                        pe.wait_ge(s_lo[0], q + 2)
                    for m in range(KD):
                        if parts == PARTS[:2]:
                            pe.wait_ge(sE, q * 2 + (m + 1))
                        for wp, xp in parts:
                            for k in range(KD):
                                mm = pe.matmul(bank[2 * l + m][:, 0:w], EWP[l][wp][:, e, k, m * P:(m + 1) * P], rhs[:, xp, k * w:(k + 1) * w],
                                               start=(wp == 0 and xp == 0 and k == 0), stop=(xp == 1 and k == KD - 1))
                        if parts == PARTS[2:]:
                            mm.then_inc(sL, 1)

            def layer3(g, e, w):
                q = g * EX + e
                if isinstance(g, int) and g == 0:
                    pe.wait_ge(s_wl, 3)
                pe.wait_ge(s_lo[1], q + 2)
                ng = w // P
                h2 = hid[1][:, e % 2, :, :]
                for s in range(ng):
                    pe.wait_ge(s_acc, g * (ROUNDS * GT) + (e * GT + s + 1))
                    for wp, xp in PARTS:
                        for k in range(KD):
                            mm = pe.matmul(bank[4 + s][:, 0:D], h2[:, xp, k * w + s * P:k * w + (s + 1) * P], EWP[2][wp][:, e, k, :],
                                           start=(wp == 0 and xp == 0 and k == 0), stop=(xp == 1 and k == KD - 1))
                    mm.then_inc(s_L3, 1 if ng == GT else GT)

            def router(g, gb, w):
                pe.wait_ge(s_wTc, g + 1)
                for s in range(w // P):
                    for part in range(2):
                        for k in range(KD):
                            mm = pe.matmul(bank[7][:, s * EX:(s + 1) * EX], as_f32(xg[:, gb, part, k * w + s * P:k * w + (s + 1) * P]), wr[:, k, :],
                                           start=(part == 0 and k == 0), stop=(part == 1 and k == KD - 1))
                mm.then_inc(s_lg, 1)

            def weights_out(g, gb, w):
                pe.wait_ge(s_ws, g + 1)
                for s in range(w // P):
                    mm = pe.transpose(bank[7][0:EX, s * P:(s + 1) * P], wsm[:, gb, s, :], ident[:, :])
                mm.then_inc(s_wT, 1)

            def bias_round(g, w):
                pe.wait_ge(s_wTc, g + 2)
                ng = w // P
                for s in range(ng):
                    pe.wait_ge(s_acc, g * (ROUNDS * GT) + (EX * GT + s + 1))
                    pe.matmul(bank[4 + s][:, 0:D], wT[:, s * P:(s + 1) * P], bo[:, :],
                              start=True, stop=True).then_inc(s_L3, 1 if ng == GT else GT)

            def first(g, gb, w):
                pe.wait_ge(s_f5, g + 1)
                pe.wait_ge(s_f6, g + 1)
                layer(0, g, 0, gb, w)
                router(g, gb, w)

            def group(g, gb, w, w_before, w_next):
                for e in range(EX):
                    if e + 1 < EX:
                        layer(0, g, e + 1, gb, w)
                    elif w_next:
                        first(g + 1, 1 - gb, w_next)
                    if e == 1 and w_before:
                        bias_round(g - 1, w_before)
                    layer(1, g, e, gb, w)
                    if e == 0 and w_before:
                        layer3(g - 1, EX - 1, w_before)
                    if e == 2:
                        weights_out(g, gb, w)
                    if e == 5 and w_next:
                        front_turn(g + 1, w_next)
                    if e > 0:
                        layer3(g, e - 1, w)

            front_turn(0)
            first(0, 0, GN)
            group(0, 0, GN, 0, GN)
            with pe.Fori(0, GROUPS // 2 - 1) as i:
                group(i * 2 + 1, 1, GN, GN, GN)
                group(i * 2 + 2, 0, GN, GN, GN)
            group(GROUPS - 1, 1, GN, GN, P)
            group(GROUPS, 0, P, GN, 0)
            layer3(GROUPS, EX - 1, P)
            bias_round(GROUPS, P)

        @block.vector
        def _(v):
            ch = Chain(v, s_dve)
            for s in (s_xs, s_kb, s_kt, s_pr):
                v.sem_inc(s, RING2)
            v.sem_inc(s_acc, GT)
            for h in range(2):
                v.sem_inc(s_lo[h], 1)
                v.sem_inc(s_out[h], 32)
                v.sem_inc(s_y[h], 16)
                v.sem_inc(s_xst[h], 16)
            v.memset(idx_all[96:P, REST:T + U], 0).then_inc(s_pad, 1)
            v.memset(idx_all[0:96, T:T + U], 0).then_inc(s_pad, 1)
            v.memset(dst_all[96:P, REST + 1:T + 1], -1).then_inc(s_pad, 1)
            v.memset(dst_all[0:1, 0:1], -1).then_inc(s_pad, 1)
            v.memset(X3[96:P, NT - 1, :], 0.0).then_inc(s_pad, 1)

            def inv_root(y, val, t):
                ch(v.tensor_tensor(t, y, y, ALU.mult))
                ch(v.tensor_tensor(t, t, val, ALU.mult))
                ch(v.tensor_scalar(t, t, -0.5, 1.5, ALU.mult, ALU.add))
                ch(v.tensor_tensor(y, y, t, ALU.mult))

            v.wait_ge(s_lk, 16)
            ch.mark(v.tensor_scalar(lo[:, :], lk[:, :], P - 1, None, ALU.bitwise_and))
            ch(v.tensor_scalar(hi[:, :], lk[:, :], 7, None, ALU.arith_shift_right))
            v.wait_ge(s_con, CONST)
            v.tensor_tensor(oh_lo, bcast(iota[0:LP, :].unsqueeze(1), [LP, LC, P]), bcast(lo[:, :].unsqueeze(2), [LP, LC, P]),
                            ALU.is_equal).then_inc(s_oh, 1)
            v.tensor_tensor(oh_hi, bcast(iota[0:LP, 0:NT].unsqueeze(1), [LP, LC, NT]), bcast(hi[:, :].unsqueeze(2), [LP, LC, NT]),
                            ALU.is_equal).then_inc(s_oh, 1)
            ch(v.memset(one_nt, 1.0))
            v.wait_ge(s_hist, 1)
            v.tensor_copy(hist, bank[3][:, 0:NT]).then_inc(s_hists, 1)
            v.wait_ge(s_pref, 1)
            ch(v.tensor_copy(tot, bank[3][:, 128:128 + NT]))
            ch(v.tensor_tensor_scan(incl, one_nt, tot, 0.0, ALU.mult, ALU.add))
            ch(v.tensor_tensor(incl, incl, tot, ALU.subtract))
            ch(v.tensor_tensor(bf, incl, bank[3][:, 64:64 + NT], ALU.add))
            ch(v.tensor_scalar(bf, bf, float(NB - 1), None, ALU.min))
            v.tensor_copy(bidx[:, :], bf).then_inc(s_bidx, 1)

            def stats(n):
                ch.mark(v.bn_stats(bn_x[:, bass.ds(n, 1), :].rearrange("p a f -> p (a f)"), X3[:, bass.ds(n, 1), :].rearrange("p a f -> p (a f)")))

            tiles = (NT - 1) // XCH
            for c in range(XCH):
                v.wait_ge(s_x[c], 16)
                for n in range(c * tiles, (c + 1) * tiles):
                    stats(n)
            v.wait_ge(s_x[XCH], 16)
            stats(NT - 1)
            v.wait_ge(s_dve, ch.n)
            half = [bn_x[:, :, n:n + 1].rearrange("p i a -> p (i a)") for n in range(6)]
            ch.mark(v.tensor_tensor(mean, half[1], half[4], ALU.add))
            ch.mark(v.tensor_tensor(tc, half[1], half[4], ALU.subtract))
            ch(v.tensor_tensor(var, half[2], half[5], ALU.add))
            ch.mark(v.tensor_scalar(mean, mean, 0.5, None, ALU.mult))
            ch.mark(v.tensor_scalar(var, var, 1.0 / D, None, ALU.mult))
            ch(v.tensor_tensor(tc, tc, tc, ALU.mult))
            ch(v.scalar_tensor_tensor(out=var, in0=tc, scalar=0.25, in1=var, op0=ALU.mult, op1=ALU.add))
            v.tensor_scalar(ta, var, LN_EPS, None, ALU.add).then_inc(s_q1, 1)
            v.wait_ge(s_q2, 1)
            ch(v.reciprocal(rstd, tb_))
            inv_root(rstd, ta, tc)
            ch(v.scalar_tensor_tensor(out=nmr, in0=mean, scalar=-1.0, in1=rstd, op0=ALU.mult, op1=ALU.mult))
            ch(v.tensor_tensor(tc, rstd, rstd, ALU.mult))
            ch(v.tensor_scalar(opr, rstd, 1.0, None, ALU.add))
            v.scalar_tensor_tensor(out=ta, in0=var, scalar=float(D), in1=tc, op0=ALU.mult, op1=ALU.mult).then_inc(s_q1, 1)

            def norm(n, h):
                v.wait_ge(s_tr, free(n))
                v.tensor_scalar(xs[:, h, :], X3[:, bass.ds(n, 1), :].rearrange("p a f -> p (a f)"), rstd[:, bass.ds(n, 1)], nmr[:, bass.ds(n, 1)],
                                ALU.mult, ALU.add).then_inc(s_xs, 1)

            with v.Fori(0, PAIRS) as i:
                for h in range(2):
                    norm(i * 2 + h, h)
            norm(NT - 1, 0)
            v.wait_ge(s_q2, 2)
            ch(v.tensor_scalar(tb_, tb_, 1e-12, None, ALU.max))
            ch(v.reciprocal(rn, tb_))
            ch(v.tensor_scalar(rn, rn, float(D) ** 0.5, None, ALU.mult))

            v.wait_ge(s_runs, 16 * 7)
            ch(v.tensor_tensor(con, dst_all[:, 1:T + 1], dst_all[:, 0:T], ALU.is_equal))
            ch(v.tensor_copy(col[:, 0:1], con[:, 0:1]))
            ch(v.memset(con[:, 0:1], 0.0))
            ch(v.tensor_scalar(neg, con, 1.0, BIG, ALU.subtract, ALU.mult))
            ch(v.tensor_tensor(col[:, 1:2], dst_all[:, 1:2], dst_all[:, T:T + 1], ALU.is_equal))
            ch(v.tensor_tensor(col[:, 1:2], col[:, 1:2], col[:, 0:1], ALU.mult))
            v.tensor_scalar(diag[:, :], ident[:, :], col[:, 1:2], None, ALU.mult).then_inc(s_dgw, 1)
            v.tensor_scalar(nidx[:, :], dst_all[:, 1:2], 1.0, None, ALU.add).then_inc(s_nix, 1)

            v.wait_ge(s_blk, 16 * NT)
            ch(v.tensor_tensor(below, blk, bcast(node[:, :].unsqueeze(2), [P, NT, LB]), ALU.is_le))
            ch(v.tensor_reduce(cnt, below, AX.X, ALU.add))
            v.scalar_tensor_tensor(out=ends, in0=bf, scalar=float(LB), in1=cnt, op0=ALU.mult, op1=ALU.add).then_inc(s_e, 1)
            v.wait_ge(s_eT, 1)
            v.tensor_copy(endsT[:, :], bank[3][0:NT, 0:P]).then_inc(s_eTs, 1)
            v.wait_ge(s_sT, 1)
            ch(v.tensor_copy(starts, bank[3][:, 128:128 + NT]))
            ch(v.tensor_tensor(edges, ends, starts, ALU.subtract))
            ch(v.tensor_scalar(deg, edges, 1.0, None, ALU.add))
            v.tensor_copy(ta, deg).then_inc(s_q1, 1)
            v.wait_ge(s_q2, 3)
            ch(v.reciprocal(dinv, tb_))
            inv_root(dinv, deg, tc)
            v.wait_ge(s_tb, done(NT - 1))
            ch(v.tensor_copy(TB3[:, :, BF:BF + 1].rearrange("p i a -> p (i a)"), dinv))
            v.sem_inc(s_dv, 1)
            ch(v.tensor_scalar(has, edges, 1.0, None, ALU.min))
            ch(v.tensor_scalar(nohas, has, 1.0, BIG, ALU.subtract, ALU.mult))
            ch(v.tensor_scalar(posf, ends, 1.0, 0.0, ALU.subtract, ALU.max))
            ch(v.tensor_copy(pos[:, :], posf))
            v.wait_ge(s_w, 16 * 20)
            for k in range(KD):
                v.tensor_scalar(wc[:, k, CW:CW + 3 * HID], wc[:, k, CW:CW + 3 * HID], gpre[:, k:k + 1], None, ALU.mult).then_inc(s_mask, 1)
            v.wait_ge(s_bnT, 1)
            for l in range(2):
                ch(v.tensor_copy(bnT[:, l, :], bank[4][:, l * P:l * P + 5 * EX * KD]))
            bp = [bnT[:, :, n * EX * KD:(n + 1) * EX * KD] for n in range(5)]
            ch(v.tensor_scalar(bp[4], bp[4], BN_EPS, None, ALU.add))
            v.tensor_copy(bns[:, :, :], bp[4]).then_inc(s_bnv, 1)
            v.wait_ge(s_bnq, 1)
            ch(v.reciprocal(bns[:, :, :], bnt[:, :, :]))
            inv_root(bns[:, :, :], bp[4], bnt[:, :, :])
            ch(v.tensor_tensor(bns[:, :, :], bns[:, :, :], bp[1], ALU.mult))
            ch(v.tensor_tensor(bnb[:, :, :], bp[0], bp[3], ALU.subtract))
            ch(v.tensor_tensor(bnb[:, :, :], bnb[:, :, :], bns[:, :, :], ALU.mult))
            ch(v.tensor_tensor(bnb[:, :, :], bnb[:, :, :], bp[2], ALU.add))
            v.wait_ge(s_Bw, 1)
            ch(v.tensor_copy(runw[:, :], bank[0][:, 0:P]))
            ch(v.tensor_scalar(runn[:, :], runw[:, :], 1.0, BIG, ALU.subtract, ALU.mult))
            ch(v.memset(carT[:, :, 0:1], 0.0))
            ch(v.memset(fix[:, :], 0.0))
            v.wait_ge(s_en, 16)
            ch(v.tensor_scalar(col[:, 4:5], node[:, 0:1], float(T), float(T), ALU.mult, ALU.add))
            ch(v.tensor_tensor(col[:, 4:5], col[:, 3:4], col[:, 4:5], ALU.is_le))
            ch(v.tensor_tensor(col[:, 4:5], col[:, 4:5], col[:, 0:1], ALU.mult))
            ch(v.scalar_tensor_tensor(out=col[:, 5:6], in0=col[:, 3:4], scalar=-1.0, in1=col[:, 4:5], op0=ALU.add, op1=ALU.mult))
            ch(v.tensor_scalar(col[:, 6:7], col[:, 4:5], -FAR, FAR, ALU.mult, ALU.add))
            ch(v.tensor_tensor(col[:, 5:6], col[:, 5:6], col[:, 6:7], ALU.add))
            v.tensor_copy(fidx[:, :], col[:, 5:6]).then_inc(s_fz, 1)
            ch(v.memset(M[:, :], -BIG))
            ch(v.memset(blockm[:, :], 0.0))
            for h in range(AH):
                ch(v.memset(blockm[h * AD:(h + 1) * AD, h * AD:(h + 1) * AD], float(AD) ** -0.5))
            ch(v.memset(vs[:, :, HID:HID + 1], 1.0))
            ch(v.memset(mT[:, 2 * P:2 * P + 1], 1.0))

            v.memset(stm[:, U - 1, :], 0.0).then_inc(s_max, U)
            v.memset(sts[:, U - 1, :], 0.0).then_inc(s_sum, U)

            def window(w, hook):
                for u in range(U):
                    pv = (u - 1) % U
                    if u % HW == 0:
                        v.wait_ge(s_out[u // HW], w * 32 + 32)
                    v.wait_ge(s_prod, w * U + u + 1)
                    v.wait_ge(s_max, w * U + U + u)
                    v.scalar_tensor_tensor(out=stm[:, u, :], in0=stm[:, pv, :], scalar=neg[:, bass.ds(w * U + u, 1)],
                                           in1=ring[:, u, 0:BF], op0=ALU.add, op1=ALU.max).then_inc(s_max, 1)
                    v.wait_ge(s_sum, w * U + U + u)
                    v.scalar_tensor_tensor(out=sts[:, u, :].rearrange("p (a b) -> p a b", a=2),
                                           in0=sts[:, pv, :].rearrange("p (a b) -> p a b", a=2),
                                           scalar=con[:, bass.ds(w * U + u, 1)],
                                           in1=ring[:, u, :].rearrange("p (a b) -> p a b", a=2)[:, :, 0:BF],
                                           op0=ALU.mult, op1=ALU.add).then_inc(s_sum, 1)
                    if hook:
                        hook(u)

            def pass_b(n, h, s, last=False):
                R = LAST if last else P
                if s == 2:
                    v.wait_ge(s_pu, done(n))
                    ch(v.scalar_tensor_tensor(out=M[0:R, :], in0=bank[1 + h][0:R, CW:CW + HID], scalar=rn[0:R, bass.ds(n, 1)],
                                              in1=M[0:R, :], op0=ALU.mult, op1=ALU.max))
                if s == 4:
                    v.tensor_tensor(CB3[:, bass.ds(n, 1), :].rearrange("p a f -> p (a f)"), bank[1 + h][:, 0:CW], b_comb[:, :],
                                    ALU.add).then_inc(s_kb, 2 if last else 1)

            v.wait_ge(s_wide, 16 * 8)
            with v.Fori(0, PAIRS) as i:
                ch.enter(i, 2)
                window(i, lambda u: pass_b(i * 2 + u // HW, u // HW, u % HW))
                ch.leave(PAIRS)
            window(PAIRS, lambda u: pass_b(NT - 1, 0, u, True) if u < HW else None)
            v.sem_inc(s_Mw, 1)
            v.wait_ge(s_MT, 1)
            ch(v.tensor_reduce(col[:, 9:10], bank[7][:, 384:512], AX.X, ALU.max))
            ch(v.tensor_reduce(col[:, 10:11], mk[:, 0, :], AX.X, ALU.max))
            ch(v.tensor_tensor(col[:, 9:10], col[:, 9:10], col[:, 10:11], ALU.max))
            v.tensor_scalar(col[:, 8:9], col[:, 9:10], -1.0, None, ALU.mult).then_inc(s_em, 1)
            v.tensor_scalar(diag[:, :], ident[:, :], col[:, 9:10], None, ALU.mult).then_inc(s_dg, 1)
            v.wait_ge(s_Mb, 1)
            ch(v.tensor_copy(Mb[:, :], bank[7][:, 256:384]))
            v.sem_inc(s_mem, 1)
            v.wait_ge(s_kb, done(NT))
            sym = CB3.rearrange("p i (h k) -> p i h k", h=HEADS)
            for h in range(HEADS):
                ch(v.tensor_tensor(sym[:, :, h, 0:BASES], sym[:, :, h, 0:BASES], bcast(dinv.unsqueeze(2), [P, NT, BASES]), ALU.mult))

            def pass_c(n, h, s, last=False):
                R = LAST if last else P
                if s == 0:
                    v.wait_ge(s_pu, done(n + UNITS))
                    v.wait_ge(s_ek, free(n))
                    v.scalar_tensor_tensor(out=kt[0:R, h, :], in0=bank[1 + h][0:R, 0:HID], scalar=rn[0:R, bass.ds(n, 1)], in1=Mb[0:R, :],
                                           op0=ALU.mult, op1=ALU.subtract).then_inc(s_kt, 2 if last else 1)

            with v.Fori(0, PAIRS) as i:
                window(i + PASS, lambda u: pass_c(i * 2 + u // HW, u // HW, u % HW))
            window(PASS + PAIRS, lambda u: pass_c(NT - 1, 0, u, True) if u < HW else None)
            v.wait_ge(s_cx, done(NT))
            ch(v.reciprocal(col[:, 11:12], bank[3][:, HID:HID + 1]))
            v.scalar_tensor_tensor(out=diag[:, :], in0=bank[3][:, 0:HID], scalar=col[:, 11:12], in1=blockm[:, :],
                                   op0=ALU.mult, op1=ALU.mult).then_inc(s_cbd, 1)

            v.wait_ge(s_m2, 1)
            v.scalar_tensor_tensor(out=m2[:, :], in0=b_out, scalar=1.0 / AH, in1=bank[7][:, 0:D], op0=ALU.mult, op1=ALU.add).then_inc(s_m2c, 1)
            v.sem_inc(s_mo, 1)
            ch(v.tensor_scalar(g_out, g_out, float(D) ** 0.5, None, ALU.mult))

            def pass_d(i, u, m=2):
                b3 = [P, AH, AD]
                if u < m:
                    q3 = bank[1 + u][:, 0:HID].rearrange("p (h d) -> p h d", h=AH)
                    if u == 0:
                        v.wait_ge(s_pu, i * 2 + (2 * UNITS + 2 + RING2))
                    ch(v.tensor_reduce(small[:, u, 0:AH], q3, AX.X, ALU.max))
                    t = v.tensor_tensor(qd[:, u, :].rearrange("p (h d) -> p h d", h=AH), q3, bcast(small[:, u, 0:AH].unsqueeze(2), b3),
                                        ALU.subtract)
                    if u == m - 1:
                        t.then_inc(s_qd, 1)
                if u == 7:
                    e3 = eq[:, 0:m, :].rearrange("p b (h d) -> p (b h) d", h=AH)
                    v.wait_ge(s_eq, i + 1)
                    ch(v.tensor_reduce(esum[:, 0:m * AH], e3, AX.X, ALU.add))
                    ch(v.reciprocal(esum[:, 2 * AH:(2 + m) * AH], esum[:, 0:m * AH]))
                    v.tensor_tensor(qn[:, 0:m, :].rearrange("p b (h d) -> p (b h) d", h=AH), e3,
                                    bcast(esum[:, 2 * AH:(2 + m) * AH].unsqueeze(2), [P, m * AH, AD]), ALU.mult).then_inc(s_qn, 1)

            def pass_d_out(i, u, m=2):
                if u == 2:
                    v.wait_ge(s_nr, i + 1)
                    ch(v.tensor_scalar(nrm[:, 4:4 + m], nrm[:, 2:2 + m], 1e-12, None, ALU.max))
                    ch(v.reciprocal(nrm[:, 6:6 + m], nrm[:, 4:4 + m]))
                if 2 <= u < 2 + m:
                    h = u - 2
                    x1 = X3[:, bass.ds(i * 2 + h, 1), :].rearrange("p a f -> p (a f)")
                    ch(v.scalar_tensor_tensor(out=mo[:, h, :], in0=bank[5 + h][:, 0:D], scalar=nrm[:, 6 + h:7 + h], in1=g_out,
                                              op0=ALU.mult, op1=ALU.mult))
                    t = v.tensor_tensor(x1, x1, mo[:, h, :], ALU.add)
                    if h == m - 1:
                        t.then_inc(s_mo, 1)

            window(2 * PASS, lambda u: pass_d(0, u))
            with v.Fori(1, PAIRS) as i:
                ch.enter(i - 1, 8)
                window(i + 2 * PASS, lambda u: (pass_d(i, u), pass_d_out(i - 1, u)))
                ch.leave(PAIRS - 1)
            window(2 * PASS + PAIRS, lambda u: (pass_d(PAIRS, u, 1), pass_d_out(PAIRS - 1, u)))
            window(3 * PASS, lambda u: pass_d_out(PAIRS, u, 1))
            with v.Fori(3 * PASS + 1, WIN) as w:
                window(w, None)

            v.wait_ge(s_tl, 1)
            for n in range(AGGS):
                v.tensor_tensor_scan(carT[:, n, 1:P + 1], (runn if n == 0 else runw)[:, :], bank[4][:, n * P:(n + 1) * P], 0.0,
                                     ALU.add if n == 0 else ALU.mult, ALU.max if n == 0 else ALU.add).then_inc(s_car, 1)
            v.wait_ge(s_carT, 1)
            v.wait_ge(s_fixg, 32)
            for n in range(AGGS):
                v.tensor_tensor(fix[:, n * BF:(n + 1) * BF], fix[:, n * BF:(n + 1) * BF], bank[5][:, n * P:(n + 1) * P],
                                ALU.max if n == 0 else ALU.add).then_inc(s_fix, 1)

            def combine(n, j, b, i7):
                g = got[:, j, :]
                own = TB3[:, bass.ds(n, 1), 0:BF].rearrange("p a f -> p (a f)")
                v.wait_ge(s_gf[j], i7 * 32 + 32)
                v.scalar_tensor_tensor(out=g[:, 0:BF], in0=g[:, 0:BF], scalar=nohas[:, bass.ds(n, 1)], in1=own,
                                       op0=ALU.add, op1=ALU.max).then_inc(s_dve, 1)
                v.scalar_tensor_tensor(out=g[:, BF:2 * BF], in0=g[:, BF:2 * BF], scalar=has[:, bass.ds(n, 1)], in1=own,
                                       op0=ALU.mult, op1=ALU.add).then_inc(s_dve, 1)
                v.tensor_scalar(g[:, 2 * BF:3 * BF], g[:, 2 * BF:3 * BF], has[:, bass.ds(n, 1)], None, ALU.mult).then_inc(s_dve, 1)
                ch.n += 3
                v.wait_ge(s_dve, ch.base + ch.n)
                ch(v.scalar_tensor_tensor(out=g[:, 2 * BF:3 * BF], in0=own, scalar=dinv[:, bass.ds(n, 1)], in1=g[:, 2 * BF:3 * BF],
                                          op0=ALU.mult, op1=ALU.add))
                v.wait_ge(s_ph, free(n))
                c = CB3[:, bass.ds(n, 1), :].rearrange("p a (h k) -> p k (a h)", h=HEADS)
                for k0, at in ((BASES, 1), (2 * BASES, 0), (0, 2)):
                    m = v.tensor_tensor(prod[:, b, k0:k0 + BASES, :].rearrange("p k (h f) -> p k h f", h=HEADS),
                                        bcast(c[:, k0:k0 + BASES, :].unsqueeze(3), [P, BASES, HEADS, F]),
                                        bcast(g[:, at * BF:(at + 1) * BF].rearrange("p (k f) -> p k f", k=BASES).unsqueeze(2), [P, BASES, HEADS, F]),
                                        ALU.mult)
                    if k0 == 2 * BASES:
                        ch.mark(m)
                v.wait_ge(s_dve, ch.base + ch.n)
                v.tensor_tensor(prod[:, b, BASES:BASES + PRE, :], prod[:, b, BASES:BASES + PRE, :], prod[:, b, 2 * BASES:2 * BASES + PRE, :],
                                ALU.add).then_inc(s_pr, 1)

            full = NT // (2 * GR)
            with v.Fori(0, full) as i:
                ch.enter(i, 5 * 2 * GR)
                for j in range(2 * GR):
                    combine(i * (2 * GR) + j, j % GR, j % 2, i * 2 + j // GR)
                ch.leave(full)
            for n in range(full * 2 * GR, NT):
                combine(n, n % GR, n % 2, n // GR)

            v.wait_ge(s_sm, 1)
            ch(v.scalar_tensor_tensor(out=gnc[:, :], in0=bank[3][:, 0:D], scalar=1.0 / N, in1=conv_b, op0=ALU.mult, op1=ALU.add))
            ch(v.tensor_tensor(gnc[:, :], gnc[:, :], gn_s, ALU.mult))
            ch(v.tensor_tensor(gnc[:, :], conv_b, gnc[:, :], ALU.subtract))

            def center(n):
                h = H3[:, bass.ds(n, 1), :].rearrange("p a f -> p (a f)")
                v.tensor_tensor(h, h, gnc[:, :], ALU.add).then_inc(s_hc, 1)

            with v.Fori(0, PAIRS) as i:
                for b in range(2):
                    center(i * 2 + b)
            center(NT - 1)
            v.wait_ge(s_vr, NT + SQ)
            v.wait_ge(s_hc, NT)
            v.tensor_scalar(gnc[:, :], bank[4][:, 0:D], 1.0 / N, GN_EPS, ALU.mult, ALU.add).then_inc(s_gq, 1)
            v.wait_ge(s_gr, 1)
            ch(v.reciprocal(gnA[:, :], gnt[:, :]))
            inv_root(gnA[:, :], gnc[:, :], gnt[:, :])
            ch(v.tensor_tensor(gnA[:, :], gnA[:, :], gn_w, ALU.mult))

            GB = 4

            def block_out_tiles(n0, count):
                def h_x(j):
                    return [t[:, bass.ds(n0 + j, 1), :].rearrange("p a f -> p (a f)") for t in (H3, X3)]
                for j in range(count):
                    h, _ = h_x(j)
                    ch.mark(v.tensor_tensor(h, h, gnA[:, :], ALU.mult))
                for j in range(count):
                    h, _ = h_x(j)
                    v.wait_ge(s_dve, ch.base + ch.n - count + 1)
                    ch.mark(v.tensor_tensor(h, h, gn_b, ALU.add))
                for j in range(count):
                    h, x1 = h_x(j)
                    v.wait_ge(s_dve, ch.base + ch.n - (count - 1 - j))
                    v.scalar_tensor_tensor(out=x1, in0=h, scalar=0.0, in1=x1, op0=ALU.max, op1=ALU.add).then_inc(s_bo, 1)


            def front(G, step, gb, w=GN, tiles_ready=None):
                ng = w // P
                y, t = ln[:, 2, 0:ng], ln[:, 3, 0:ng]
                if step == (1, 2):
                    v.wait_ge(s_bo, NT if tiles_ready is None else tiles_ready)
                if step[0] == 1 and 2 <= step[1] < 2 + ng:
                    n = step[1] - 2
                    ch.mark(v.bn_stats(bn6[:, n, :], X3[:, bass.ds(G * GT + n, 1), :].rearrange("p a f -> p (a f)")))
                if step == (2, 0):
                    v.wait_ge(s_dve, ch.base + ch.n)
                    v.sem_inc(s_step, 1)
                    for n in range(ng):
                        ch.mark(v.bn_aggr(mv[:, n, :], bn6[:, n, :]))
                if step == (2, 1):
                    v.wait_ge(s_dve, ch.base + ch.n)
                    v.tensor_scalar(ln[:, 0, 0:ng], mv[:, 0:ng, 1:2].rearrange("p s a -> p (s a)"), LN_EPS, None, ALU.add).then_inc(s_f1, 1)
                if step == (3, 0):
                    v.wait_ge(s_f2, G + 1)
                    ch.mark(v.tensor_tensor(t, y, y, ALU.mult))
                if step == (3, 1):
                    v.wait_ge(s_dve, ch.base + ch.n)
                    ch.mark(v.tensor_tensor(t, t, ln[:, 0, 0:ng], ALU.mult))
                if step == (3, 2):
                    v.wait_ge(s_dve, ch.base + ch.n)
                    ch.mark(v.tensor_scalar(t, t, -0.5, 1.5, ALU.mult, ALU.add))
                if step == (3, 3):
                    v.wait_ge(s_dve, ch.base + ch.n)
                    ch.mark(v.tensor_tensor(y, y, t, ALU.mult))
                if step == (4, 0):
                    v.wait_ge(s_dve, ch.base + ch.n)
                    ch.mark(v.scalar_tensor_tensor(out=ln[:, 4, 0:ng], in0=mv[:, 0:ng, 0:1].rearrange("p s a -> p (s a)"), scalar=-1.0,
                                                   in1=y, op0=ALU.mult, op1=ALU.mult))
                if step == (4, 1):
                    v.wait_ge(s_dve, ch.base + ch.n)
                    for n in range(ng):
                        m = v.tensor_scalar(xf[:, n, :], X3[:, bass.ds(G * GT + n, 1), :].rearrange("p a f -> p (a f)"), ln[:, 2, n:n + 1], ln[:, 4, n:n + 1],
                                            ALU.mult, ALU.add)
                    m.then_inc(s_f3, 1)
                if step == (5, 3):
                    v.wait_ge(s_f5, G + 1)
                    v.tensor_tensor(xg[:, gb, 1, 0:KD * w], bank[6][:, 0:KD * w], as_f32(xg[:, gb, 0, 0:KD * w]), ALU.subtract).then_inc(s_f6, 1)

            def softmax(g, step, gb, ng):
                b3 = [P, ng, EX]
                if step == (0, 0):
                    v.wait_ge(s_lg, g + 1)
                    ch.mark(v.tensor_tensor(lg[:, 0:ng, :], bank[7][:, 0:ng * EX].rearrange("p (s e) -> p s e", s=ng),
                                            bcast(b_r[:, :].unsqueeze(1), b3), ALU.add))
                if step == (0, 1):
                    v.wait_ge(s_dve, ch.base + ch.n)
                    ch(v.tensor_reduce(rsm[:, 0, 0:ng], lg[:, 0:ng, :], AX.X, ALU.max))
                    v.tensor_tensor(lg[:, 0:ng, :], lg[:, 0:ng, :], bcast(rsm[:, 0, 0:ng].unsqueeze(2), b3), ALU.subtract).then_inc(s_lm, 1)
                if step == (1, 0):
                    v.wait_ge(s_le, g + 1)
                    ch(v.tensor_reduce(rsm[:, 1, 0:ng], lg[:, 0:ng, :], AX.X, ALU.add))
                    ch.mark(v.reciprocal(rsm[:, 0, 0:ng], rsm[:, 1, 0:ng]))
                if step == (1, 1):
                    v.wait_ge(s_dve, ch.base + ch.n)
                    v.tensor_tensor(wsm[:, gb, 0:ng, :], lg[:, 0:ng, :], bcast(rsm[:, 0, 0:ng].unsqueeze(2), b3), ALU.mult).then_inc(s_ws, 1)

            def split(l, g, e, w):
                v.wait_ge((s_h1, s_h2)[l], g * (2 * EX) + (2 * e + 2 + KD))
                v.tensor_copy(hid[l][:, e % 2, 0, 0:KD * w], hf[:, l, 0:KD * w]).then_inc(s_up[l], 1)
                v.wait_ge(s_up[l], g * EX + (e + 1))
                v.tensor_tensor(hid[l][:, e % 2, 1, 0:KD * w], hf[:, l, 0:KD * w], as_f32(hid[l][:, e % 2, 0, 0:KD * w]),
                                ALU.subtract).then_inc(s_lo[l], 1)

            def add_tile(g, gb, e, s, ng):
                if s >= ng:
                    return
                r = g * (ROUNDS * GT) + (e * GT + s)
                inc = 1 if ng == GT else GT
                v.wait_ge(s_L3, r + inc + L3_START)
                out, ps = acc[:, gb, s, :], bank[4 + s][:, 0:D]
                v.wait_ge(s_acc, r + 1)
                if e == 0:
                    x1 = X3[:, bass.ds(g * GT + s, 1), :].rearrange("p a f -> p (a f)")
                    v.scalar_tensor_tensor(out=out, in0=ps, scalar=wsm[:, gb, s, 0:1], in1=x1, op0=ALU.mult, op1=ALU.add).then_inc(s_acc, inc)
                elif e < EX:
                    v.scalar_tensor_tensor(out=out, in0=ps, scalar=wsm[:, gb, s, e:e + 1], in1=out, op0=ALU.mult, op1=ALU.add).then_inc(s_acc, inc)
                else:
                    v.tensor_tensor(out, out, ps, ALU.add).then_inc(s_acc, inc)

            def group(g, gb, w, w_before, w_next, prev_stores):
                ng = w // P
                for e in range(EX):
                    def between(place):
                        softmax(g, (e, place), gb, ng)
                        if w_next:
                            front(g + 1, (e, place), 1 - gb, w_next)
                    if e + 1 < EX:
                        split(0, g, e + 1, w)
                    elif w_next:
                        split(0, g + 1, 0, w_next)
                    between(0)
                    if e == 1 and w_before:
                        for s in range(GT):
                            add_tile(g - 1, 1 - gb, EX, s, w_before // P)
                    split(1, g, e, w)
                    between(1)
                    if e == 1:
                        v.wait_ge(s_ws, g + 1)
                        v.wait_ge(s_y[gb], prev_stores + 16)
                    for s in range(GT):
                        if e > 0:
                            add_tile(g, gb, e - 1, s, ng)
                        elif w_before:
                            add_tile(g - 1, 1 - gb, EX - 1, s, w_before // P)
                        between(2 + s)

            block_out_tiles(0, GB)
            for e in range(EX):
                for place in range(4):
                    front(0, (e, place), 0, tiles_ready=GB)
                if e in (2, 4):
                    block_out_tiles(GB * e // 2, GB)
            with v.Fori(3, NT // GB) as i:
                ch.enter(i - 3, 2 * GB)
                block_out_tiles(i * GB, GB)
                ch.leave(NT // GB - 3)
            block_out_tiles(NT - 1, 1)
            split(0, 0, 0, GN)
            group(0, 0, GN, 0, GN, 0)
            with v.Fori(0, GROUPS // 2 - 1) as i:
                ch.enter(i, 2 * (4 + 2 * GT + 5))
                group(i * 2 + 1, 1, GN, GN, GN, i * 16)
                group(i * 2 + 2, 0, GN, GN, GN, i * 16 + 16)
                ch.leave(GROUPS // 2 - 1)
            group(GROUPS - 1, 1, GN, GN, P, 16 * (GROUPS // 2 - 1))
            group(GROUPS, 0, P, GN, 0, 16 * (GROUPS // 2))
            for e in (EX - 1, EX):
                add_tile(GROUPS, 0, e, 0, 1)


_INS = ["x", "src", "dst", "L0_gnn_W_bases", "L0_gnn_W_comb", "L0_gnn_b_comb", "L0_gnn_conv_bias", "L0_gnn_gn_weight",
        "L0_gnn_gn_bias", "L0_gnn_gn_mean_scale", "L0_mix_w_qkv", "L0_mix_mem_kv", "L0_mix_w_out", "L0_mix_b_out",
        "L0_mix_g_out", "L0_mix_g_pre", "L0_ffn_Wr", "L0_ffn_br"] + [
        f"L0_ffn_{n}{l}" for l in (1, 2) for n in ("W", "b", "g", "be", "m", "v")] + ["L0_ffn_Wo", "L0_ffn_bo"]


def kernel(**inputs):
    import numpy as _np
    import concourse.bacc as _bacc
    from concourse import mybir as _mybir
    from concourse.bass_utils import run_bass_kernel_spmd as _run

    nc = _bacc.Bacc("TRN2", target_bir_lowering=False, num_devices=1)
    arrays, aps = {}, {}
    for name in _INS:
        arr = _np.ascontiguousarray(inputs[name])
        arrays[f"in_{name}"] = arr
        aps[name] = nc.dram_tensor(f"in_{name}", arr.shape, _mybir.dt.from_np(arr.dtype), kind="ExternalInput").ap()
    out = nc.dram_tensor("out_y", (N, D), F32, kind="ExternalOutput").ap()
    scratch = {
        "tbl": nc.dram_tensor("scratch_table", (NT * P, RW), F32, kind="Internal").ap(),
        "xtd": nc.dram_tensor("scratch_xt", (NT * P, D), F32, kind="Internal").ap(),
        "maxes": nc.dram_tensor("scratch_maxes", (P * T, BF), F32, kind="Internal").ap(),
        "sums": nc.dram_tensor("scratch_sums", (P * T, 2 * BF), F32, kind="Internal").ap(),
        "ends": nc.dram_tensor("scratch_ends", (NT * P + 1, 1), F32, kind="Internal").ap(),
    }
    program(nc, aps, out, scratch)
    r = _run(nc, [arrays], core_ids=[0])
    return r.results[0]["out_y"]
```

```python
from contextlib import ExitStack

import concourse.bass as bass
from concourse import mybir

F32 = mybir.dt.float32
I32 = mybir.dt.int32
F32R = mybir.dt.float32r
ALU = mybir.AluOpType
ACT = mybir.ActivationFunctionType
AX = mybir.AxisListType

N = 6250
E = 200000
D = 256
P = 128
KD = D // P
NT = -(-N // P)
LAST = N - (NT - 1) * P
HEADS, BASES, AGGS = 8, 4, 3
F = D // HEADS
BF = BASES * F
KC = BASES * AGGS
CW = HEADS * KC
AH, AD, MEM = 4, 32, 4
HID = AH * AD
EX = 8
LN_EPS, GN_EPS, BN_EPS = 1e-5, 1e-5, 1e-3
BIG = 3.0e38
FAR = 1.0e9

U = 16
HW = U // 2
WIN = -(-E // (P * U))
T = WIN * U
RW = BF + 4
ST = AGGS * BF
FULL = E // T
REST = E - FULL * T

LB = 125
NB = E // LB
LP = 100
LC = NB // LP

XS = 4
CPARTS = 6
CPER = NT // CPARTS // 2 * 2

PAIRS = NT // 2
PASS = PAIRS + 1
UNITS = 2 * PASS

VCH = 12
CH = 4
NCH = NT // CH
BO_START = 4

GT = 2
GN = GT * P
GROUPS = NT // GT
ROUNDS = EX + 1

L_START = 4
L3_START = 3 * GT
ACC_START = 2 * GT

RING2 = 2


def done(n):
    return n + 1 + RING2


def free(n):
    return n + 1


class Chain:

    def __init__(self, eng, sem):
        self.eng, self.sem, self.base, self.n = eng, sem, 0, 0

    def __call__(self, ins):
        ins.then_inc(self.sem, 1)
        self.n += 1
        self.eng.wait_ge(self.sem, self.base + self.n)

    def mark(self, ins):
        ins.then_inc(self.sem, 1)
        self.n += 1

    def enter(self, i, per):
        self.start, self.per = self.base + self.n, per
        self.base, self.n = self.start + i * per, 0

    def leave(self, times):
        assert self.n == self.per, (self.n, self.per)
        self.base, self.n = self.start + times * self.per, 0


def as_f32(ap):
    return ap.bitcast(F32)


def bcast(ap, shape):
    return ap.broadcast_to(shape)


def program(nc, a, y, scratch):
    ctx = ExitStack()
    with ctx:
        def sb(name, shape, dt=F32):
            return ctx.enter_context(nc.sbuf_tensor(name, shape, dt))

        def sem(name):
            return ctx.enter_context(nc.semaphore(name))

        X = sb("X", [P, NT * D])
        X3 = X[:, :].rearrange("p (i d) -> p i d", d=D)
        sizes = {"R1": NT * D, "TB": NT * RW, "CB": NT * CW, "AUX": 3 * EX * KD * D}
        with ExitStack() as first_use:
            R1, TB, CB, AUX = [first_use.enter_context(nc.sbuf_tensor(n, [P, w], F32)) for n, w in sizes.items()]
        R1H, TBH, CBH, AUXH = [ctx.enter_context(nc.sbuf_tensor(n + "_rounded", [P, w], F32R)) for n, w in sizes.items()]
        HT = R1[:, :].rearrange("p (i k m) -> p i k m", k=KD, m=P)
        blk = R1[:, 0:NT * LB].bitcast(I32).rearrange("p (i j) -> p i j", j=LB)
        OH = -(-NT * LB // 64) * 64
        below = R1[:, OH:OH + NT * LB].rearrange("p (i j) -> p i j", j=LB)
        oh_lo = R1[0:LP, OH:OH + LC * P].rearrange("p (c m) -> p c m", m=P)
        oh_hi = R1[0:LP, OH + LC * P:OH + LC * (P + NT)].rearrange("p (c m) -> p c m", m=NT)
        o = OH + NT * LB
        upto = R1[:, o:o + P]
        iota = R1[:, o + P:o + 2 * P].bitcast(I32)
        assert o + 2 * P <= NT * D
        GS = 2 * RW
        ring = R1[:, 0:U * GS].rearrange("p (u f) -> p u f", f=GS)
        stm = R1[:, U * GS:U * (GS + BF)].rearrange("p (u f) -> p u f", f=BF)
        sts = R1[:, U * (GS + BF):U * (GS + ST)].rearrange("p (u f) -> p u f", f=2 * BF)
        TB3 = TB[:, :].rearrange("p (i f) -> p i f", f=RW)
        bn_x = CB[:, 0:NT * 6].rearrange("p (i f) -> p i f", f=6)
        endsT, startsT = [CB[0:NT, NT * 6 + n * P:NT * 6 + (n + 1) * P] for n in range(2)]
        CB3 = CB[:, :].rearrange("p (i f) -> p i f", f=CW)
        idx_all = AUX[:, 0:T + U].bitcast(I32)
        dst_all = AUX[:, T + U:T + U + T + 2].bitcast(I32)
        o = 2 * T + U + 2
        con = AUX[:, o:o + T]
        neg = AUX[:, o + T:o + 2 * T]
        o += 2 * T
        xs = AUX[:, o:o + XS * D].rearrange("p (b f) -> p b f", b=XS)
        o += (XS - 2) * D
        xt = AUX[:, o + 512:o + 1536].rearrange("p (b k n) -> p b k n", b=XS, k=KD)
        xl = AUX[:, o + 1024:o + 1536].rearrange("p (b k n) -> p b k n", b=2, k=KD)
        kt = AUX[:, o + 1536:o + 1792].rearrange("p (b n) -> p b n", b=2)
        ek = AUX[:, o + 1792:o + 2048].rearrange("p (b n) -> p b n", b=2)
        vs = AUX[:, o + 2048:o + 2048 + 2 * (HID + 1)].rearrange("p (b n) -> p b n", b=2)
        o += 2048 + 2 * (HID + 1) + 2
        qd = AUX[:, o:o + 256].rearrange("p (b n) -> p b n", b=2)
        eq = AUX[:, o + 256:o + 512].rearrange("p (b n) -> p b n", b=2)
        qn = AUX[:, o + 512:o + 768].rearrange("p (b n) -> p b n", b=2)
        qT = AUX[:, o + 768:o + 1024].rearrange("p (b n) -> p b n", b=2)
        mo = AUX[:, o + 1024:o + 1536].rearrange("p (b n) -> p b n", b=2)
        carT = AUX[:, o + 1536:o + 1536 + 3 * (P + 1)].rearrange("p (a n) -> p a n", a=3)
        o += 1536 + 3 * (P + 1) + 1
        wb = AUX[:, o:o + KD * BF].rearrange("p (k n) -> p k n", k=KD)
        o += KD * BF
        wc = AUX[:, o:o + KD * (CW + 3 * HID)].rearrange("p (k n) -> p k n", k=KD)
        o += KD * (CW + 3 * HID)
        assert o <= 3 * EX * KD * D
        o = U * (GS + ST)
        M, Mb, blockm, runw, runn = [R1[:, o + n * P:o + (n + 1) * P] for n in range(5)]
        m2, b_out, g_out = [R1[:, o + 5 * P + n * D:o + 5 * P + (n + 1) * D] for n in range(3)]
        fix = R1[:, o + 5 * P + 3 * D:o + 5 * P + 3 * D + ST]
        assert o + 5 * P + 3 * D + ST <= NT * D
        PRE = 1
        GR = 7
        got = AUX[:, 0:GR * ST].rearrange("p (u f) -> p u f", f=ST)
        prod = AUX[:, GR * ST:GR * ST + 2 * KC * D].rearrange("p (b k n) -> p b k n", b=2, k=KC)
        assert GR * ST + 2 * KC * D <= 3 * EX * KD * D
        EWN = EX * KD * D
        EW = [AUX[:, n * EWN:(n + 1) * EWN] for n in range(3)]
        EWH, EWL = [[t[:, n * EWN:(n + 1) * EWN] for n in range(3)] for t in (R1H, AUXH)]
        EWP = [[t.rearrange("p (e k n) -> p e k n", e=EX, k=KD) for t in (EWH[n], EWL[n])] for n in range(3)]
        HB = 2 * 2 * KD * GN
        hid = [TBH[:, l * HB:(l + 1) * HB].rearrange("p (b q f) -> p b q f", b=2, q=2) for l in range(2)]
        hf = TB[:, 2 * HB:2 * HB + 2 * KD * GN].rearrange("p (l f) -> p l f", l=2)
        o = 2 * HB + 2 * KD * GN
        acc = TB[:, o:o + 2 * GT * D].rearrange("p (b s n) -> p b s n", b=2, s=GT)
        assert o + 2 * GT * D <= NT * RW
        xg = CBH[:, 0:HB].rearrange("p (b q f) -> p b q f", b=2, q=2)
        xf = CB[:, HB:HB + 2 * D].rearrange("p (b n) -> p b n", b=2)
        o = HB + 2 * D
        wT = CB[0:EX, o:o + GN]
        assert o + GN <= NT * CW
        junk = TB[:, 0:4 * VCH * P].rearrange("p (b i m) -> p b i m", b=4, m=P)
        hr = TB[:, 0:2 * KD * CH * P].rearrange("p (b k n) -> p b k n", b=2, k=KD)

        wo = sb("wo", [P, D])
        ident = sb("ident", [P, P])
        ones = sb("ones", [P, P])
        node = sb("node", [P, NT], I32)
        lk = sb("lk", [LP, LC], I32)
        lo = sb("lo", [LP, LC], I32)
        hi = sb("hi", [LP, LC], I32)
        tabs = sb("tabs", [P, 24, NT])
        (hist, tot, incl, bf, cnt, ends, starts, edges, deg, dinv, has, nohas, mean, var, rstd,
         nmr, rn, opr, ta, tb_, tc, posf, one_nt, tnorm) = [tabs[:, n, :] for n in range(24)]
        bidx = sb("bidx", [P, NT], I32)
        pos = sb("pos", [P, NT], I32)
        bn6 = sb("bn6", [P, 2, 6])
        mv = sb("mv", [P, 2, 2])
        nrm = sb("nrm", [P, 8])
        esum = sb("esum", [P, 4 * AH])
        iw = sb("iw", [P, U], I32)
        wr = sb("wr", [P, KD, EX])
        wrp = sb("wrp", [P, 2, KD, EX], F32R)
        bo = sb("bo", [EX, D])
        gpre = sb("gpre", [P, KD])
        gpar = sb("gpar", [P, 4, KD])
        conv_b, gn_w, gn_b, gn_s = [gpar[:, n, :] for n in range(4)]
        gst = sb("gst", [P, 8, KD])
        g_m, g_c, g_v, g_r, g_A, g_B, g_t = [gst[:, n, :] for n in range(7)]
        hsum = sb("hsum", [P, KD, NT])
        vsum = sb("vsum", [P, KD, NT // VCH + 1])
        b_comb = sb("b_comb", [P, CW])
        b_r = sb("b_r", [P, EX])
        bnp = sb("bnp", [5 * EX * KD, 2, P])
        bnT = sb("bnT", [P, 2, 5 * EX * KD])
        bns = sb("bns", [P, 2, EX * KD])
        bnb = sb("bnb", [P, 2, EX * KD])
        bnt = sb("bnt", [P, 2, EX * KD])
        diag = sb("diag", [P, P])
        mk = sb("mk", [P, 2, MEM])
        mkm = sb("mkm", [P, 8])
        mT = sb("mT", [MEM, 2 * P + 1])
        col = sb("col", [P, 24])
        nidx = sb("nidx", [P, 1], I32)
        fidx = sb("fidx", [P, 1], I32)
        small = sb("small", [P, 2, 32])
        lg = sb("lg", [P, GT, EX])
        wsm = sb("wsm", [P, 2, GT, EX])
        rsm = sb("rsm", [P, 2, GT])
        ln = sb("ln", [P, 6, GT])

        bank = [ctx.enter_context(nc.psum_tensor(f"bank{n}", [P, 512], F32)) for n in range(8)]

        tbl, xtd, Wd, e_d = scratch["tbl"], scratch["xtd"], (scratch["maxes"], scratch["sums"]), scratch["ends"]
        tbl_p = tbl.rearrange("(i p) f -> p i f", p=P)
        x_in = a["x"]
        W_run = [w.rearrange("(p t) f -> p (t f)", p=P) for w in Wd]
        src1, dst1 = a["src"], a["dst"]
        dst_blocks = dst1.rearrange("(k j) -> k j", j=LB)

        def row_of(v):
            return v.partition_broadcast(P)

        def sems(name, n):
            return [sem(f"{name}_{k}") for k in range(n)]

        XCH = 3
        padding_set = sem("padding_set")
        block_ends_loaded = sem("block_ends_loaded")
        x_loaded = sems("x_loaded", XCH + 1)
        runs_loaded = sem("runs_loaded")
        weights_loaded = sem("weights_loaded")
        rows_loaded = sem("rows_loaded")
        constants_made = sem("constants_made")
        gain_in_weights = sem("gain_in_weights")
        vector_steps = sem("vector_steps")
        scalar_steps = sem("scalar_steps")
        waits_carried = sem("waits_carried")
        histogram_fed = sem("histogram_fed")
        histogram_made = sem("histogram_made")
        prefixes_made = sem("prefixes_made")
        blocks_found = sem("blocks_found")
        blocks_gathered = sems("blocks_gathered", CPARTS)
        ends_made = sem("ends_made")
        ends_turned = sem("ends_turned")
        ends_stored = sem("ends_stored")
        starts_loaded = sem("starts_loaded")
        starts_turned = sem("starts_turned")
        root_wanted = sem("root_wanted")
        root_made = sem("root_made")
        table_made = sem("table_made")
        table_stored = sem("table_stored")
        tile_normalised = sem("tile_normalised")
        tile_turned = sem("tile_turned")
        turned_copied = sem("turned_copied")
        turned_stored = sems("turned_stored", XS)
        bases_made = sem("bases_made")
        bases_copied = sem("bases_copied")
        bn_turned = sem("bn_turned")
        bn_var_made = sem("bn_var_made")
        bn_root_made = sem("bn_root_made")
        indices_copied = sem("indices_copied")
        row_gathered = sems("row_gathered", U)
        row_weighted = sem("row_weighted")
        max_stepped = sem("max_stepped")
        sums_stepped = sem("sums_stepped")
        states_stored = sems("states_stored", 2)
        tile_loaded = sems("tile_loaded", 2)
        tile_projected = sem("tile_projected")
        comb_copied = sem("comb_copied")
        keys_shifted = sem("keys_shifted")
        keys_exp_made = sem("keys_exp_made")
        context_added = sem("context_added")
        key_max_made = sem("key_max_made")
        key_max_turned = sem("key_max_turned")
        key_max_diag_made = sem("key_max_diag_made")
        key_max_spread = sem("key_max_spread")
        memory_exp_made = sem("memory_exp_made")
        memory_turned = sem("memory_turned")
        memory_copied = sem("memory_copied")
        key_max_copied = sem("key_max_copied")
        context_made = sem("context_made")
        context_turned = sem("context_turned")
        context_copied = sem("context_copied")
        out_map_made = sem("out_map_made")
        out_map_biased = sem("out_map_biased")
        queries_shifted = sem("queries_shifted")
        queries_exp_made = sem("queries_exp_made")
        queries_normalised = sem("queries_normalised")
        queries_turned = sem("queries_turned")
        queries_copied = sem("queries_copied")
        mix_made = sem("mix_made")
        mix_added = sem("mix_added")
        mix_norm_made = sem("mix_norm_made")
        first_node_found = sem("first_node_found")
        first_end_gathered = sem("first_end_gathered")
        handed_diag_made = sem("handed_diag_made")
        handed_spread = sem("handed_spread")
        tails_turned = sem("tails_turned")
        carries_scanned = sem("carries_scanned")
        carries_turned = sem("carries_turned")
        fix_index_made = sem("fix_index_made")
        fix_rows_gathered = sem("fix_rows_gathered")
        fix_rows_made = sem("fix_rows_made")
        fix_rows_stored = sem("fix_rows_stored")
        last_states_gathered = sems("last_states_gathered", GR)
        products_made = sem("products_made")
        h_summed = sem("h_summed")
        h_copied = sem("h_copied")
        center_made = sem("center_made")
        squares_summed = sem("squares_summed")
        norm_var_made = sem("norm_var_made")
        norm_root_made = sem("norm_root_made")
        norm_factors_made = sem("norm_factors_made")
        chunk_normed = sem("chunk_normed")
        chunk_turned = sem("chunk_turned")
        branch_added = sem("branch_added")
        experts_loaded = sems("experts_loaded", 3)
        weights_upper_made = sem("weights_upper_made")
        weights_lower_made = sems("weights_lower_made", 3)
        front_var_made = sem("front_var_made")
        front_log_made = sem("front_log_made")
        front_root_made = sem("front_root_made")
        front_normalised = sem("front_normalised")
        front_turned = sem("front_turned")
        group_upper_made = sem("group_upper_made")
        group_lower_made = sem("group_lower_made")
        layer1_made = sem("layer1_made")
        layer2_made = sem("layer2_made")
        layer3_made = sem("layer3_made")
        layer1_copied = sem("layer1_copied")
        layer2_copied = sem("layer2_copied")
        hidden_upper_made = sems("hidden_upper_made", 2)
        hidden_lower_made = sems("hidden_lower_made", 2)
        expert_added = sem("expert_added")
        logits_made = sem("logits_made")
        logits_shifted = sem("logits_shifted")
        logits_exp_made = sem("logits_exp_made")
        router_made = sem("router_made")
        router_turned = sem("router_turned")
        router_copied = sem("router_copied")
        output_stored = sems("output_stored", 2)

        CONST = 7
        block = ctx.enter_context(nc.Block())

        @block.sync
        def _(sp):
            with nc.allow_non_contiguous_dma(reason="one edge of each block"):
                sp.dma_start(lk[:, :], dst1.rearrange("(p c j) -> p c j", c=LC, j=LB)[:, :, LB - 1]).then_inc(block_ends_loaded, 16)
            tiles = (NT - 1) // XCH
            for n in range(XCH):
                sp.dma_start(X3[:, n * tiles:(n + 1) * tiles, :],
                             x_in[n * tiles * P:(n + 1) * tiles * P, :].rearrange("(i p) d -> p i d", p=P)).then_inc(x_loaded[n], 16)
            sp.wait_ge(padding_set, 5)
            sp.dma_start(X3[0:LAST, NT - 1, :], x_in[(NT - 1) * P:N, :]).then_inc(x_loaded[XCH], 16)
            even = FULL // 16 * 16
            for n, (v, at) in enumerate(((dst1, dst_all[:, 1:T + 1]), (src1, idx_all[:, 0:T]))):
                sp.dma_start(at[0:even, :], v[0:even * T].rearrange("(p t) -> p t", t=T)).then_inc(runs_loaded, 16)
                sp.dma_start(at[even:FULL, :], v[even * T:FULL * T].rearrange("(p t) -> p t", t=T)).then_inc(runs_loaded, 16)
                sp.dma_start(at[FULL:FULL + 1, 0:REST], v[FULL * T:E].rearrange("(p t) -> p t", p=1)).then_inc(runs_loaded, 16)
            with nc.allow_non_contiguous_dma(reason="the edge before each run"):
                sp.dma_start(dst_all[1:P, 0:1], 
                             dst1[0:(P - 1) * T].rearrange("(p t) -> p t", t=T)[:, T - 1:T]).then_inc(runs_loaded, 16)

            def store_turned(n, slot):
                sp.wait_ge(turned_copied, done(n))
                sp.dma_start(xtd[bass.ds(n * P, P), :], xt[:, slot, :, :].rearrange("p k n -> p (k n)")).then_inc(turned_stored[slot], 16)

            with sp.Fori(0, NT // XS) as i:
                for j in range(XS):
                    store_turned(i * XS + j, j)
            store_turned(NT - 1, 0)
            sp.wait_ge(ends_made, 2)
            sp.dma_start(e_d[1:NT * P + 1, :].rearrange("(i p) a -> i (p a)", p=P), endsT[:, :]).then_inc(ends_stored, 16)
            sp.wait_ge(constants_made, CONST)
            sp.dma_start(e_d[0:1, :], upto[1:2, 0:1]).then_inc(ends_stored, 16)
            sp.wait_ge(ends_stored, 32)
            sp.dma_start(startsT[:, :], e_d[0:NT * P, :].rearrange("(i p) a -> i (p a)", p=P)).then_inc(starts_loaded, 16)
            sp.wait_ge(table_made, 1)
            sp.dma_start(tbl_p, TB3).then_inc(table_stored, 16)

            def window(w, loads=(None, None)):
                for h in range(2):
                    if loads[h]:
                        load_tile(*loads[h])
                    sp.wait_ge(max_stepped, w * U + (h + 1) * HW + U)
                    sp.wait_ge(sums_stepped, w * U + (h + 1) * HW + U)
                    for to, ring_, c in ((W_run[0], stm, BF), (W_run[1], sts, 2 * BF)):
                        sp.dma_start(to[:, bass.ds(w * (U * c) + h * HW * c, HW * c)],
                                     ring_[:, h * HW:(h + 1) * HW, :].rearrange("p a b -> p (a b)")).then_inc(states_stored[h], 16)

            def load_tile(n, ti, h):
                sp.wait_ge(tile_projected, free(n))
                sp.dma_start(xl[:, h, :, :].rearrange("p k n -> p (k n)"), xtd[bass.ds(ti * P, P), :]).then_inc(tile_loaded[h], 16)

            for n in range(XS):
                sp.wait_ge(turned_stored[n], 16 * (NT // XS + (n < NT % XS)) + 16)
            sp.wait_ge(bases_made, done(NT - 1))
            load_tile(0, 0, 0)
            load_tile(1, 1, 1)
            for ps in range(3):
                n0 = ps * UNITS
                for h in range(2):
                    load_tile(n0 + 2 + h, 2 + h, h)
                with sp.Fori(0, PAIRS - 2) as i:
                    window(i + ps * PASS, [(i * 2 + (n0 + 4 + h), i * 2 + (4 + h), h) for h in range(2)])
                window(ps * PASS + PAIRS - 2, ((n0 + NT - 1, NT - 1, 0), None))
                window(ps * PASS + PAIRS - 1, [(n0 + UNITS + h, h, h) if ps < 2 else None for h in range(2)])
                window(ps * PASS + PAIRS)
            with sp.Fori(3 * PASS, WIN) as w:
                window(w)
            sp.wait_ge(h_summed, done(NT - 1))
            for n, name in enumerate(("L0_ffn_W1", "L0_ffn_W2", "L0_ffn_Wo")):
                for k in range(KD):
                    sp.dma_start(EW[n].rearrange("p (e k n) -> p e k n", e=EX, k=KD)[:, :, k, :],
                                 a[name][:, k * P:(k + 1) * P, :].rearrange("e p n -> p e n")).then_inc(experts_loaded[n], 16)

            def store(g, b, n=GT):
                sp.wait_ge(expert_added, (g + 1) * (ROUNDS * GT) + ACC_START)
                if n == GT:
                    sp.dma_start(y[bass.ds(g * GN, GN), :].rearrange("(s p) d -> p s d", p=P), acc[:, b, :, :]).then_inc(output_stored[b], 16)
                else:
                    sp.dma_start(y[(NT - 1) * P:N, :], acc[0:LAST, b, 0, :]).then_inc(output_stored[b], 16)

            store(0, 0)
            with sp.Fori(0, GROUPS // 2 - 1) as i:
                store(i * 2 + 1, 1)
                store(i * 2 + 2, 0)
            store(GROUPS - 1, 1)
            store(GROUPS, 0, 1)
            sp.wait_ge(output_stored[0], 16 * (GROUPS // 2 + 1) + 16)
            sp.wait_ge(output_stored[1], 16 * (GROUPS // 2) + 16)

        @block.gpsimd
        def _(pool):
            pool.iota(iota[:, :], pattern=[[1, P]], base=0, channel_multiplier=0).then_inc(constants_made, 1)
            pool.iota(node[:, :], pattern=[[P, NT]], base=0, channel_multiplier=1).then_inc(constants_made, 1)
            pool.memset(ident[:, :], 0.0).then_inc(constants_made, 1)
            pool.memset(ones[:, :], 1.0).then_inc(constants_made, 1)
            pool.wait_ge(constants_made, 4)
            pool.affine_select(out=upto[:, :], in_=ones[:, :], compare_op=ALU.is_ge, fill=0.0, base=0,
                               pattern=[[1, P]], channel_multiplier=-1).then_inc(constants_made, 1)
            pool.affine_select(out=ident[:, :], in_=ident[:, :], compare_op=ALU.not_equal, fill=1.0, base=0,
                               pattern=[[-1, P]], channel_multiplier=1).then_inc(constants_made, 1)
            pool.memset(TB3[:, :, BF + 1:RW], 0.0).then_inc(constants_made, 1)
            pool.dma_start(b_comb[:, :], row_of(a["L0_gnn_b_comb"])).then_inc(rows_loaded, 16)
            pool.dma_start(b_r[:, :], row_of(a["L0_ffn_br"])).then_inc(rows_loaded, 16)
            pool.wait_ge(blocks_found, 1)
            for i in range(NT):
                pool.indirect_dma_start(out=blk[:, i, :], out_offset=None, in_=dst_blocks,
                                        in_offset=bass.IndirectOffsetOnAxis(ap=bidx[:, i:i + 1], axis=0)
                                        ).then_inc(blocks_gathered[min(i // CPER, CPARTS - 1)], 16)
            pool.wait_ge(ends_stored, 32)
            pool.wait_ge(first_node_found, 1)
            pool.indirect_dma_start(out=col[:, 3:4], out_offset=None, in_=e_d[:, :],
                                    in_offset=bass.IndirectOffsetOnAxis(ap=nidx[:, 0:1], axis=0)).then_inc(first_end_gathered, 16)
            pool.wait_ge(table_stored, 16)
            pool.dma_start(b_out, row_of(a["L0_mix_b_out"])).then_inc(rows_loaded, 16)
            pool.dma_start(g_out, row_of(a["L0_mix_g_out"])).then_inc(rows_loaded, 16)
            with pool.Fori(0, WIN) as w:
                for u in range(U):
                    if u % HW == 0:
                        pool.wait_ge(indices_copied, w * 2 + u // HW + 1)
                    if u % 4 == 0:
                        pool.wait_ge(max_stepped, w * U + u + 4)
                        pool.wait_ge(sums_stepped, w * U + u + 4)
                        pool.sem_inc(waits_carried, 1)
                    pool.indirect_dma_start(out=ring[:, u, 0:RW], out_offset=None, in_=tbl[:, :],
                                            in_offset=bass.IndirectOffsetOnAxis(ap=iw[:, u:u + 1], axis=0)).then_inc(row_gathered[u], 16)
            pool.wait_ge(indices_copied, 2 * WIN + 2)
            pool.wait_ge(states_stored[0], 32 * WIN + 32)
            pool.wait_ge(states_stored[1], 32 * WIN + 32)
            pool.wait_ge(fix_index_made, 1)
            at = bass.IndirectOffsetOnAxis(ap=fidx[:, 0:1], axis=0)
            parts = ((Wd[0], 0, BF), (Wd[1], BF, ST))
            for wd, c0, c1 in parts:
                pool.indirect_dma_start(out=fix[:, c0:c1], out_offset=None, in_=wd[:, :], in_offset=at,
                                        bounds_check=E - 1, oob_is_err=False).then_inc(fix_rows_gathered, 16)
            pool.wait_ge(fix_rows_made, 3)
            for wd, c0, c1 in parts:
                pool.indirect_dma_start(out=wd[:, :], out_offset=at, in_=fix[:, c0:c1], in_offset=None,
                                        bounds_check=E - 1, oob_is_err=False).then_inc(fix_rows_stored, 16)
            pool.wait_ge(fix_rows_stored, 32)
            for i in range(NT):
                if i >= GR:
                    pool.wait_ge(products_made, done(i - GR))
                for wd, c0, c1 in parts:
                    pool.indirect_dma_start(out=got[:, i % GR, c0:c1], out_offset=None, in_=wd[:, :],
                                            in_offset=bass.IndirectOffsetOnAxis(ap=pos[:, i:i + 1], axis=0)).then_inc(last_states_gathered[i % GR], 16)

            pool.wait_ge(weights_upper_made, 1)
            pool.tensor_tensor(EWL[0], EW[0], as_f32(EWH[0]), ALU.subtract).then_inc(weights_lower_made[0], 1)

        @block.scalar
        def _(act):
            act.dma_start(wb[:, :, :], a["L0_gnn_W_bases"].rearrange("(k p) n -> p k n", p=P)).then_inc(weights_loaded, 16)
            act.dma_start(wc[:, :, 0:CW], a["L0_gnn_W_comb"].rearrange("(k p) n -> p k n", p=P)).then_inc(weights_loaded, 16)
            wq = a["L0_mix_w_qkv"].rearrange("(k p) n -> p k n", p=P)
            act.dma_start(wc[:, :, CW:CW + 2 * HID], wq[:, :, HID:3 * HID]).then_inc(weights_loaded, 16)
            act.dma_start(wc[:, :, CW + 2 * HID:CW + 3 * HID], wq[:, :, 0:HID]).then_inc(weights_loaded, 16)
            act.dma_start(wo[:, :], a["L0_mix_w_out"]).then_inc(weights_loaded, 16)
            act.dma_start(wr[:, :, :], a["L0_ffn_Wr"].rearrange("(k p) n -> p k n", p=P)).then_inc(weights_loaded, 16)
            act.dma_start(bo[:, :], a["L0_ffn_bo"]).then_inc(weights_loaded, 16)
            for l in range(2):
                for n, name in enumerate(("b", "g", "be", "m", "v")):
                    act.dma_start(bnp[n * EX * KD:(n + 1) * EX * KD, l, :],
                                  a[f"L0_ffn_{name}{l + 1}"].rearrange("e (k p) -> (e k) p", p=P)).then_inc(weights_loaded, 16)
            for n in range(2):
                act.dma_start(mk[:, n, :], a["L0_mix_mem_kv"][n].rearrange("h d m -> (h d) m")).then_inc(weights_loaded, 16)
            with nc.allow_non_contiguous_dma(reason="a vector as columns"):
                act.dma_start(gpre[:, :], a["L0_mix_g_pre"].rearrange("(k p) -> p k", p=P)).then_inc(weights_loaded, 16)
                for n, name in enumerate(("L0_gnn_conv_bias", "L0_gnn_gn_weight", "L0_gnn_gn_bias", "L0_gnn_gn_mean_scale")):
                    act.dma_start(gpar[:, n, :], a[name].rearrange("(k p) -> p k", p=P)).then_inc(weights_loaded, 16)
            for s in (turned_copied, bases_copied, keys_exp_made, h_copied):
                act.sem_inc(s, RING2)
            act.sem_inc(layer1_copied, KD)
            act.sem_inc(layer2_copied, KD)
            act.wait_ge(root_wanted, 1)
            act.activation(tb_, ta, ACT.Sqrt).then_inc(root_made, 1)
            act.wait_ge(root_wanted, 2)
            act.activation(tnorm, ta, ACT.Sqrt).then_inc(root_made, 1)

            def tile_a(n, slot, before):
                act.wait_ge(tile_turned, n + (1 + XS))
                act.wait_ge(bases_made, free(n))
                act.wait_ge(turned_stored[slot], before * 16 + 16)
                act.activation(xt[:, slot, :, :].rearrange("p k n -> p (k n)"), bank[5 * (slot % 2)][:, 0:D], ACT.Copy).then_inc(turned_copied, 1)

            def tile_b(n, h):
                act.wait_ge(bases_made, done(n))
                act.activation(TB3[:, bass.ds(n, 1), 0:BF].rearrange("p a f -> p (a f)"), bank[1 + h][:, 0:BF], ACT.Copy).then_inc(bases_copied, 1)

            tile_a(0, 0, 0)
            tile_a(1, 1, 0)
            with act.Fori(0, (NT - 5) // XS) as i:
                for j in range(XS):
                    tile_b(i * XS + j, j % 2)
                    tile_a(i * XS + (j + 2), (j + 2) % XS, i + (j + 2) // XS)
            for n in range(NT - 5, NT - 1):
                tile_b(n, n % 2)
                if n + 2 < NT:
                    tile_a(n + 2, (n + 2) % XS, (n + 2) // XS)
            tile_b(NT - 1, 0)
            act.wait_ge(root_wanted, 3)
            act.activation(tb_, ta, ACT.Sqrt).then_inc(root_made, 1)
            act.wait_ge(runs_loaded, 16 * 7)
            act.wait_ge(padding_set, 5)
            for h in range(2):
                act.copy(iw[:, h * HW:(h + 1) * HW], idx_all[:, h * HW:(h + 1) * HW]).then_inc(indices_copied, 1)
            act.wait_ge(bn_var_made, 1)
            act.activation(bnt[:, :, :].rearrange("p a b -> p (a b)"), bns[:, :, :].rearrange("p a b -> p (a b)"), ACT.Sqrt).then_inc(bn_root_made, 1)

            def window(w, hook):
                for u in range(U):
                    act.wait_ge(row_gathered[u], w * 16 + 16)
                    act.activation(ring[:, u, RW:RW + BF], ring[:, u, 0:BF], ACT.Copy, scale=ring[:, u, BF:BF + 1]).then_inc(row_weighted, 1)
                    if u % HW == HW - 1:
                        h = u // HW
                        act.copy(iw[:, h * HW:(h + 1) * HW], idx_all[:, bass.ds(w * U + U + h * HW, HW)]).then_inc(indices_copied, 1)
                    if hook:
                        hook(u)

            def pass_c(n, h, s, last=False):
                R = LAST if last else P
                if s == 2:
                    act.wait_ge(tile_projected, done(n + UNITS))
                    act.wait_ge(context_added, free(n))
                    act.activation(vs[0:R, h, 0:HID], bank[5 + h][0:R, 0:HID], ACT.Copy, scale=rn[0:R, bass.ds(n, 1)])
                    act.wait_ge(keys_shifted, done(n))
                    act.activation(ek[0:R, h, :], kt[0:R, h, :], ACT.Exp).then_inc(keys_exp_made, 2 if last else 1)

            def pass_d(i, u, m=2):
                if u == 4:
                    act.wait_ge(queries_shifted, i + 1)
                    for h in range(m):
                        e = act.activation(eq[:, h, :], qd[:, h, :], ACT.Exp, scale=rn[:, bass.ds(i * 2 + h, 1)])
                    e.then_inc(queries_exp_made, 1)
                if u == 1:
                    for h in range(m):
                        x1 = X3[:, bass.ds(i * 2 + h, 1), :].rearrange("p a f -> p (a f)")
                        act.activation(x1, x1, ACT.Identity, scale=opr[:, bass.ds(i * 2 + h, 1)], bias=nmr[:, bass.ds(i * 2 + h, 1)])
                if u == 10:
                    act.wait_ge(queries_turned, i + 1)
                    act.activation(qT[:, 0:m, :], bank[4][:, 0:m * P].rearrange("p (b n) -> p b n", b=m), ACT.Copy).then_inc(queries_copied, 1)
                if u == 13:
                    act.wait_ge(mix_made, i + 1)
                    for h in range(m):
                        q = act.activation(xs[:, h, :], bank[5 + h][:, 0:D], ACT.Square, accum_out=nrm[:, h:h + 1])
                    q.then_inc(scalar_steps, 1)
                    act.wait_ge(scalar_steps, i + 1)
                    act.activation(nrm[:, 2:2 + m], nrm[:, 0:m], ACT.Sqrt).then_inc(mix_norm_made, 1)

            with act.Fori(0, PASS) as w:
                window(w, None)
            act.wait_ge(memory_exp_made, 1)
            act.activation(mkm[:, 0:MEM], mk[:, 0, :], ACT.Exp, bias=col[:, 8:9]).then_inc(memory_exp_made, 1)
            act.wait_ge(memory_turned, 1)
            act.activation(mT[:, 0:2 * P], bank[6][0:MEM, 0:2 * P], ACT.Copy).then_inc(memory_copied, 1)
            with act.Fori(0, PAIRS) as i:
                window(i + PASS, lambda u: pass_c(i * 2 + u // HW, u // HW, u % HW))
            window(PASS + PAIRS, lambda u: pass_c(NT - 1, 0, u, True) if u < HW else None)
            act.wait_ge(context_turned, 1)
            act.activation(diag[:, :], bank[7][:, 256:384], ACT.Copy).then_inc(context_copied, 1)
            with act.Fori(0, PAIRS) as i:
                window(i + 2 * PASS, lambda u: pass_d(i, u))
            window(2 * PASS + PAIRS, lambda u: pass_d(PAIRS, u, 1))
            with act.Fori(3 * PASS, WIN) as w:
                window(w, None)

            def h_out(n, b, w=P):
                act.wait_ge(h_summed, done(n))
                for k in range(KD):
                    m = act.activation(HT[:, bass.ds(n, 1), k, 0:w].rearrange("p a f -> p (a f)"), bank[1 + b][:, k * P:k * P + w], ACT.Copy,
                                       accum_out=hsum[:, k, bass.ds(n, 1)])
                m.then_inc(h_copied, 1)

            with act.Fori(0, PAIRS) as i:
                for b in range(2):
                    h_out(i * 2 + b, b)
            h_out(NT - 1, 0, LAST)

            act.wait_ge(center_made, 1)
            n = 0
            for c in range(NT // VCH + 1):
                i0, i1, w = (c * VCH, (c + 1) * VCH, P) if c < NT // VCH else (NT - 1, NT, LAST)
                for k in range(KD):
                    if n >= 4:
                        act.wait_ge(squares_summed, n - 3)
                    act.activation(junk[:, n % 4, 0:i1 - i0, 0:w], HT[:, i0:i1, k, 0:w], ACT.Square, bias=g_c[:, k:k + 1],
                                   accum_out=vsum[:, k, c:c + 1]).then_inc(squares_summed, 1)
                    n += 1
            act.wait_ge(norm_var_made, 1)
            act.activation(g_r, g_v, ACT.Sqrt).then_inc(norm_root_made, 1)

            def norm_chunk(c, b, tiles=CH, w=P):
                act.wait_ge(chunk_turned, c * 2 + (BO_START - 2))
                for k in range(KD):
                    m = act.activation(hr[:, b, k, 0:tiles * w].rearrange("p (i m) -> p i m", m=w), HT[:, bass.ds(c * CH, tiles), k, 0:w],
                                       ACT.Relu, scale=g_A[:, k:k + 1], bias=g_B[:, k:k + 1])
                m.then_inc(chunk_normed, 1)


            def evac(l, g, e, w, m_bias):
                sL, sh = ((layer1_made, layer1_copied), (layer2_made, layer2_copied))[l]
                q = g * EX + e
                act.wait_ge(hidden_lower_made[l], q + 1)
                if l == 0:
                    act.wait_ge(layer2_made, q * 2 + (L_START - 2))
                else:
                    act.wait_ge(layer3_made, g * (ROUNDS * GT) + e * GT + (GT if e >= 2 else 0) + L3_START - 2 * GT)
                for m in range(KD):
                    act.wait_ge(sL, q * 2 + (m + 1 + L_START))
                    bias, scale = bnb[:, l, m_bias + m:m_bias + m + 1], bns[:, l, m_bias + m:m_bias + m + 1]
                    act.activation(hf[:, l, m * w:(m + 1) * w], bank[2 * l + m][:, 0:w], ACT.Relu, bias=bias, scale=scale).then_inc(sh, 1)

            def front_root(G, ng=GT):
                act.wait_ge(front_var_made, G + 1)
                act.activation(ln[:, 1, 0:ng], ln[:, 0, 0:ng], ACT.Ln).then_inc(front_log_made, 1)
                act.wait_ge(front_log_made, G + 1)
                act.activation(ln[:, 2, 0:ng], ln[:, 1, 0:ng], ACT.Exp, scale=-0.5).then_inc(front_root_made, 1)

            def front_out(G, gb, w=GN):
                act.wait_ge(front_turned, G + 1)
                act.activation(xg[:, gb, 0, 0:KD * w], bank[6][:, 0:KD * w], ACT.Copy).then_inc(group_upper_made, 1)

            def group(g, gb, w, w_next):
                ng = w // P
                for e in range(EX):
                    if e + 1 < EX:
                        evac(0, g, e + 1, w, (e + 1) * KD)
                    elif w_next:
                        evac(0, g + 1, 0, w_next, 0)
                    evac(1, g, e, w, e * KD)
                    if e == 0:
                        act.wait_ge(logits_shifted, g + 1)
                        act.activation(lg[:, 0:ng, :], lg[:, 0:ng, :], ACT.Exp).then_inc(logits_exp_made, 1)
                    if e == 2:
                        act.wait_ge(router_turned, g + 1)
                        act.activation(wT[:, 0:w], bank[7][0:EX, 0:w], ACT.Copy).then_inc(router_copied, 1)
                    if e == 2 and w_next:
                        front_root(g + 1, w_next // P)
                    if e == 5 and w_next:
                        front_out(g + 1, 1 - gb, w_next)

            def upper(n):
                act.wait_ge(experts_loaded[n], 16 * KD)
                act.wait_ge(chunk_normed, min(-(-(n + 1) * EWN // (D * CH)), NCH + 1))
                act.activation(EWH[n], EW[n], ACT.Copy).then_inc(weights_upper_made, 1)

            act.wait_ge(norm_factors_made, 1)
            norm_chunk(0, 0)
            norm_chunk(1, 1)
            norm_chunk(2, 0)
            norm_chunk(3, 1)
            front_root(0)
            upper(0)
            front_out(0, 0)
            with act.Fori(2, NCH // 2) as i:
                for b in range(2):
                    norm_chunk(i * 2 + b, b)
            norm_chunk(NCH, 0, 1, LAST)
            upper(1)
            upper(2)
            evac(0, 0, 0, GN, 0)
            group(0, 0, GN, GN)
            with act.Fori(0, GROUPS // 2 - 1) as i:
                group(i * 2 + 1, 1, GN, GN)
                group(i * 2 + 2, 0, GN, GN)
            group(GROUPS - 1, 1, GN, P)
            group(GROUPS, 0, P, 0)

        @block.tensor
        def _(pe):
            for s in (bases_made, tile_projected, context_added, h_summed):
                pe.sem_inc(s, RING2)
            pe.sem_inc(tile_turned, XS)
            pe.sem_inc(chunk_turned, BO_START)
            pe.sem_inc(layer1_made, L_START)
            pe.sem_inc(router_copied, 1)
            pe.sem_inc(layer2_made, L_START)
            pe.sem_inc(layer3_made, L3_START)
            pe.wait_ge(constants_made, CONST)
            pe.wait_ge(histogram_fed, 2)
            for c in range(LC):
                mm = pe.matmul(bank[3][:, 0:NT], oh_lo[:, c, :], oh_hi[:, c, :], start=(c == 0), stop=(c == LC - 1))
            mm.then_inc(histogram_made, 1)
            pe.wait_ge(histogram_fed, 3)
            pe.matmul(bank[3][:, 64:64 + NT], upto[:, :], hist, start=True, stop=True)
            pe.matmul(bank[3][:, 128:128 + NT], ones[:, :], hist, start=True, stop=True).then_inc(prefixes_made, 1)
            pe.wait_ge(weights_loaded, 16 * 24)

            def turn(n, h, slot):
                pe.wait_ge(tile_normalised, done(n))
                pe.wait_ge(turned_copied, free(n))
                for k in range(KD):
                    mm = pe.transpose(bank[5 * h][:, k * P:(k + 1) * P], xs[:, slot, k * P:(k + 1) * P], ident[:, :])
                mm.then_inc(tile_turned, 1)

            def base(n, h, slot):
                pe.wait_ge(turned_copied, done(n))
                pe.wait_ge(bases_copied, free(n))
                for k in range(KD):
                    mm = pe.matmul(bank[1 + h][:, 0:BF], xt[:, slot, k, :], wb[:, k, :], start=(k == 0), stop=(k == KD - 1))
                mm.then_inc(bases_made, 1)

            turn(0, 0, 0)
            turn(1, 1, 1)
            with pe.Fori(0, (NT - 5) // XS) as i:
                for j in range(XS):
                    base(i * XS + j, j % 2, j)
                    turn(i * XS + (j + 2), j % 2, (j + 2) % XS)
            for n in range(NT - 5, NT - 1):
                base(n, n % 2, n % XS)
                if n + 2 < NT:
                    turn(n + 2, n % 2, (n + 2) % XS)
            base(NT - 1, 0, 0)
            pe.wait_ge(ends_made, 1)
            pe.transpose(bank[3][0:NT, 0:P], ends, ident[:, :]).then_inc(ends_turned, 1)
            pe.wait_ge(starts_loaded, 16)
            pe.transpose(bank[3][:, 128:128 + NT], startsT[:, :], ident[0:NT, 0:NT]).then_inc(starts_turned, 1)
            for l in range(2):
                mm = pe.transpose(bank[4][:, l * P:l * P + 5 * EX * KD], bnp[:, l, :], ident[0:5 * EX * KD, 0:5 * EX * KD])
            mm.then_inc(bn_turned, 1)
            pe.wait_ge(handed_diag_made, 1)
            pe.matmul(bank[0][:, 0:P], ones[:, :], diag[:, :], start=True, stop=True).then_inc(handed_spread, 1)

            def unit(ps, i, h, parts, inc=1):
                pe.wait_ge(tile_loaded[h], i * 16 + 16 * (ps * (PAIRS if h else PASS) + 1))
                for to, c0, c1 in parts:
                    for k in range(KD):
                        mm = pe.matmul(bank[to + h][:, 0:c1 - c0], xl[:, h, k, :], wc[:, k, c0:c1], start=(k == 0), stop=(k == KD - 1))
                mm.then_inc(tile_projected, inc)

            pe.wait_ge(bases_copied, done(NT - 1))
            pe.wait_ge(gain_in_weights, 2)
            with pe.Fori(0, PAIRS) as i:
                for h in range(2):
                    pe.wait_ge(comb_copied, free(i * 2 + h))
                    unit(0, i, h, ((1, 0, CW + HID),))
            pe.wait_ge(comb_copied, free(NT - 1))
            unit(0, PAIRS, 0, ((1, 0, CW + HID),), 2)
            pe.wait_ge(key_max_made, 1)
            pe.transpose(bank[7][:, 384:512], M[:, :], ident[:, :]).then_inc(key_max_turned, 1)
            pe.wait_ge(key_max_diag_made, 1)
            pe.matmul(bank[7][:, 256:384], ones[:, :], diag[:, :], start=True, stop=True).then_inc(key_max_spread, 1)
            pe.wait_ge(memory_exp_made, 2)
            pe.transpose(bank[6][0:MEM, 0:P], mkm[:, 0:MEM], ident[:, :])
            pe.transpose(bank[6][0:MEM, P:2 * P], mk[:, 1, :], ident[:, :]).then_inc(memory_turned, 1)
            pe.wait_ge(memory_copied, 1)
            pe.wait_ge(key_max_copied, 1)
            pe.matmul(bank[3][:, 0:HID + 1], mT[:, 0:P], mT[:, P:2 * P + 1], start=True, stop=False)

            def ctx_mm(n, h, last=False):
                R = LAST if last else P
                pe.wait_ge(keys_exp_made, done(n))
                pe.matmul(bank[3][:, 0:HID + 1], ek[0:R, h, :], vs[0:R, h, :], start=False, stop=last).then_inc(context_added, 2 if last else 1)

            def kv(n, i, h, inc=1):
                pe.wait_ge(keys_shifted, free(n))
                pe.wait_ge(keys_exp_made, free(n))
                unit(1, i, h, ((1, CW, CW + HID), (5, CW + HID, CW + 2 * HID)), inc)

            pe.wait_ge(comb_copied, done(NT))
            for h in range(2):
                kv(h, 0, h)
            with pe.Fori(0, PAIRS - 1) as i:
                for h in range(2):
                    ctx_mm(i * 2 + h, h)
                    kv(i * 2 + (2 + h), i + 1, h)
            ctx_mm(NT - 3, 0)
            kv(NT - 1, PAIRS, 0, 2)
            ctx_mm(NT - 2, 1)
            ctx_mm(NT - 1, 0, True)
            pe.wait_ge(context_made, 1)
            pe.transpose(bank[7][:, 256:384], diag[:, :], ident[:, :]).then_inc(context_turned, 1)
            pe.wait_ge(context_copied, 1)
            pe.matmul(bank[7][:, 0:D], diag[:, :], wo[:, :], start=True, stop=True).then_inc(out_map_made, 1)
            pe.wait_ge(out_map_biased, 1)

            def q_mm(i, m=2):
                for h in range(m):
                    unit(2, i, h, ((1, CW + 2 * HID, CW + 3 * HID),), 3 - m)

            def mix(i, m=2):
                pe.wait_ge(queries_normalised, i + 1)
                for h in range(m):
                    mm = pe.transpose(bank[4][:, h * P:(h + 1) * P], qn[:, h, :], ident[:, :])
                mm.then_inc(queries_turned, 1)
                pe.wait_ge(queries_copied, i + 1)
                pe.wait_ge(mix_added, i + 1)
                for h in range(m):
                    mm = pe.matmul(bank[5 + h][:, 0:D], qT[:, h, :], m2[:, :], start=True, stop=True)
                mm.then_inc(mix_made, 1)

            pe.wait_ge(keys_shifted, done(NT))
            pe.wait_ge(keys_exp_made, done(NT))
            q_mm(0)
            with pe.Fori(0, PAIRS - 1) as i:
                pe.wait_ge(queries_shifted, i + 1)
                q_mm(i + 1)
                mix(i)
            pe.wait_ge(queries_shifted, PAIRS)
            q_mm(PAIRS, 1)
            mix(PAIRS - 1)
            mix(PAIRS, 1)

            pe.wait_ge(max_stepped, WIN * U + U)
            pe.wait_ge(sums_stepped, WIN * U + U)
            for n in range(AGGS):
                mm = pe.transpose(bank[4][:, n * P:(n + 1) * P], stm[:, U - 1, :] if n == 0 else sts[:, U - 1, (n - 1) * BF:n * BF], ident[:, :])
            mm.then_inc(tails_turned, 1)
            pe.wait_ge(carries_scanned, AGGS)
            pe.wait_ge(mix_added, PASS + 1)
            for n in range(AGGS):
                mm = pe.transpose(bank[5][:, n * P:(n + 1) * P], carT[:, n, 0:P], ident[:, :])
            mm.then_inc(carries_turned, 1)

            def add_up(n, b):
                pe.wait_ge(products_made, done(n))
                pe.wait_ge(h_copied, free(n))
                for f in range(KD):
                    for k in (*range(2 * BASES), *range(2 * BASES + PRE, KC)):
                        mm = pe.matmul(bank[1 + b][:, f * P:(f + 1) * P], prod[:, b, k, f * P:(f + 1) * P], ident[:, :],
                                       start=(k == 0), stop=(k == KC - 1))
                mm.then_inc(h_summed, 1)

            with pe.Fori(0, PAIRS) as i:
                for b in range(2):
                    add_up(i * 2 + b, b)
            add_up(NT - 1, 0)

            def turn_chunk(c, b, tiles=CH, w=P):
                pe.wait_ge(chunk_normed, c + 1)
                for j in range(-(-tiles // 2)):
                    pe.wait_ge(branch_added, c * 4 + (j * 2 + BO_START - 2))
                    for t in range(min(2, tiles)):
                        for k in range(KD):
                            mm = pe.transpose(bank[4 + j][0:w, t * D + k * P:t * D + (k + 1) * P],
                                              hr[:, b, k, (j * 2 + t) * w:(j * 2 + t + 1) * w], ident[:, :])
                    mm.then_inc(chunk_turned, 1)

            PARTS = ((0, 0), (1, 0), (0, 1))

            def front_turn(G, w=GN):
                pe.wait_ge(front_normalised, G + 1)
                for k in range(KD):
                    for s in range(w // P):
                        mm = pe.transpose(bank[6][:, k * w + s * P:k * w + (s + 1) * P], xf[:, s, k * P:(k + 1) * P], ident[:, :])
                mm.then_inc(front_turned, 1)

            def layer(l, g, e, gb, w):
                q = g * EX + e
                sL, sE = ((layer1_made, layer1_copied), (layer2_made, layer2_copied))[l]
                rhs = xg[:, gb, :, :] if l == 0 else hid[0][:, e % 2, :, :]
                if isinstance(g, int) and g == 0:
                    pe.wait_ge(weights_lower_made[l], 1)
                if l == 1:
                    pe.wait_ge(hidden_upper_made[0], q + 1)
                for parts in (PARTS[:2], PARTS[2:]):
                    if l == 1 and parts == PARTS[2:]:
                        pe.wait_ge(hidden_lower_made[0], q + 2)
                    for m in range(KD):
                        if parts == PARTS[:2]:
                            pe.wait_ge(sE, q * 2 + (m + 1))
                        for wp, xp in parts:
                            for k in range(KD):
                                mm = pe.matmul(bank[2 * l + m][:, 0:w], EWP[l][wp][:, e, k, m * P:(m + 1) * P], rhs[:, xp, k * w:(k + 1) * w],
                                               start=(wp == 0 and xp == 0 and k == 0), stop=(xp == 1 and k == KD - 1))
                        if parts == PARTS[2:]:
                            mm.then_inc(sL, 1)

            def layer3(g, e, w):
                q = g * EX + e
                if isinstance(g, int) and g == 0:
                    pe.wait_ge(weights_lower_made[2], 1)
                pe.wait_ge(hidden_lower_made[1], q + 2)
                ng = w // P
                h2 = hid[1][:, e % 2, :, :]
                for s in range(ng):
                    pe.wait_ge(expert_added, g * (ROUNDS * GT) + ((e - 1 if e else -2) * GT + s + 1 + ACC_START))
                    for wp, xp in PARTS:
                        for k in range(KD):
                            mm = pe.matmul(bank[4 + s][:, 0:D], h2[:, xp, k * w + s * P:k * w + (s + 1) * P], EWP[2][wp][:, e, k, :],
                                           start=(wp == 0 and xp == 0 and k == 0), stop=(xp == 1 and k == KD - 1))
                    mm.then_inc(layer3_made, 1 if ng == GT else GT)

            def router(g, gb, w):
                pe.wait_ge(router_copied, g + 1)
                for s in range(w // P):
                    for wp, xp in PARTS:
                        for k in range(KD):
                            mm = pe.matmul(bank[7][:, s * EX:(s + 1) * EX], xg[:, gb, xp, k * w + s * P:k * w + (s + 1) * P], wrp[:, wp, k, :],
                                           start=(wp == 0 and xp == 0 and k == 0), stop=(xp == 1 and k == KD - 1))
                mm.then_inc(logits_made, 1)

            def weights_out(g, gb, w):
                pe.wait_ge(router_made, g + 1)
                for s in range(w // P):
                    mm = pe.transpose(bank[7][0:EX, s * P:(s + 1) * P], wsm[:, gb, s, :], ident[:, :])
                mm.then_inc(router_turned, 1)

            def bias_round(g, w):
                pe.wait_ge(router_copied, g + 2)
                ng = w // P
                for s in range(ng):
                    pe.matmul(bank[6][:, s * D:(s + 1) * D], wT[:, s * P:(s + 1) * P], bo[:, :],
                              start=True, stop=True).then_inc(layer3_made, 1 if ng == GT else GT)

            def first(g, gb, w):
                pe.wait_ge(group_upper_made, g + 1)
                pe.wait_ge(group_lower_made, g + 1)
                layer(0, g, 0, gb, w)
                router(g, gb, w)

            def group(g, gb, w, w_before, w_next):
                for e in range(EX):
                    if e + 1 < EX:
                        layer(0, g, e + 1, gb, w)
                    elif w_next:
                        first(g + 1, 1 - gb, w_next)
                    if e == 1 and w_before:
                        bias_round(g - 1, w_before)
                    layer(1, g, e, gb, w)
                    if e == 0 and w_before:
                        layer3(g - 1, EX - 1, w_before)
                    if e == 2:
                        weights_out(g, gb, w)
                    if e == 5 and w_next:
                        front_turn(g + 1, w_next)
                    if e > 0:
                        layer3(g, e - 1, w)

            turn_chunk(0, 0)
            turn_chunk(1, 1)
            turn_chunk(2, 0)
            front_turn(0)
            turn_chunk(3, 1)
            with pe.Fori(2, NCH // 2) as i:
                for b in range(2):
                    turn_chunk(i * 2 + b, b)
            turn_chunk(NCH, 0, 1, LAST)
            pe.wait_ge(branch_added, NT + BO_START)
            first(0, 0, GN)
            group(0, 0, GN, 0, GN)
            with pe.Fori(0, GROUPS // 2 - 1) as i:
                group(i * 2 + 1, 1, GN, GN, GN)
                group(i * 2 + 2, 0, GN, GN, GN)
            group(GROUPS - 1, 1, GN, GN, P)
            group(GROUPS, 0, P, GN, 0)
            layer3(GROUPS, EX - 1, P)
            bias_round(GROUPS, P)

        @block.vector
        def _(v):
            ch = Chain(v, vector_steps)
            for s in (tile_normalised, comb_copied, keys_shifted, products_made):
                v.sem_inc(s, RING2)
            v.sem_inc(expert_added, ACC_START)
            v.sem_inc(branch_added, BO_START)
            for h in range(2):
                v.sem_inc(hidden_lower_made[h], 1)
                v.sem_inc(states_stored[h], 32)
                v.sem_inc(output_stored[h], 16)
            for n in range(XS):
                v.sem_inc(turned_stored[n], 16)
            v.memset(idx_all[96:P, REST:T + U], 0).then_inc(padding_set, 1)
            v.memset(idx_all[0:96, T:T + U], 0).then_inc(padding_set, 1)
            v.memset(dst_all[96:P, REST + 1:T + 1], -1).then_inc(padding_set, 1)
            v.memset(dst_all[0:1, 0:1], -1).then_inc(padding_set, 1)
            v.memset(X3[96:P, NT - 1, :], 0.0).then_inc(padding_set, 1)

            def inv_root(y, val, t):
                ch(v.tensor_tensor(t, y, y, ALU.mult))
                ch(v.tensor_tensor(t, t, val, ALU.mult))
                ch(v.tensor_scalar(t, t, -0.5, 1.5, ALU.mult, ALU.add))
                ch(v.tensor_tensor(y, y, t, ALU.mult))

            v.wait_ge(block_ends_loaded, 16)
            ch.mark(v.tensor_scalar(lo[:, :], lk[:, :], P - 1, None, ALU.bitwise_and))
            ch(v.tensor_scalar(hi[:, :], lk[:, :], 7, None, ALU.arith_shift_right))
            v.wait_ge(constants_made, CONST)
            v.tensor_tensor(oh_lo, bcast(iota[0:LP, :].unsqueeze(1), [LP, LC, P]), bcast(lo[:, :].unsqueeze(2), [LP, LC, P]),
                            ALU.is_equal).then_inc(histogram_fed, 1)
            v.tensor_tensor(oh_hi, bcast(iota[0:LP, 0:NT].unsqueeze(1), [LP, LC, NT]), bcast(hi[:, :].unsqueeze(2), [LP, LC, NT]),
                            ALU.is_equal).then_inc(histogram_fed, 1)
            ch(v.memset(one_nt, 1.0))
            v.wait_ge(histogram_made, 1)
            v.tensor_copy(hist, bank[3][:, 0:NT]).then_inc(histogram_fed, 1)
            v.wait_ge(prefixes_made, 1)
            ch(v.tensor_copy(tot, bank[3][:, 128:128 + NT]))
            ch(v.tensor_tensor_scan(incl, one_nt, tot, 0.0, ALU.mult, ALU.add))
            ch(v.tensor_tensor(incl, incl, tot, ALU.subtract))
            ch(v.tensor_tensor(bf, incl, bank[3][:, 64:64 + NT], ALU.add))
            ch(v.tensor_scalar(bf, bf, float(NB - 1), None, ALU.min))
            v.tensor_copy(bidx[:, :], bf).then_inc(blocks_found, 1)

            def stats(n):
                ch.mark(v.bn_stats(bn_x[:, bass.ds(n, 1), :].rearrange("p a f -> p (a f)"), X3[:, bass.ds(n, 1), :].rearrange("p a f -> p (a f)")))

            tiles = (NT - 1) // XCH
            for c in range(XCH):
                v.wait_ge(x_loaded[c], 16)
                for n in range(c * tiles, (c + 1) * tiles):
                    stats(n)
            v.wait_ge(x_loaded[XCH], 16)
            stats(NT - 1)
            v.wait_ge(vector_steps, ch.n)
            half = [bn_x[:, :, n:n + 1].rearrange("p i a -> p (i a)") for n in range(6)]
            ch.mark(v.tensor_tensor(mean, half[1], half[4], ALU.add))
            ch.mark(v.tensor_tensor(tc, half[1], half[4], ALU.subtract))
            ch(v.tensor_tensor(var, half[2], half[5], ALU.add))
            ch.mark(v.tensor_scalar(mean, mean, 0.5, None, ALU.mult))
            ch.mark(v.tensor_scalar(var, var, 1.0 / D, None, ALU.mult))
            ch(v.tensor_tensor(tc, tc, tc, ALU.mult))
            ch(v.scalar_tensor_tensor(out=var, in0=tc, scalar=0.25, in1=var, op0=ALU.mult, op1=ALU.add))
            v.tensor_scalar(ta, var, LN_EPS, None, ALU.add).then_inc(root_wanted, 1)
            v.wait_ge(root_made, 1)
            ch(v.reciprocal(rstd, tb_))
            inv_root(rstd, ta, tc)
            ch(v.scalar_tensor_tensor(out=nmr, in0=mean, scalar=-1.0, in1=rstd, op0=ALU.mult, op1=ALU.mult))
            ch(v.tensor_tensor(tc, rstd, rstd, ALU.mult))
            ch(v.tensor_scalar(opr, rstd, 1.0, None, ALU.add))
            v.scalar_tensor_tensor(out=ta, in0=var, scalar=float(D), in1=tc, op0=ALU.mult, op1=ALU.mult).then_inc(root_wanted, 1)

            def norm(n, h):
                v.wait_ge(tile_turned, n + 1)
                v.tensor_scalar(xs[:, h, :], X3[:, bass.ds(n, 1), :].rearrange("p a f -> p (a f)"), rstd[:, bass.ds(n, 1)], nmr[:, bass.ds(n, 1)],
                                ALU.mult, ALU.add).then_inc(tile_normalised, 1)

            def count(c):
                t0, t1 = c * CPER, (c + 1) * CPER if c < CPARTS - 1 else NT
                v.wait_ge(blocks_gathered[c], 16 * (t1 - t0))
                ch(v.tensor_tensor(below[:, t0:t1, :], blk[:, t0:t1, :], bcast(node[:, t0:t1].unsqueeze(2), [P, t1 - t0, LB]), ALU.is_le))
                ch(v.tensor_reduce(cnt[:, t0:t1], below[:, t0:t1, :], AX.X, ALU.add))

            for c in range(CPARTS):
                with v.Fori(c * CPER // XS, (c + 1) * CPER // XS) as i:
                    for h in range(XS):
                        norm(i * XS + h, h)
                if c == CPARTS - 1:
                    norm(NT - 1, 0)
                count(c)
            v.scalar_tensor_tensor(out=ends, in0=bf, scalar=float(LB), in1=cnt, op0=ALU.mult, op1=ALU.add).then_inc(ends_made, 1)
            v.wait_ge(ends_turned, 1)
            v.tensor_copy(endsT[:, :], bank[3][0:NT, 0:P]).then_inc(ends_made, 1)
            v.wait_ge(runs_loaded, 16 * 7)
            v.tensor_scalar(nidx[:, :], dst_all[:, 1:2], 1.0, None, ALU.add).then_inc(first_node_found, 1)

            v.wait_ge(padding_set, 5)
            ch(v.tensor_tensor(con, dst_all[:, 1:T + 1], dst_all[:, 0:T], ALU.is_equal))
            ch(v.tensor_copy(col[:, 0:1], con[:, 0:1]))
            ch(v.memset(con[:, 0:1], 0.0))
            ch(v.tensor_scalar(neg, con, 1.0, BIG, ALU.subtract, ALU.mult))
            ch(v.tensor_tensor(col[:, 1:2], dst_all[:, 1:2], dst_all[:, T:T + 1], ALU.is_equal))
            ch(v.tensor_tensor(col[:, 1:2], col[:, 1:2], col[:, 0:1], ALU.mult))
            v.tensor_scalar(diag[:, :], ident[:, :], col[:, 1:2], None, ALU.mult).then_inc(handed_diag_made, 1)
            v.wait_ge(starts_turned, 1)
            ch(v.tensor_copy(starts, bank[3][:, 128:128 + NT]))
            ch(v.tensor_tensor(edges, ends, starts, ALU.subtract))
            ch(v.tensor_scalar(deg, edges, 1.0, None, ALU.add))
            v.wait_ge(root_made, 2)
            v.tensor_copy(ta, deg).then_inc(root_wanted, 1)
            v.wait_ge(root_made, 3)
            ch(v.reciprocal(dinv, tb_))
            inv_root(dinv, deg, tc)
            v.wait_ge(bases_copied, done(NT - 1))
            ch(v.tensor_copy(TB3[:, :, BF:BF + 1].rearrange("p i a -> p (i a)"), dinv))
            v.sem_inc(table_made, 1)
            ch(v.tensor_scalar(has, edges, 1.0, None, ALU.min))
            ch(v.tensor_scalar(rn, tnorm, 1e-12, None, ALU.max))
            ch(v.reciprocal(rn, rn))
            ch(v.tensor_scalar(rn, rn, float(D) ** 0.5, None, ALU.mult))
            ch(v.tensor_scalar(nohas, has, 1.0, BIG, ALU.subtract, ALU.mult))
            ch(v.tensor_scalar(posf, ends, 1.0, 0.0, ALU.subtract, ALU.max))
            ch(v.tensor_copy(pos[:, :], posf))
            v.wait_ge(weights_loaded, 16 * 24)
            for k in range(KD):
                v.tensor_scalar(wc[:, k, CW:CW + 3 * HID], wc[:, k, CW:CW + 3 * HID], gpre[:, k:k + 1], None, ALU.mult).then_inc(gain_in_weights, 1)
            ch(v.tensor_copy(wrp[:, 0, :, :], wr[:, :, :]))
            ch(v.tensor_tensor(wrp[:, 1, :, :], wr[:, :, :], as_f32(wrp[:, 0, :, :]), ALU.subtract))
            v.wait_ge(bn_turned, 1)
            for l in range(2):
                ch(v.tensor_copy(bnT[:, l, :], bank[4][:, l * P:l * P + 5 * EX * KD]))
            bp = [bnT[:, :, n * EX * KD:(n + 1) * EX * KD] for n in range(5)]
            ch(v.tensor_scalar(bp[4], bp[4], BN_EPS, None, ALU.add))
            v.tensor_copy(bns[:, :, :], bp[4]).then_inc(bn_var_made, 1)
            v.wait_ge(bn_root_made, 1)
            ch(v.reciprocal(bns[:, :, :], bnt[:, :, :]))
            inv_root(bns[:, :, :], bp[4], bnt[:, :, :])
            ch(v.tensor_tensor(bns[:, :, :], bns[:, :, :], bp[1], ALU.mult))
            ch(v.tensor_tensor(bnb[:, :, :], bp[0], bp[3], ALU.subtract))
            ch(v.tensor_tensor(bnb[:, :, :], bnb[:, :, :], bns[:, :, :], ALU.mult))
            ch(v.tensor_tensor(bnb[:, :, :], bnb[:, :, :], bp[2], ALU.add))
            v.wait_ge(handed_spread, 1)
            ch(v.tensor_copy(runw[:, :], bank[0][:, 0:P]))
            ch(v.tensor_scalar(runn[:, :], runw[:, :], 1.0, BIG, ALU.subtract, ALU.mult))
            ch(v.memset(carT[:, :, 0:1], 0.0))
            ch(v.memset(fix[:, :], 0.0))
            v.wait_ge(first_end_gathered, 16)
            ch(v.tensor_scalar(col[:, 4:5], node[:, 0:1], float(T), float(T), ALU.mult, ALU.add))
            ch(v.tensor_tensor(col[:, 4:5], col[:, 3:4], col[:, 4:5], ALU.is_le))
            ch(v.tensor_tensor(col[:, 4:5], col[:, 4:5], col[:, 0:1], ALU.mult))
            ch(v.scalar_tensor_tensor(out=col[:, 5:6], in0=col[:, 3:4], scalar=-1.0, in1=col[:, 4:5], op0=ALU.add, op1=ALU.mult))
            ch(v.tensor_scalar(col[:, 6:7], col[:, 4:5], -FAR, FAR, ALU.mult, ALU.add))
            ch(v.tensor_tensor(col[:, 5:6], col[:, 5:6], col[:, 6:7], ALU.add))
            v.tensor_copy(fidx[:, :], col[:, 5:6]).then_inc(fix_index_made, 1)
            ch(v.memset(M[:, :], -BIG))
            ch(v.memset(blockm[:, :], 0.0))
            for h in range(AH):
                ch(v.memset(blockm[h * AD:(h + 1) * AD, h * AD:(h + 1) * AD], float(AD) ** -0.5))
            ch(v.memset(vs[:, :, HID:HID + 1], 1.0))
            ch(v.memset(mT[:, 2 * P:2 * P + 1], 1.0))

            v.memset(stm[:, U - 1, :], 0.0).then_inc(max_stepped, U)
            v.memset(sts[:, U - 1, :], 0.0).then_inc(sums_stepped, U)

            def window(w, hook):
                for u in range(U):
                    pv = (u - 1) % U
                    if u % HW == 0:
                        v.wait_ge(states_stored[u // HW], w * 32 + 32)
                    v.wait_ge(row_weighted, w * U + u + 1)
                    v.wait_ge(max_stepped, w * U + U + u)
                    v.scalar_tensor_tensor(out=stm[:, u, :], in0=stm[:, pv, :], scalar=neg[:, bass.ds(w * U + u, 1)],
                                           in1=ring[:, u, 0:BF], op0=ALU.add, op1=ALU.max).then_inc(max_stepped, 1)
                    v.wait_ge(sums_stepped, w * U + U + u)
                    v.scalar_tensor_tensor(out=sts[:, u, :].rearrange("p (a b) -> p a b", a=2),
                                           in0=sts[:, pv, :].rearrange("p (a b) -> p a b", a=2),
                                           scalar=con[:, bass.ds(w * U + u, 1)],
                                           in1=ring[:, u, :].rearrange("p (a b) -> p a b", a=2)[:, :, 0:BF],
                                           op0=ALU.mult, op1=ALU.add).then_inc(sums_stepped, 1)
                    if hook:
                        hook(u)

            def pass_b(n, h, s, last=False):
                R = LAST if last else P
                if s == 2:
                    v.wait_ge(tile_projected, done(n))
                    ch(v.scalar_tensor_tensor(out=M[0:R, :], in0=bank[1 + h][0:R, CW:CW + HID], scalar=rn[0:R, bass.ds(n, 1)],
                                              in1=M[0:R, :], op0=ALU.mult, op1=ALU.max))
                if s == 4:
                    v.tensor_tensor(CB3[:, bass.ds(n, 1), :].rearrange("p a f -> p (a f)"), bank[1 + h][:, 0:CW], b_comb[:, :],
                                    ALU.add).then_inc(comb_copied, 2 if last else 1)

            v.wait_ge(rows_loaded, 16 * 4)
            with v.Fori(0, PAIRS) as i:
                ch.enter(i, 2)
                window(i, lambda u: pass_b(i * 2 + u // HW, u // HW, u % HW))
                ch.leave(PAIRS)
            window(PAIRS, lambda u: pass_b(NT - 1, 0, u, True) if u < HW else None)
            v.sem_inc(key_max_made, 1)
            v.wait_ge(key_max_turned, 1)
            ch(v.tensor_reduce(col[:, 9:10], bank[7][:, 384:512], AX.X, ALU.max))
            ch(v.tensor_reduce(col[:, 10:11], mk[:, 0, :], AX.X, ALU.max))
            ch(v.tensor_tensor(col[:, 9:10], col[:, 9:10], col[:, 10:11], ALU.max))
            v.tensor_scalar(col[:, 8:9], col[:, 9:10], -1.0, None, ALU.mult).then_inc(memory_exp_made, 1)
            v.tensor_scalar(diag[:, :], ident[:, :], col[:, 9:10], None, ALU.mult).then_inc(key_max_diag_made, 1)
            v.wait_ge(key_max_spread, 1)
            ch(v.tensor_copy(Mb[:, :], bank[7][:, 256:384]))
            v.sem_inc(key_max_copied, 1)
            v.wait_ge(comb_copied, done(NT))
            sym = CB3.rearrange("p i (h k) -> p i h k", h=HEADS)
            for h in range(HEADS):
                ch(v.tensor_tensor(sym[:, :, h, 0:BASES], sym[:, :, h, 0:BASES], bcast(dinv.unsqueeze(2), [P, NT, BASES]), ALU.mult))

            def pass_c(n, h, s, last=False):
                R = LAST if last else P
                if s == 0:
                    v.wait_ge(tile_projected, done(n + UNITS))
                    v.wait_ge(keys_exp_made, free(n))
                    v.scalar_tensor_tensor(out=kt[0:R, h, :], in0=bank[1 + h][0:R, 0:HID], scalar=rn[0:R, bass.ds(n, 1)], in1=Mb[0:R, :],
                                           op0=ALU.mult, op1=ALU.subtract).then_inc(keys_shifted, 2 if last else 1)

            with v.Fori(0, PAIRS) as i:
                window(i + PASS, lambda u: pass_c(i * 2 + u // HW, u // HW, u % HW))
            window(PASS + PAIRS, lambda u: pass_c(NT - 1, 0, u, True) if u < HW else None)
            v.wait_ge(context_added, done(NT))
            ch(v.reciprocal(col[:, 11:12], bank[3][:, HID:HID + 1]))
            v.scalar_tensor_tensor(out=diag[:, :], in0=bank[3][:, 0:HID], scalar=col[:, 11:12], in1=blockm[:, :],
                                   op0=ALU.mult, op1=ALU.mult).then_inc(context_made, 1)

            v.wait_ge(out_map_made, 1)
            v.scalar_tensor_tensor(out=m2[:, :], in0=b_out, scalar=1.0 / AH, in1=bank[7][:, 0:D], op0=ALU.mult, op1=ALU.add).then_inc(out_map_biased, 1)
            v.sem_inc(mix_added, 1)
            ch(v.tensor_scalar(g_out, g_out, float(D) ** 0.5, None, ALU.mult))

            def pass_d(i, u, m=2):
                b3 = [P, AH, AD]
                if u < m:
                    q3 = bank[1 + u][:, 0:HID].rearrange("p (h d) -> p h d", h=AH)
                    if u == 0:
                        v.wait_ge(tile_projected, i * 2 + (2 * UNITS + 2 + RING2))
                    ch(v.tensor_reduce(small[:, u, 0:AH], q3, AX.X, ALU.max))
                    t = v.tensor_tensor(qd[:, u, :].rearrange("p (h d) -> p h d", h=AH), q3, bcast(small[:, u, 0:AH].unsqueeze(2), b3),
                                        ALU.subtract)
                    if u == m - 1:
                        t.then_inc(queries_shifted, 1)
                if u == 7:
                    e3 = eq[:, 0:m, :].rearrange("p b (h d) -> p (b h) d", h=AH)
                    v.wait_ge(queries_exp_made, i + 1)
                    ch(v.tensor_reduce(esum[:, 0:m * AH], e3, AX.X, ALU.add))
                    ch(v.reciprocal(esum[:, 2 * AH:(2 + m) * AH], esum[:, 0:m * AH]))
                    v.tensor_tensor(qn[:, 0:m, :].rearrange("p b (h d) -> p (b h) d", h=AH), e3,
                                    bcast(esum[:, 2 * AH:(2 + m) * AH].unsqueeze(2), [P, m * AH, AD]), ALU.mult).then_inc(queries_normalised, 1)

            def pass_d_out(i, u, m=2):
                if u == 2:
                    v.wait_ge(mix_norm_made, i + 1)
                    ch(v.tensor_scalar(nrm[:, 4:4 + m], nrm[:, 2:2 + m], 1e-12, None, ALU.max))
                    ch(v.reciprocal(nrm[:, 6:6 + m], nrm[:, 4:4 + m]))
                if 2 <= u < 2 + m:
                    h = u - 2
                    x1 = X3[:, bass.ds(i * 2 + h, 1), :].rearrange("p a f -> p (a f)")
                    ch(v.scalar_tensor_tensor(out=mo[:, h, :], in0=bank[5 + h][:, 0:D], scalar=nrm[:, 6 + h:7 + h], in1=g_out,
                                              op0=ALU.mult, op1=ALU.mult))
                    t = v.tensor_tensor(x1, x1, mo[:, h, :], ALU.add)
                    if h == m - 1:
                        t.then_inc(mix_added, 1)

            window(2 * PASS, lambda u: pass_d(0, u))
            with v.Fori(1, PAIRS) as i:
                ch.enter(i - 1, 8)
                window(i + 2 * PASS, lambda u: (pass_d(i, u), pass_d_out(i - 1, u)))
                ch.leave(PAIRS - 1)
            window(2 * PASS + PAIRS, lambda u: (pass_d(PAIRS, u, 1), pass_d_out(PAIRS - 1, u)))
            window(3 * PASS, lambda u: pass_d_out(PAIRS, u, 1))
            with v.Fori(3 * PASS + 1, WIN) as w:
                window(w, None)

            v.wait_ge(tails_turned, 1)
            for n in range(AGGS):
                v.tensor_tensor_scan(carT[:, n, 1:P + 1], (runn if n == 0 else runw)[:, :], bank[4][:, n * P:(n + 1) * P], 0.0,
                                     ALU.add if n == 0 else ALU.mult, ALU.max if n == 0 else ALU.add).then_inc(carries_scanned, 1)
            v.wait_ge(carries_turned, 1)
            v.wait_ge(fix_rows_gathered, 32)
            for n in range(AGGS):
                v.tensor_tensor(fix[:, n * BF:(n + 1) * BF], fix[:, n * BF:(n + 1) * BF], bank[5][:, n * P:(n + 1) * P],
                                ALU.max if n == 0 else ALU.add).then_inc(fix_rows_made, 1)

            def combine(n, j, b, i7):
                g = got[:, j, :]
                own = TB3[:, bass.ds(n, 1), 0:BF].rearrange("p a f -> p (a f)")
                c = CB3[:, bass.ds(n, 1), :].rearrange("p a (h k) -> p k (a h)", h=HEADS)

                def product(k0, at):
                    return v.tensor_tensor(prod[:, b, k0:k0 + BASES, :].rearrange("p k (h f) -> p k h f", h=HEADS),
                                           bcast(c[:, k0:k0 + BASES, :].unsqueeze(3), [P, BASES, HEADS, F]),
                                           bcast(g[:, at * BF:(at + 1) * BF].rearrange("p (k f) -> p k f", k=BASES).unsqueeze(2), [P, BASES, HEADS, F]),
                                           ALU.mult)

                v.wait_ge(last_states_gathered[j], i7 * 32 + 32)
                ch.mark(v.scalar_tensor_tensor(out=g[:, BF:2 * BF], in0=g[:, BF:2 * BF], scalar=has[:, bass.ds(n, 1)], in1=own,
                                               op0=ALU.mult, op1=ALU.add))
                ch.mark(v.tensor_scalar(g[:, 2 * BF:3 * BF], g[:, 2 * BF:3 * BF], has[:, bass.ds(n, 1)], None, ALU.mult))
                ch.mark(v.scalar_tensor_tensor(out=g[:, 0:BF], in0=g[:, 0:BF], scalar=nohas[:, bass.ds(n, 1)], in1=own,
                                               op0=ALU.add, op1=ALU.max))
                v.wait_ge(vector_steps, ch.base + ch.n - 1)
                ch.mark(v.scalar_tensor_tensor(out=g[:, 2 * BF:3 * BF], in0=own, scalar=dinv[:, bass.ds(n, 1)], in1=g[:, 2 * BF:3 * BF],
                                               op0=ALU.mult, op1=ALU.add))
                v.wait_ge(h_summed, free(n))
                v.wait_ge(vector_steps, ch.base + ch.n - 1)
                ch.mark(product(BASES, 1))
                ch.mark(product(2 * BASES, 0))
                v.wait_ge(vector_steps, ch.base + ch.n - 2)
                product(0, 2)
                v.wait_ge(vector_steps, ch.base + ch.n)
                v.tensor_tensor(prod[:, b, BASES:BASES + PRE, :], prod[:, b, BASES:BASES + PRE, :], prod[:, b, 2 * BASES:2 * BASES + PRE, :],
                                ALU.add).then_inc(products_made, 1)

            full = NT // (2 * GR)
            with v.Fori(0, full) as i:
                ch.enter(i, 6 * 2 * GR)
                for j in range(2 * GR):
                    combine(i * (2 * GR) + j, j % GR, j % 2, i * 2 + j // GR)
                ch.leave(full)
            for n in range(full * 2 * GR, NT):
                combine(n, n % GR, n % 2, n // GR)

            v.wait_ge(h_copied, done(NT - 1))
            ch(v.tensor_reduce(g_m, hsum[:, :, :], AX.X, ALU.add))
            ch(v.scalar_tensor_tensor(out=g_m, in0=g_m, scalar=1.0 / N, in1=conv_b, op0=ALU.mult, op1=ALU.add))
            ch(v.tensor_tensor(g_m, g_m, gn_s, ALU.mult))
            v.tensor_tensor(g_c, conv_b, g_m, ALU.subtract).then_inc(center_made, 1)
            v.wait_ge(squares_summed, KD * (NT // VCH + 1))
            ch(v.tensor_reduce(g_v, vsum[:, :, :], AX.X, ALU.add))
            v.tensor_scalar(g_v, g_v, 1.0 / N, GN_EPS, ALU.mult, ALU.add).then_inc(norm_var_made, 1)
            v.wait_ge(norm_root_made, 1)
            ch(v.reciprocal(g_A, g_r))
            inv_root(g_A, g_v, g_t)
            ch(v.tensor_tensor(g_A, g_A, gn_w, ALU.mult))
            ch(v.tensor_tensor(g_B, g_c, g_A, ALU.mult))
            v.tensor_tensor(g_B, g_B, gn_b, ALU.add).then_inc(norm_factors_made, 1)

            def add_chunk(c, tiles=CH, w=P):
                for j in range(-(-tiles // 2)):
                    n = min(2, tiles)
                    x1 = X3[0:w, bass.ds(c * CH + j * 2, n), :].rearrange("p i f -> p (i f)")
                    v.wait_ge(chunk_turned, c * 2 + (j + 1 + BO_START))
                    v.tensor_tensor(x1, x1, bank[4 + j][0:w, 0:n * D], ALU.add).then_inc(branch_added, n)

            def front(G, step, gb, w=GN, tiles_ready=None):
                ng = w // P
                y, t = ln[:, 2, 0:ng], ln[:, 3, 0:ng]
                if step == (1, 2):
                    v.wait_ge(branch_added, BO_START + (NT if tiles_ready is None else tiles_ready))
                if step[0] == 1 and 2 <= step[1] < 2 + ng:
                    n = step[1] - 2
                    ch.mark(v.bn_stats(bn6[:, n, :], X3[:, bass.ds(G * GT + n, 1), :].rearrange("p a f -> p (a f)")))
                if step == (2, 0):
                    v.wait_ge(vector_steps, ch.base + ch.n)
                    v.sem_inc(waits_carried, 1)
                    for n in range(ng):
                        ch.mark(v.bn_aggr(mv[:, n, :], bn6[:, n, :]))
                if step == (2, 1):
                    v.wait_ge(vector_steps, ch.base + ch.n)
                    v.tensor_scalar(ln[:, 0, 0:ng], mv[:, 0:ng, 1:2].rearrange("p s a -> p (s a)"), LN_EPS, None, ALU.add).then_inc(front_var_made, 1)
                if step == (3, 0):
                    v.wait_ge(front_root_made, G + 1)
                    ch.mark(v.tensor_tensor(t, y, y, ALU.mult))
                if step == (3, 1):
                    v.wait_ge(vector_steps, ch.base + ch.n)
                    ch.mark(v.tensor_tensor(t, t, ln[:, 0, 0:ng], ALU.mult))
                if step == (3, 2):
                    v.wait_ge(vector_steps, ch.base + ch.n)
                    ch.mark(v.tensor_scalar(t, t, -0.5, 1.5, ALU.mult, ALU.add))
                if step == (3, 3):
                    v.wait_ge(vector_steps, ch.base + ch.n)
                    ch.mark(v.tensor_tensor(y, y, t, ALU.mult))
                if step == (4, 0):
                    v.wait_ge(vector_steps, ch.base + ch.n)
                    ch.mark(v.scalar_tensor_tensor(out=ln[:, 4, 0:ng], in0=mv[:, 0:ng, 0:1].rearrange("p s a -> p (s a)"), scalar=-1.0,
                                                   in1=y, op0=ALU.mult, op1=ALU.mult))
                if step == (4, 1):
                    v.wait_ge(vector_steps, ch.base + ch.n)
                    for n in range(ng):
                        m = v.tensor_scalar(xf[:, n, :], X3[:, bass.ds(G * GT + n, 1), :].rearrange("p a f -> p (a f)"), ln[:, 2, n:n + 1], ln[:, 4, n:n + 1],
                                            ALU.mult, ALU.add)
                    m.then_inc(front_normalised, 1)
                if step == (5, 3):
                    v.wait_ge(group_upper_made, G + 1)
                    v.tensor_tensor(xg[:, gb, 1, 0:KD * w], bank[6][:, 0:KD * w], as_f32(xg[:, gb, 0, 0:KD * w]),
                                    ALU.subtract).then_inc(group_lower_made, 1)

            def softmax(g, step, gb, ng):
                b3 = [P, ng, EX]
                if step == (0, 0):
                    v.wait_ge(logits_made, g + 1)
                    ch.mark(v.tensor_tensor(lg[:, 0:ng, :], bank[7][:, 0:ng * EX].rearrange("p (s e) -> p s e", s=ng),
                                            bcast(b_r[:, :].unsqueeze(1), b3), ALU.add))
                if step == (0, 1):
                    v.wait_ge(vector_steps, ch.base + ch.n)
                    ch(v.tensor_reduce(rsm[:, 0, 0:ng], lg[:, 0:ng, :], AX.X, ALU.max))
                    v.tensor_tensor(lg[:, 0:ng, :], lg[:, 0:ng, :], bcast(rsm[:, 0, 0:ng].unsqueeze(2), b3), ALU.subtract).then_inc(logits_shifted, 1)
                if step == (1, 0):
                    v.wait_ge(logits_exp_made, g + 1)
                    ch(v.tensor_reduce(rsm[:, 1, 0:ng], lg[:, 0:ng, :], AX.X, ALU.add))
                    ch.mark(v.reciprocal(rsm[:, 0, 0:ng], rsm[:, 1, 0:ng]))
                if step == (1, 1):
                    v.wait_ge(vector_steps, ch.base + ch.n)
                    v.tensor_tensor(wsm[:, gb, 0:ng, :], lg[:, 0:ng, :], bcast(rsm[:, 0, 0:ng].unsqueeze(2), b3), ALU.mult).then_inc(router_made, 1)

            def split(l, g, e, w):
                v.wait_ge((layer1_copied, layer2_copied)[l], g * (2 * EX) + (2 * e + 2 + KD))
                v.tensor_copy(hid[l][:, e % 2, 0, 0:KD * w], hf[:, l, 0:KD * w]).then_inc(hidden_upper_made[l], 1)
                v.wait_ge(hidden_upper_made[l], g * EX + (e + 1))
                v.tensor_tensor(hid[l][:, e % 2, 1, 0:KD * w], hf[:, l, 0:KD * w], as_f32(hid[l][:, e % 2, 0, 0:KD * w]),
                                ALU.subtract).then_inc(hidden_lower_made[l], 1)

            def add_tile(g, gb, e, s, ng):
                if s >= ng:
                    return
                r = g * (ROUNDS * GT) + (e * GT + s)
                inc = 1 if ng == GT else GT
                v.wait_ge(layer3_made, r + inc + L3_START + (GT - 1 - s if e == EX and ng == GT else 0))
                out, ps = acc[:, gb, s, :], bank[4 + s][:, 0:D] if e < EX else bank[6][:, s * D:(s + 1) * D]
                v.wait_ge(expert_added, r + (1 - GT + ACC_START))
                if e == 0:
                    x1 = X3[:, bass.ds(g * GT + s, 1), :].rearrange("p a f -> p (a f)")
                    v.scalar_tensor_tensor(out=out, in0=ps, scalar=wsm[:, gb, s, 0:1], in1=x1,
                                           op0=ALU.mult, op1=ALU.add).then_inc(expert_added, inc)
                elif e < EX:
                    v.scalar_tensor_tensor(out=out, in0=ps, scalar=wsm[:, gb, s, e:e + 1], in1=out,
                                           op0=ALU.mult, op1=ALU.add).then_inc(expert_added, inc)
                else:
                    v.tensor_tensor(out, out, ps, ALU.add).then_inc(expert_added, inc)

            def group(g, gb, w, w_before, w_next, prev_stores):
                ng = w // P
                for e in range(EX):
                    def between(place):
                        softmax(g, (e, place), gb, ng)
                        if w_next:
                            front(g + 1, (e, place), 1 - gb, w_next)
                    if e + 1 < EX:
                        split(0, g, e + 1, w)
                    elif w_next:
                        split(0, g + 1, 0, w_next)
                    between(0)
                    split(1, g, e, w)
                    if e == 1 and w_before:
                        for s in range(GT):
                            add_tile(g - 1, 1 - gb, EX, s, w_before // P)
                    between(1)
                    if e == 1:
                        v.wait_ge(router_made, g + 1)
                        v.wait_ge(output_stored[gb], prev_stores + 16)
                    for s in range(GT):
                        if e > 0:
                            add_tile(g, gb, e - 1, s, ng)
                        elif w_before:
                            add_tile(g - 1, 1 - gb, EX - 1, s, w_before // P)
                        between(2 + s)

            add_chunk(0)
            for e in range(EX):
                for place in range(4):
                    front(0, (e, place), 0, tiles_ready=CH)
                if e in (2, 4):
                    add_chunk(e // 2)
            with v.Fori(3, NCH) as i:
                add_chunk(i)
            add_chunk(NCH, 1, LAST)
            for n in (1, 2):
                v.wait_ge(weights_upper_made, n + 1)
                v.tensor_tensor(EWL[n], EW[n], as_f32(EWH[n]), ALU.subtract).then_inc(weights_lower_made[n], 1)
            split(0, 0, 0, GN)
            group(0, 0, GN, 0, GN, 0)
            with v.Fori(0, GROUPS // 2 - 1) as i:
                ch.enter(i, 2 * (4 + 2 * GT + 5))
                group(i * 2 + 1, 1, GN, GN, GN, i * 16)
                group(i * 2 + 2, 0, GN, GN, GN, i * 16 + 16)
                ch.leave(GROUPS // 2 - 1)
            group(GROUPS - 1, 1, GN, GN, P, 16 * (GROUPS // 2 - 1))
            group(GROUPS, 0, P, GN, 0, 16 * (GROUPS // 2))
            for e in (EX - 1, EX):
                add_tile(GROUPS, 0, e, 0, 1)


_INS = ["x", "src", "dst", "L0_gnn_W_bases", "L0_gnn_W_comb", "L0_gnn_b_comb", "L0_gnn_conv_bias", "L0_gnn_gn_weight",
        "L0_gnn_gn_bias", "L0_gnn_gn_mean_scale", "L0_mix_w_qkv", "L0_mix_mem_kv", "L0_mix_w_out", "L0_mix_b_out",
        "L0_mix_g_out", "L0_mix_g_pre", "L0_ffn_Wr", "L0_ffn_br"] + [
        f"L0_ffn_{n}{l}" for l in (1, 2) for n in ("W", "b", "g", "be", "m", "v")] + ["L0_ffn_Wo", "L0_ffn_bo"]


def kernel(**inputs):
    import numpy as _np
    import concourse.bacc as _bacc
    from concourse import mybir as _mybir
    from concourse.bass_utils import run_bass_kernel_spmd as _run

    nc = _bacc.Bacc("TRN2", target_bir_lowering=False, num_devices=1)
    arrays, aps = {}, {}
    for name in _INS:
        arr = _np.ascontiguousarray(inputs[name])
        arrays[f"in_{name}"] = arr
        aps[name] = nc.dram_tensor(f"in_{name}", arr.shape, _mybir.dt.from_np(arr.dtype), kind="ExternalInput").ap()
    out = nc.dram_tensor("out_y", (N, D), F32, kind="ExternalOutput").ap()
    scratch = {
        "tbl": nc.dram_tensor("scratch_table", (NT * P, RW), F32, kind="Internal").ap(),
        "xtd": nc.dram_tensor("scratch_xt", (NT * P, D), F32, kind="Internal").ap(),
        "maxes": nc.dram_tensor("scratch_maxes", (P * T, BF), F32, kind="Internal").ap(),
        "sums": nc.dram_tensor("scratch_sums", (P * T, 2 * BF), F32, kind="Internal").ap(),
        "ends": nc.dram_tensor("scratch_ends", (NT * P + 1, 1), F32, kind="Internal").ap(),
    }
    program(nc, aps, out, scratch)
    r = _run(nc, [arrays], core_ids=[0])
    return r.results[0]["out_y"]
```
